# Optimizing a Trainium2 kernel written in Bass

```python
import numpy as np
import jax
import jax.numpy as jnp

def _softmax(x, axis=-1):
    return jax.nn.softmax(x, axis=axis)

def _gelu(x):
    return jax.nn.gelu(x, approximate=True)

def _silu(x):
    return jax.nn.silu(x)

def _sigmoid(x):
    return jax.nn.sigmoid(x)

def _layernorm(x, axis=-1, eps=1e-05):
    m = jnp.mean(x, axis=axis, keepdims=True)
    v = jnp.var(x, axis=axis, keepdims=True)
    return (x - m) / jnp.sqrt(v + eps)

def _scatter_add(tgt, idx, src, axis=0):
    return tgt.at[idx].add(src)

def _segment_sum(src, seg, n):
    return jax.ops.segment_sum(src, seg, n)
kernel_name = 'mk_seq_preln_d1_jaxref_r4_e9ffb5'

def setup_inputs(seed: int=0):
    np.random.seed(seed)
    _w = jnp.asarray

    def _L0_attn_setup():
        import jax, jax.numpy as jnp
        import numpy as np
        EMBED_DIM = 256
        NUM_HEADS = 16
        HEAD_DIM = EMBED_DIM // NUM_HEADS
        NUM_DECAYS = 2
        BATCH = 2
        SEQ = 512
        W_SCALE = 0.02
        key = jax.random.key(seed)
        ks = jax.random.split(key, 12)
        d = EMBED_DIM
        inp = {'x': jax.random.normal(ks[0], (BATCH, SEQ, d), dtype=jnp.float32), 'Wq': jax.random.normal(ks[1], (d, d), dtype=jnp.float32) * W_SCALE, 'bq': jnp.zeros((d,), dtype=jnp.float32), 'Wk': jax.random.normal(ks[2], (d, d), dtype=jnp.float32) * W_SCALE, 'bk': jnp.zeros((d,), dtype=jnp.float32), 'Wv': jax.random.normal(ks[3], (d, d), dtype=jnp.float32) * W_SCALE, 'bv': jnp.zeros((d,), dtype=jnp.float32), 'Wo': jax.random.normal(ks[4], (d, d), dtype=jnp.float32) * W_SCALE, 'bo': jnp.zeros((d,), dtype=jnp.float32), 'decay_params': jax.random.uniform(ks[5], (NUM_HEADS, NUM_DECAYS), dtype=jnp.float32), 'mix_weights': jax.random.normal(ks[6], (NUM_HEADS, NUM_DECAYS), dtype=jnp.float32)}
        return inp
    _L0_attn_in = _L0_attn_setup()

    def _L0_ffn_setup():
        import jax, jax.numpy as jnp
        import numpy as np
        EPS = 1e-05

        def _quantize(W):
            gamma = jnp.mean(jnp.abs(W))
            return jnp.clip(jnp.round(W / (gamma + EPS)), -1.0, 1.0)
        key = jax.random.key(seed)
        k_x, k_w1, k_b1, k_w2, k_b2 = jax.random.split(key, 5)
        n_embd = 256
        d_ff = 4 * n_embd
        B, S = (4, 1024)
        bound1 = 1.0 / np.sqrt(n_embd)
        bound2 = 1.0 / np.sqrt(d_ff)
        x = jax.random.normal(k_x, (B, S, n_embd), dtype=jnp.float32)
        W1 = jax.random.uniform(k_w1, (d_ff, n_embd), jnp.float32, -bound1, bound1)
        b1 = jax.random.uniform(k_b1, (d_ff,), jnp.float32, -bound1, bound1)
        W2 = jax.random.uniform(k_w2, (n_embd, d_ff), jnp.float32, -bound2, bound2)
        b2 = jax.random.uniform(k_b2, (n_embd,), jnp.float32, -bound2, bound2)
        return {'x': x, 'W1': W1, 'b1': b1, 'W2': W2, 'b2': b2}
    _L0_ffn_in = _L0_ffn_setup()
    _d = {'L0_attn_x': _L0_attn_in['x'], 'L0_attn_Wq': _L0_attn_in['Wq'], 'L0_attn_bq': _L0_attn_in['bq'], 'L0_attn_Wk': _L0_attn_in['Wk'], 'L0_attn_bk': _L0_attn_in['bk'], 'L0_attn_Wv': _L0_attn_in['Wv'], 'L0_attn_bv': _L0_attn_in['bv'], 'L0_attn_Wo': _L0_attn_in['Wo'], 'L0_attn_bo': _L0_attn_in['bo'], 'L0_attn_decay_params': _L0_attn_in['decay_params'], 'L0_attn_mix_weights': _L0_attn_in['mix_weights'], 'L0_ffn_W1': _L0_ffn_in['W1'], 'L0_ffn_b1': _L0_ffn_in['b1'], 'L0_ffn_W2': _L0_ffn_in['W2'], 'L0_ffn_b2': _L0_ffn_in['b2']}
    _x0 = _d['L0_attn_x']
    _d['L0_attn_x'] = jax.random.normal(jax.random.fold_in(jax.random.key(seed), 1), (2, 2048, 256), dtype=_x0.dtype)
    del _x0
    return _d

def reference(L0_attn_x, L0_attn_Wq, L0_attn_bq, L0_attn_Wk, L0_attn_bk, L0_attn_Wv, L0_attn_bv, L0_attn_Wo, L0_attn_bo, L0_attn_decay_params, L0_attn_mix_weights, L0_ffn_W1, L0_ffn_b1, L0_ffn_W2, L0_ffn_b2):

    def _L0_attn_ref(x, Wq, bq, Wk, bk, Wv, bv, Wo, bo, decay_params, mix_weights):
        import jax, jax.numpy as jnp
        import numpy as np
        EMBED_DIM = 256
        NUM_HEADS = 16
        HEAD_DIM = EMBED_DIM // NUM_HEADS
        NUM_DECAYS = 2
        BATCH = 2
        SEQ = 512
        W_SCALE = 0.02
        B, S, _ = x.shape
        H, D = (NUM_HEADS, HEAD_DIM)

        def proj(W, b):
            return (jnp.einsum('bse,fe->bsf', x, W) + b).reshape(B, S, H, D).transpose(0, 2, 1, 3)
        q = proj(Wq, bq)
        k = proj(Wk, bk)
        v = proj(Wv, bv)
        attn_scores = jnp.einsum('bhqd,bhkd->bhqk', q, k) / jnp.sqrt(jnp.float32(D))
        t = jnp.arange(S, dtype=jnp.float32)
        time_diffs = jnp.abs(t[:, None] - t[None, :])
        dp = jnp.clip(decay_params, 0.01, 0.9999)
        decay_masks = dp[:, :, None, None] ** time_diffs[None, None, :, :]
        mix = jax.nn.softmax(mix_weights, axis=-1)
        decay_mask = jnp.einsum('hnqk,hn->hqk', decay_masks, mix)
        attn_scores = attn_scores * decay_mask[None]
        attn_probs = jax.nn.softmax(attn_scores, axis=-1)
        out = jnp.einsum('bhqk,bhkd->bhqd', attn_probs, v)
        out = out.transpose(0, 2, 1, 3).reshape(B, S, H * D)
        return jnp.einsum('bse,fe->bsf', out, Wo) + bo

    def _L0_ffn_ref(x, W1, b1, W2, b2):
        import jax, jax.numpy as jnp
        import numpy as np
        EPS = 1e-05

        def _quantize(W):
            gamma = jnp.mean(jnp.abs(W))
            return jnp.clip(jnp.round(W / (gamma + EPS)), -1.0, 1.0)
        Wq1 = _quantize(W1)
        Wq2 = _quantize(W2)
        h = jax.nn.relu(jnp.einsum('bsd,fd->bsf', x, Wq1) + b1)
        out = jnp.einsum('bsf,df->bsd', h, Wq2) + b2
        return out
    x = L0_attn_x
    x = x + _L0_attn_ref(_layernorm(x, axis=-1), L0_attn_Wq, L0_attn_bq, L0_attn_Wk, L0_attn_bk, L0_attn_Wv, L0_attn_bv, L0_attn_Wo, L0_attn_bo, L0_attn_decay_params, L0_attn_mix_weights)
    x = x + _L0_ffn_ref(_layernorm(x, axis=-1), L0_ffn_W1, L0_ffn_b1, L0_ffn_W2, L0_ffn_b2)
    return x

_drawn_inputs = setup_inputs


def setup_inputs(seed=0):
    import zlib

    import numpy as np

    out = dict(_drawn_inputs(seed))
    spreads = {'L0_attn_bq': (0.0, 0.8),
     'L0_attn_bk': (0.0, 0.8),
     'L0_attn_bv': (0.0, 0.281),
     'L0_attn_bo': (0.0, 0.1)}
    factors = {'L0_attn_Wq': 8.0,
     'L0_attn_Wk': 8.0,
     'L0_attn_Wv': 8.0,
     'L0_attn_decay_params': 8.0,
     'L0_attn_mix_weights': 8.0,
     'L0_ffn_b1': 22.387,
     'L0_ffn_b2': 64.0}
    for name, (base, spread) in spreads.items():
        noise = np.random.default_rng([zlib.crc32(name.encode()), seed]).standard_normal(out[name].shape)
        drawn = base * np.exp(spread * noise) if base else spread * noise
        out[name] = jnp.asarray(drawn.astype(out[name].dtype))
    for name, factor in factors.items():
        out[name] = (out[name] * factor).astype(out[name].dtype)
    return out
```

```python
from contextlib import ExitStack

import concourse.bass as bass
from concourse import mybir

F32 = mybir.dt.float32
F16 = mybir.dt.float16
ALU = mybir.AluOpType
ACT = mybir.ActivationFunctionType
AX = mybir.AxisListType

P = 128
BATCH, SEQ, EMBED = 2, 2048, 256
HEADS, HEAD_DIM, DECAYS = 16, 16, 2
FF = 4 * EMBED
EC = EMBED // P
FC = FF // P
BLOCKS = SEQ // P
PAIRS = HEADS // 2
STEPS = BATCH * PAIRS
GROUP = 512
TILES = GROUP // P
GROUPS = BATCH * SEQ // GROUP
HALF = SEQ // 2
LEVELS = (1024, 512, 256, 128)
RAW = len(LEVELS)
ROWS = DECAYS * HEAD_DIM
STACK = 3 * ROWS
MAXROWS = 2
SCALE = 32.0
MAXUNIT = 1024.0
LN_EPS = 1e-5
Q_EPS = 1e-5
QUADS = 16


def lead(ap, n):
    p, x = ap.shape
    return ap.unsqueeze(1).broadcast_to([p, n, x])


def setup_block(nc, a, keep, early, scr):
    ident, w1t, w2t, wot = keep["ident"], keep["w1t"], keep["w2t"], keep["wot"]
    wqkvt, qscale, qbias = early["wqkvt"], early["qscale"], early["qbias"]
    kbias, bv_all = early["kbias"], early["bv_all"]
    NTAB = PAIRS
    with ExitStack() as ctx:
        def sb(name, shape, dt=F32):
            return ctx.enter_context(nc.sbuf_tensor(name, shape, dt))

        def sem(name):
            return ctx.enter_context(nc.semaphore(name))

        wn = sb("wn", [P, 4, EC, EMBED])
        w1n = sb("w1n", [P, FC, EMBED])
        w2n = sb("w2n", [P, EC, FF])
        ternary = sb("ternary", [P, 2, FF * EC])
        below = sb("below", [P, FF * EC])
        decay_rows = sb("decay_rows", [P, NTAB])
        table = sb("table", [P, NTAB, 2 * HALF])
        mix_rows = sb("mix_rows", [P, 2, DECAYS])
        mix_w = sb("mix_w", [P, 2, DECAYS])
        mix_m = sb("mix_m", [P, 2, 1])
        q_bias_in = sb("q_bias_in", [P, 2])
        k_bias_in = sb("k_bias_in", [P, 2])
        decay_h = sb("decay_h", [HEADS, DECAYS])
        mix_h = sb("mix_h", [HEADS, DECAYS])
        mix_hw = sb("mix_hw", [HEADS, DECAYS])
        mix_hm = sb("mix_hm", [HEADS, 1])
        power_up = sb("power_up", [HEADS, DECAYS, P])
        power_down = sb("power_down", [HEADS, DECAYS, P])
        hat = sb("hat", [HEADS, 2 * P])
        hankel = sb("hankel", [P, HEADS, P])
        flip = sb("flip", [P, P])
        masks = sb("masks", [P, HEADS, P])
        ones = sb("ones", [P, P])
        abs_sum = sb("abs_sum", [P, 2])
        cut = sb("cut", [P, 2])
        neg_cut = sb("neg_cut", [P, 2])
        bank = ctx.enter_context(nc.psum_tensor("setup_bank", [P, 8, 512], F32))

        w_in, ffn_in, small_in = sem("w_in"), sem("ffn_in"), sem("small_in")
        ident_done, ones_done, turned, turned_out = sem("ident_done"), sem("ones_done"), sem("turned"), sem("turned_out")
        dve_step, pool_step, act_step = sem("dve_step"), sem("pool_step"), sem("act_step")
        sums_ready, total_ready, ternary_ready = sem("sums_ready"), sem("total_ready"), sem("ternary_ready")
        hat_ready, hat_stored, hankel_in = sem("hat_ready"), sem("hat_stored"), sem("hankel_in")
        flipped, masks_ready, table_ready, stored = sem("flipped"), sem("masks_ready"), sem("table_ready"), sem("stored")
        mix_exp, mix_diff = sem("mix_exp"), sem("mix_diff")
        block = ctx.enter_context(nc.Block())

        @block.sync
        def _(sp):
            for m, name in enumerate(("Wq", "Wk", "Wv", "Wo")):
                sp.dma_start(wn[:, m], a[name].rearrange("(c p) e -> p c e", p=P)).then_inc(w_in, QUADS)
            sp.dma_start(w1n[:], a["W1"].rearrange("(c p) e -> p c e", p=P)).then_inc(ffn_in, QUADS)
            sp.dma_start(w2n[:], a["W2"].rearrange("(c p) f -> p c f", p=P)).then_inc(ffn_in, QUADS)
            sp.wait_ge(hat_ready, 1)
            sp.dma_start(scr["hat"], hat[:]).then_inc(hat_stored, QUADS)
            sp.wait_ge(hat_stored, QUADS)
            windows = bass.AP(scr["hat"].tensor, 0, [[1, P], [2 * P, HEADS], [1, P]])
            sp.dma_start(hankel[:], windows).then_inc(hankel_in, QUADS)
            sp.wait_ge(table_ready, 2)
            sp.dma_start(scr["table"].rearrange("t p x -> p t x"), table[:]).then_inc(stored, QUADS)
            sp.wait_ge(masks_ready, 4)
            sp.dma_start(scr["mask"].rearrange("h p x -> p h x"), masks[:]).then_inc(stored, QUADS)
            sp.wait_ge(stored, 2 * QUADS)

        @block.gpsimd
        def _(pool):
            nc.gpsimd.memset(ident[:], 0.0).then_inc(pool_step, 1)
            nc.gpsimd.memset(flip[:], 0.0).then_inc(pool_step, 1)
            pool.wait_ge(pool_step, 2)
            nc.gpsimd.affine_select(out=ident[:], in_=ident[:], compare_op=ALU.not_equal, fill=1.0, base=0,
                                    pattern=[[-1, P]], channel_multiplier=1).then_inc(ident_done, 1)
            nc.gpsimd.affine_select(out=flip[:], in_=flip[:], compare_op=ALU.not_equal, fill=1.0, base=1 - P,
                                    pattern=[[1, P]], channel_multiplier=1).then_inc(ident_done, 1)
            pool.wait_ge(dve_step, 2)
            step = 2
            n = 1
            while n < HALF:
                part = table[:, :, 2 * HALF - n:2 * HALF]
                top = table[:, :, 2 * HALF - n:2 * HALF - n + 1].broadcast_to([P, NTAB, n])
                ins = nc.gpsimd.tensor_tensor(table[:, :, 2 * HALF - 2 * n:2 * HALF - n], part, top, ALU.mult)
                n *= 2
                if n < HALF:
                    step += 1
                    ins.then_inc(pool_step, 1)
                    pool.wait_ge(pool_step, step)
                else:
                    ins.then_inc(table_ready, 1)

        @block.scalar
        def _(act):
            for name, tile in (("bo", keep["bo_all"]), ("b2", keep["b2_all"]), ("bv", bv_all)):
                src = bass.AP(a[name].tensor, 0, [[0, P], [1, EMBED]])
                act.dma_start(tile[:], src).then_inc(small_in, QUADS)
            act.dma_start(keep["b1_col"][:], a["b1"].rearrange("(c p) -> p c", p=P), allow_slow_non_contiguous=True).then_inc(small_in, QUADS)
            act.dma_start(q_bias_in[:], a["bq"].rearrange("(c p) -> p c", p=P), allow_slow_non_contiguous=True).then_inc(small_in, QUADS)
            act.dma_start(k_bias_in[:], a["bk"].rearrange("(c p) -> p c", p=P), allow_slow_non_contiguous=True).then_inc(small_in, QUADS)
            act.dma_start(decay_h[:], a["decay"]).then_inc(small_in, QUADS)
            act.dma_start(mix_h[:], a["mix"]).then_inc(small_in, QUADS)
            for m in range(2):
                src = bass.AP(a["mix"].tensor, m * 8 * DECAYS, [[DECAYS, 8], [0, HEAD_DIM], [1, DECAYS]])
                act.dma_start(mix_rows[:, m, :], src).then_inc(small_in, QUADS)
            for r in range(8):
                src = bass.AP(a["decay"].tensor, (r // 4) * DECAYS + r % 2, [[0, HEAD_DIM], [2 * DECAYS, NTAB]])
                act.dma_start(decay_rows[HEAD_DIM * r:HEAD_DIM * (r + 1), :], src,
                              allow_slow_non_contiguous=True).then_inc(small_in, QUADS)
            act.wait_ge(mix_diff, 2)
            nc.scalar.activation(mix_w[:], mix_w[:], ACT.Exp).then_inc(mix_exp, 1)
            nc.scalar.activation(mix_hw[:], mix_hw[:], ACT.Exp).then_inc(mix_exp, 1)
            for m in range(4):
                act.wait_ge(turned, m + 1)
                dst = wot[:] if m == 3 else wqkvt[:, m]
                nc.scalar.copy(dst.rearrange("p c f -> p (c f)"), bank[:, m]).then_inc(turned_out, 1)

        @block.vector
        def _(dve):
            steps = [0]

            def then(ins):
                steps[0] += 1
                ins.then_inc(dve_step, 1)
                dve.wait_ge(dve_step, steps[0])

            small = 18 * QUADS
            dve.wait_ge(small_in, small)
            nc.vector.memset(ones[:], 1.0).then_inc(ones_done, 1)
            then(nc.vector.tensor_scalar(decay_rows[:], decay_rows[:], 0.01, 0.9999, ALU.max, ALU.min))
            then(nc.vector.tensor_copy(table[:, :, 2 * HALF - 1], decay_rows[:]))
            nc.vector.memset(table[:, :, 0:1], 1.0)
            then(nc.vector.tensor_copy(table[:, :, 1], decay_rows[:]))
            nc.vector.tensor_reduce(mix_m[:], mix_rows[:], AX.X, ALU.max)
            then(nc.vector.tensor_reduce(mix_hm[:], mix_h[:], AX.X, ALU.max))
            nc.vector.tensor_tensor(mix_w[:], mix_rows[:], mix_m[:].broadcast_to([P, 2, DECAYS]),
                                    ALU.subtract).then_inc(mix_diff, 1)
            nc.vector.tensor_scalar(mix_hw[:], mix_h[:], mix_hm[:, 0:1], None, ALU.subtract).then_inc(mix_diff, 1)
            then(nc.vector.tensor_scalar(decay_h[:], decay_h[:], 0.01, 0.9999, ALU.max, ALU.min))
            dve.wait_ge(mix_exp, 2)
            nc.vector.tensor_reduce(mix_m[:], mix_w[:], AX.X, ALU.add)
            then(nc.vector.tensor_reduce(mix_hm[:], mix_hw[:], AX.X, ALU.add))
            nc.vector.reciprocal(mix_m[:], mix_m[:])
            then(nc.vector.reciprocal(mix_hm[:], mix_hm[:]))
            nc.vector.tensor_tensor(mix_w[:], mix_w[:], mix_m[:].broadcast_to([P, 2, DECAYS]), ALU.mult)
            then(nc.vector.tensor_scalar(mix_hw[:], mix_hw[:], mix_hm[:, 0:1], None, ALU.mult))
            nc.vector.tensor_scalar(kbias[:], k_bias_in[:], SCALE, None, ALU.mult)
            then(nc.vector.tensor_scalar(qscale[:], mix_w[:], SCALE, None, ALU.mult))
            nc.vector.tensor_tensor(qbias[:], qscale[:], q_bias_in[:].unsqueeze(2).broadcast_to([P, 2, DECAYS]), ALU.mult)
            nc.vector.memset(power_up[:, :, 0:1], 1.0)
            nc.vector.tensor_copy(power_up[:, :, 1], decay_h[:])
            then(nc.vector.tensor_copy(power_down[:, :, P - 1], decay_h[:]))
            n = 1
            while n < P:
                top = min(n, P - 1 - n)
                if top > 0:
                    nc.vector.tensor_tensor(power_up[:, :, n + 1:n + 1 + top], power_up[:, :, 1:1 + top],
                                            power_up[:, :, n:n + 1].broadcast_to([HEADS, DECAYS, top]), ALU.mult)
                then(nc.vector.tensor_tensor(power_down[:, :, P - 2 * n:P - n], power_down[:, :, P - n:P],
                                             power_down[:, :, P - n:P - n + 1].broadcast_to([HEADS, DECAYS, n]), ALU.mult))
                n *= 2
            nc.vector.memset(hat[:, 2 * P - 1:2 * P], 0.0)
            nc.vector.tensor_scalar(hat[:, 0:P - 1], power_down[:, 0, 1:P], mix_hw[:, 0:1], None, ALU.mult)
            then(nc.vector.tensor_scalar(hat[:, P - 1:2 * P - 1], power_up[:, 0, :], mix_hw[:, 0:1], None, ALU.mult))
            nc.vector.scalar_tensor_tensor(out=hat[:, 0:P - 1], in0=power_down[:, 1, 1:P], scalar=mix_hw[:, 1:2],
                                           in1=hat[:, 0:P - 1], op0=ALU.mult, op1=ALU.add)
            nc.vector.scalar_tensor_tensor(out=hat[:, P - 1:2 * P - 1], in0=power_up[:, 1, :], scalar=mix_hw[:, 1:2],
                                           in1=hat[:, P - 1:2 * P - 1], op0=ALU.mult, op1=ALU.add).then_inc(hat_ready, 1)
            n = 1
            while n < HALF:
                top = min(n, HALF - 1 - n)
                if top > 0:
                    ins = nc.vector.tensor_tensor(table[:, :, n + 1:n + 1 + top], table[:, :, 1:1 + top],
                                                  table[:, :, n:n + 1].broadcast_to([P, NTAB, top]), ALU.mult)
                    if 2 * n >= HALF:
                        ins.then_inc(table_ready, 1)
                    else:
                        then(ins)
                n *= 2
            dve.wait_ge(ffn_in, 2 * QUADS)
            flat = (w1n[:].rearrange("p c e -> p (c e)"), w2n[:].rearrange("p c e -> p (c e)"))
            for m in range(2):
                nc.vector.tensor_reduce(abs_sum[:, m:m + 1], flat[m], AX.X, ALU.add,
                                        apply_absolute_value=True).then_inc(sums_ready, 1)
            dve.wait_ge(total_ready, 1)
            then(nc.vector.tensor_scalar(cut[:], bank[:, 4, 0:2], 1.0 / (FF * EMBED), Q_EPS, ALU.mult, ALU.add))
            nc.vector.tensor_scalar(neg_cut[:], cut[:], -0.5, None, ALU.mult)
            then(nc.vector.tensor_scalar(cut[:], cut[:], 0.5, None, ALU.mult))
            for m in range(2):
                then(nc.vector.tensor_scalar(below[:], flat[m], neg_cut[:, m:m + 1], None, ALU.is_lt))
                then(nc.vector.scalar_tensor_tensor(out=ternary[:, m], in0=flat[m], scalar=cut[:, m:m + 1],
                                                    in1=below[:], op0=ALU.is_gt, op1=ALU.subtract))
            nc.vector.tensor_copy(below[:, 0:1], ternary[:, 0, 0:1]).then_inc(ternary_ready, 1)
            for q in range(4):
                dve.wait_ge(flipped, q + 1)
                nc.vector.tensor_copy(masks[:].rearrange("p h x -> p (h x)")[:, q * 512:(q + 1) * 512],
                                      bank[:, 4 + q]).then_inc(masks_ready, 1)
            for q in range(8):
                dve.wait_ge(turned, 4 + q + 1)
                out = (w1t[:, q // 2, (q % 2) * 512:(q % 2 + 1) * 512] if q < 4 else
                       w2t[:, 2 * (q - 4):2 * (q - 4) + 2, :].rearrange("p c e -> p (c e)"))
                nc.vector.tensor_copy(out, bank[:, q])

        @block.tensor
        def _(pe):
            pe.wait_ge(ident_done, 2)
            pe.wait_ge(w_in, 4 * QUADS)
            for m in range(4):
                for ec in range(EC):
                    for fc in range(EC):
                        last = nc.tensor.transpose(bank[:, m, (ec * EC + fc) * P:(ec * EC + fc + 1) * P],
                                                   wn[:, m, fc, ec * P:(ec + 1) * P], ident[:])
                last.then_inc(turned, 1)
            pe.wait_ge(ones_done, 1)
            pe.wait_ge(sums_ready, 2)
            nc.tensor.matmul(bank[:, 4, 0:2], ones[:], abs_sum[:], start=True, stop=True).then_inc(total_ready, 1)
            pe.wait_ge(ternary_ready, 1)
            pe.wait_ge(hankel_in, QUADS)
            for q in range(4):
                nc.tensor.matmul(bank[:, 4 + q], flip[:], hankel[:].rearrange("p h x -> p (h x)")[:, q * 512:(q + 1) * 512],
                                 start=True, stop=True).then_inc(flipped, 1)
            tern1 = ternary[:, 0].rearrange("p (c e) -> p c e", c=FC)
            tern2 = ternary[:, 1].rearrange("p (c f) -> p c f", c=EC)
            for q in range(8):
                if q < 4:
                    pe.wait_ge(turned_out, q + 1)
                else:
                    pe.wait_ge(masks_ready, q - 3)
                for j in range(4):
                    if q < 4:
                        src = tern1[:, (q % 2) * 4 + j, (q // 2) * P:(q // 2 + 1) * P]
                    else:
                        src = tern2[:, j % 2, (2 * (q - 4) + j // 2) * P:(2 * (q - 4) + j // 2 + 1) * P]
                    last = nc.tensor.transpose(bank[:, q, j * P:(j + 1) * P], src, ident[:])
                last.then_inc(turned, 1)


def normalize(nc, dve, x, out, stats, mv, rstd, spare, step, sqrt_in, sqrt_out, sqrt_count, last):
    for t in range(TILES):
        ins = nc.vector.bn_stats(stats[:, t], x[:, t])
    step(ins)
    nc.vector.memset(spare[:], 0.0)
    for t in range(TILES):
        ins = nc.vector.bn_aggr(mv[:, t], stats[:, t])
    step(ins)
    nc.vector.tensor_scalar(rstd[:], mv[:, :, 1], LN_EPS, None, ALU.add).then_inc(sqrt_in, 1)
    dve.wait_ge(sqrt_out, sqrt_count)
    step(nc.vector.reciprocal(rstd[:], rstd[:]))
    for t in range(TILES):
        ins = nc.vector.tensor_scalar(out[:, t], x[:, t], mv[:, t, 0:1], rstd[:, t:t + 1], ALU.subtract, ALU.mult)
    last(ins)


def token_block(nc, a, keep, early, scr):
    ident = keep["ident"]
    wqkvt, qscale, qbias = early["wqkvt"], early["qscale"], early["qbias"]
    kbias, bv_all = early["kbias"], early["bv_all"]
    with ExitStack() as ctx:
        def sb(name, shape, dt=F32):
            return ctx.enter_context(nc.sbuf_tensor(name, shape, dt))

        def sem(name):
            return ctx.enter_context(nc.semaphore(name))

        x_in = sb("x_in", [P, 2, TILES, EMBED])
        x_hat = sb("x_hat", [P, 2, TILES, EMBED])
        x_t = sb("x_t", [P, 2, EC, GROUP])
        q_out = sb("q_out", [P, 2, 2, DECAYS, GROUP])
        k_out = sb("k_out", [P, 2, 2, GROUP])
        v_out = sb("v_out", [P, 2, TILES, HEADS, ROWS])
        stats = sb("stats", [P, TILES, 6])
        mv = sb("mv", [P, TILES, 2])
        rstd = sb("rstd", [P, TILES])
        spare = sb("spare", [P, 1])
        turn = ctx.enter_context(nc.psum_tensor("turn", [P, EC, GROUP], F32))
        v_bank = ctx.enter_context(nc.psum_tensor("v_bank", [P, 2, 512], F32))
        qk_bank = ctx.enter_context(nc.psum_tensor("qk_bank", [P, 4, GROUP], F32))

        x_loaded = [sem(f"x_loaded{u}") for u in range(2)]
        stored = [sem(f"stored{u}") for u in range(2)]
        hat_done, sqrt_in, sqrt_out = sem("hat_done"), sem("sqrt_in"), sem("sqrt_out")
        turned, xt_dve, xt_act = sem("turned"), sem("xt_dve"), sem("xt_act")
        v_done, v_taken, qk_done, q_taken, k_taken = (sem("v_done"), sem("v_taken"), sem("qk_done"),
                                                      sem("q_taken"), sem("k_taken"))
        dve_step, credit = sem("dve_step"), sem("credit")
        DVE_STEPS = 3
        STORES = TILES + 8
        block = ctx.enter_context(nc.Block())
        x_groups = a["x"].rearrange("b s e -> (b s) e").rearrange("(i u t p) e -> i u p t e", u=2, t=TILES, p=P)
        v_scr = scr["v"].rearrange("b h p k c -> b p k h c")

        @block.sync
        def _(sp):
            for u in range(2):
                sp.sem_inc(stored[u], STORES * QUADS)
            with sp.Fori(0, GROUPS // 2) as i:
                for u in range(2):
                    b, half = sp.snap(i // 2), sp.snap(i % 2)
                    at = half * (2 * GROUP) + u * GROUP
                    kb = half * (2 * TILES) + u * TILES
                    g1 = 2 * i + u + 1
                    sp.wait_ge(v_taken, 2 * g1 + 2)
                    for t in range(TILES):
                        sp.dma_start(v_scr[b, :, kb + t], v_out[:, u, t]).then_inc(stored[u], QUADS)
                    sp.wait_ge(q_taken, 2 * g1 + 2)
                    sp.wait_ge(k_taken, 2 * g1 + 2)
                    for m in range(2):
                        for n in range(DECAYS):
                            sp.dma_start(scr["qk"][b, m, :, 1, n, :, bass.ds(at, GROUP)],
                                           k_out[:, u, m, :]).then_inc(stored[u], QUADS)
                    for m in range(2):
                        for n in range(DECAYS):
                            sp.dma_start(scr["qk"][b, m, :, 0, n, :, bass.ds(at, GROUP)],
                                           q_out[:, u, m, n, :]).then_inc(stored[u], QUADS)
            for u in range(2):
                sp.wait_ge(stored[u], (GROUPS // 2 + 1) * STORES * QUADS)

        @block.gpsimd
        def _(pool):
            pool.sem_inc(hat_done, 2)
            with pool.Fori(0, GROUPS // 2) as i:
                for u in range(2):
                    pool.wait_ge(hat_done, 2 * i + u + 1)
                    pool.dma_start(x_in[:, u], x_groups[i, u]).then_inc(x_loaded[u], QUADS)

        @block.vector
        def _(dve):
            nc.vector.memset(v_out[:], 1.0).then_inc(credit, 1)
            dve.wait_ge(credit, 1)
            dve.sem_inc(xt_dve, 1)
            dve.sem_inc(v_taken, 2)
            dve.sem_inc(k_taken, 2)
            with dve.Fori(0, GROUPS // 2) as i:
                for u in range(2):
                    g = 2 * i + u
                    taken = [0]

                    def step(ins, g=g, taken=taken):
                        taken[0] += 1
                        ins.then_inc(dve_step, 1)
                        dve.wait_ge(dve_step, DVE_STEPS * g + taken[0])

                    dve.wait_ge(x_loaded[u], QUADS * (i + 1))
                    dve.wait_ge(turned, g + 1)
                    normalize(nc, dve, x_in[:, u], x_hat[:, u], stats, mv, rstd, spare, step, sqrt_in, sqrt_out, g + 1,
                              lambda ins: ins.then_inc(hat_done, 1))
                    dve.wait_ge(turned, g + 2)
                    dve.wait_ge(qk_done, 4 * g + 4)
                    nc.vector.tensor_copy(x_t[:, u, 1], turn[:, 1]).then_inc(xt_dve, 1)
                    dve.wait_ge(stored[u], STORES * QUADS * (i + 1))
                    for h in range(2):
                        dve.wait_ge(v_done, 2 * g + h + 1)
                        nc.vector.tensor_tensor(
                            v_out[:, u, 2 * h:2 * h + 2, :, 0:HEAD_DIM],
                            v_bank[:, h].rearrange("p (t h d) -> p t h d", t=2, d=HEAD_DIM),
                            bv_all[:].rearrange("p (h d) -> p h d", d=HEAD_DIM).unsqueeze(1)
                            .broadcast_to([P, 2, HEADS, HEAD_DIM]), ALU.add).then_inc(v_taken, 1)
                    for m in range(2):
                        dve.wait_ge(qk_done, 4 * g + m + 9)
                        nc.vector.tensor_scalar(k_out[:, u, m], qk_bank[:, m], SCALE, kbias[:, m:m + 1],
                                                ALU.mult, ALU.add).then_inc(k_taken, 1)

        @block.scalar
        def _(act):
            act.sem_inc(xt_act, 1)
            act.sem_inc(q_taken, 2)
            with act.Fori(0, GROUPS // 2) as i:
                for u in range(2):
                    g = 2 * i + u
                    act.wait_ge(sqrt_in, g + 1)
                    nc.scalar.activation(rstd[:], rstd[:], ACT.Sqrt).then_inc(sqrt_out, 1)
                    act.wait_ge(turned, g + 2)
                    act.wait_ge(qk_done, 4 * g + 4)
                    nc.scalar.copy(x_t[:, u, 0], turn[:, 0]).then_inc(xt_act, 1)
                    act.wait_ge(stored[u], STORES * QUADS * (i + 1))
                    for m in range(2):
                        act.wait_ge(qk_done, 4 * g + m + 11)
                        for n in range(DECAYS):
                            ins = nc.scalar.activation(q_out[:, u, m, n], qk_bank[:, 2 + m], ACT.Identity,
                                                       bias=qbias[:, m, n:n + 1], scale=qscale[:, m, n:n + 1])
                        ins.then_inc(q_taken, 1)

        @block.tensor
        def _(pe):
            pe.sem_inc(turned, 1)
            pe.sem_inc(qk_done, 8)
            with pe.Fori(0, GROUPS // 2) as i:
                for u in range(2):
                    g = 2 * i + u
                    pe.wait_ge(hat_done, g + 3)
                    pe.wait_ge(xt_dve, g + 1)
                    pe.wait_ge(xt_act, g + 1)
                    for c in range(EC):
                        for t in range(TILES):
                            last = nc.tensor.transpose(turn[:, c, t * P:(t + 1) * P],
                                                       x_hat[:, u, t, c * P:(c + 1) * P], ident[:])
                    last.then_inc(turned, 1)
                    pe.wait_ge(xt_dve, g + 2)
                    pe.wait_ge(xt_act, g + 2)
                    pe.wait_ge(v_taken, 2 * g + 2)
                    for t in range(TILES):
                        for c in range(EC):
                            last = nc.tensor.matmul(v_bank[:, t // 2, (t % 2) * EMBED:(t % 2 + 1) * EMBED],
                                                    x_t[:, u, c, t * P:(t + 1) * P], wqkvt[:, 2, c],
                                                    start=(c == 0), stop=(c == EC - 1), skip_group_check=True)
                        if t % 2:
                            last.then_inc(v_done, 1)
                    for k, (w, m) in enumerate(((1, 0), (1, 1), (0, 0), (0, 1))):
                        if k == 0:
                            pe.wait_ge(k_taken, 2 * g + 2)
                        if k == 2:
                            pe.wait_ge(q_taken, 2 * g + 2)
                        for c in range(EC):
                            last = nc.tensor.matmul(qk_bank[:, k], wqkvt[:, w, c, m * P:(m + 1) * P], x_t[:, u, c],
                                                    start=(c == 0), stop=(c == EC - 1))
                        last.then_inc(qk_done, 1)


SLOTS = BLOCKS * 2
UNIT_SLOTS = BLOCKS // 2
UNITS = 4
LEAD = UNIT_SLOTS + 4
RING = 3
ITEMS = 4
RED_SLOT, TURN_SLOT = 4, 5
RING_STEP = ITEMS * SLOTS + UNITS
AHEAD_ITEMS = ITEMS * LEAD + 1
EXPS = 2 * SLOTS


def ring_item(slot, k):
    turns = sum(1 for s in range(min(slot, 0), max(slot, 0)) if s % UNIT_SLOTS == TURN_SLOT and s >= 1 - UNIT_SLOTS)
    return ITEMS * slot + k + (turns if slot > 0 else -turns)


def score_parts(block, side):
    at = block * P
    parts = []
    for level, hs in enumerate(LEVELS):
        mate = (at // hs) ^ 1
        for col in range(mate * hs, (mate + 1) * hs, min(hs, 512)):
            parts.append((level, col, min(hs, 512)))
    parts.append((RAW, at, P))
    return [p for p in parts if side is None or p[1] // HALF == side]


def attention_block(nc, keep, scr):
    ident = keep["ident"]
    with ExitStack() as ctx:
        def sb(name, shape, dt=F32):
            return ctx.enter_context(nc.sbuf_tensor(name, shape, dt))

        def sem(name):
            return ctx.enter_context(nc.semaphore(name))

        q_stack = [sb(f"q_stack{h}", [STACK + MAXROWS, RAW + 1, SEQ], F16) for h in range(2)]
        k_stack = [sb(f"k_stack{h}", [STACK + MAXROWS, RAW + 1, SEQ], F16) for h in range(2)]
        hi = sb("hi", [P, RAW + 1, SEQ], F16)
        lo = sb("lo", [P, RAW + 1, SEQ], F16)
        qk = sb("qk", [P, SEQ])
        table = sb("table_in", [P, 2 * HALF])
        decayed = sb("decayed", [P, 2, HALF])
        probs = sb("probs", [P, 4, HALF])
        diag = [sb(f"diag{h}", [P, BLOCKS, P]) for h in range(2)]
        mask = [sb(f"mask{h}", [P, P]) for h in range(2)]
        v_ones = [sb(f"v_ones{h}", [P, BLOCKS, ROWS]) for h in range(2)]
        part_max = sb("part_max", [P, 2, UNIT_SLOTS, 5])
        row_max = sb("row_max", [P, 2, UNIT_SLOTS])
        max_hi = sb("max_hi", [UNIT_SLOTS, P], F16)
        max_lo = sb("max_lo", [UNIT_SLOTS, P], F16)
        scrap = sb("scrap", [UNIT_SLOTS, 1])
        heads_out = sb("heads_out", [P, 2, 512])
        tile = [ctx.enter_context(nc.psum_tensor(f"tile{t}", [P, 2, 512], F32)) for t in range(2)]
        ring = ctx.enter_context(nc.psum_tensor("ring", [P, RING, 512], F32))
        acc = ctx.enter_context(nc.psum_tensor("acc", [P, 512], F32))

        tile_full = sem("tile_full")
        exp_done = sem("exp_done")
        probs_used = sem("probs_used")
        ring_full = sem("ring_full")
        ring_free = sem("ring_free")
        acc_full, acc_free = sem("acc_full"), sem("acc_free")
        out_stored = [sem(f"out_stored{h}") for h in range(2)]
        blocks_seen = sem("blocks_seen")
        max_ready, max_seen = sem("max_ready"), sem("max_seen")
        rows_ready, rows_in = sem("rows_ready"), sem("rows_in")
        diag_ready = sem("diag_ready")
        stack_free = [sem(f"stack_free{h}") for h in range(2)]
        stack_in = [[sem(f"stack{h}_{lv}") for lv in range(RAW + 1)] for h in range(2)]
        mask_in = [sem(f"mask_in{h}") for h in range(2)]
        v_in = [sem(f"v_in{h}") for h in range(2)]
        qk_in = sem("qk_in")
        decayed_ready, hi_ready, lo_ready = sem("decayed_ready"), sem("hi_ready"), sem("lo_ready")
        const_ready = sem("const_ready")
        CHUNKS = 2 * (RAW + 1)
        STACK_DMAS = 6
        ROW_DMAS = 2 * RAW
        OUT_DMAS = 4

        block = ctx.enter_context(nc.Block())

        def half_view(t, level, side):
            if level == RAW:
                return t[:, side * HALF:(side + 1) * HALF].unsqueeze(1)
            hs = LEVELS[level]
            return t.rearrange("p (r s x) -> p r s x", s=2, x=hs)[:, :, side, :]

        def factors(level, side):
            hs = LEVELS[level]
            part = table[:, 2 * HALF - hs:2 * HALF] if side == 0 else table[:, 0:hs]
            return lead(part, HALF // hs)

        def compact(c, level):
            hs = HALF if level == RAW else LEVELS[level]
            return decayed[:, c % 2].rearrange("p (r x) -> p r x", x=hs)

        mul_slot = (1, 2, 5, 6, 8, 9, 10, 13, 14, 15)
        hi_slot = (3, 4, 7, 8, 10, 11, 13, 15, 17, 18)

        @block.sync
        def _(sp):
            def load_qk(pair):
                sp.dma_start(qk[:], scr["qk"].rearrange("b m (h s) k n d t -> (b m h) (s k n d) t", s=2)[pair]
                             ).then_inc(qk_in, QUADS)
                sp.dma_start(table[:], scr["table"][pair % PAIRS]).then_inc(qk_in, QUADS)

            def load_stack(h, built):
                for level in range(RAW + 1):
                    sp.wait_ge(lo_ready, built - CHUNKS + 2 * level + 2)
                    for dst, k, parts in ((q_stack[h], 0, (hi, hi, lo)), (k_stack[h], 1, (hi, lo, hi))):
                        for j, part in enumerate(parts):
                            row = (2 * h + k) * ROWS
                            sp.dma_start(dst[j * ROWS:(j + 1) * ROWS, level], part[row:row + ROWS, level]
                                         ).then_inc(stack_in[h][level], QUADS)

            def load_v(h, pair):
                sp.dma_start(v_ones[h][:], scr["v"].rearrange("b (h s) p k c -> (b h) s p k c", s=2)[pair, h]
                             ).then_inc(v_in[h], QUADS)

            def load_mask(h, pair):
                sp.dma_start(mask[h][:], scr["mask"].rearrange("(h s) p x -> h s p x", s=2)[pair % PAIRS, h]
                             ).then_inc(mask_in[h], QUADS)

            def store_max_rows(h, half, count):
                sp.wait_ge(rows_ready, count)
                for j, src in enumerate((max_hi, max_lo)):
                    for level in range(RAW):
                        dst = q_stack[h][STACK + j:STACK + j + 1, level, half * HALF:(half + 1) * HALF]
                        sp.dma_start(dst.rearrange("o (b x) -> o b x", x=P), src[:]).then_inc(rows_in, QUADS)

            def store_out(i, u):
                sp.wait_ge(acc_free, UNITS * i + u + 2)
                head = (i % (PAIRS // 2)) * 2 + u // 2
                dst = scr["out"].rearrange("a r k (h d) t -> a h r k d t", d=HEAD_DIM)[i // (PAIRS // 2), head]
                for par in range(2):
                    for qt in range(2):
                        row, col = (2 * par + qt) * ROWS, (u % 2) * HALF + qt * 512
                        sp.dma_start(dst[par, :, :, col:col + 512], heads_out[row:row + ROWS, u % 2]
                                     ).then_inc(out_stored[u % 2], QUADS)

            load_qk(0)
            load_mask(0, 0)
            load_mask(1, 0)
            load_v(0, 0)
            load_stack(0, CHUNKS)
            load_qk(1)
            store_max_rows(0, 0, 1)
            with sp.Fori(0, STEPS) as i:
                sp.wait_ge(stack_free[1], i + 1)
                load_stack(1, CHUNKS * (i + 1))
                sp.wait_ge(acc_free, UNITS * i + 1)
                load_v(1, i)
                store_max_rows(0, 1, UNITS * i + 2)
                sp.wait_ge(blocks_seen, SLOTS * i + BLOCKS + 1)
                load_mask(0, (i + 1) % STEPS)
                store_out(i, 0)
                store_max_rows(1, 0, UNITS * i + 3)
                sp.wait_ge(stack_free[0], i + 1)
                load_stack(0, CHUNKS * (i + 2))
                store_out(i, 1)
                load_v(0, (i + 1) % STEPS)
                load_qk((i + 2) % STEPS)
                store_max_rows(1, 1, UNITS * i + 4)
                sp.wait_ge(blocks_seen, SLOTS * i + 2 * BLOCKS + 1)
                load_mask(1, (i + 1) % STEPS)
                store_out(i, 2)
                store_max_rows(0, 0, UNITS * i + 5)
                store_out(i, 3)
            for h in range(2):
                sp.wait_ge(out_stored[h], (2 * STEPS + 1) * OUT_DMAS * QUADS)
                for level in range(RAW + 1):
                    sp.wait_ge(stack_in[h][level], STACK_DMAS * QUADS * (STEPS + (1 - h)))
                sp.wait_ge(mask_in[h], QUADS * (STEPS + 1))
            sp.wait_ge(v_in[0], QUADS * (STEPS + 1))
            sp.wait_ge(v_in[1], QUADS * STEPS)
            sp.wait_ge(qk_in, 2 * QUADS * (STEPS + 2))
            sp.wait_ge(rows_in, ROW_DMAS * QUADS * (UNITS * STEPS + 1))

        @block.gpsimd
        def _(pool):
            def multiply(c, built):
                level, side = c // 2, c % 2
                if c == 0:
                    pool.wait_ge(qk_in, 2 * QUADS * (built + 1))
                if level < RAW:
                    if not (isinstance(built, int) and built == 0 and c < 2):
                        pool.wait_ge(lo_ready, CHUNKS * built + max(c - 1, 0))
                    nc.gpsimd.tensor_tensor(compact(c, level), half_view(qk[:], level, side), factors(level, side),
                                            ALU.mult).then_inc(decayed_ready, 1)

            def rest(c, built):
                level, side = c // 2, c % 2
                pool.wait_ge(hi_ready, CHUNKS * built + c + 1)
                src = half_view(qk[:], level, side) if level == RAW else compact(c, level)
                nc.gpsimd.tensor_tensor(half_view(lo[:, level], level, side), src, half_view(hi[:, level], level, side),
                                        ALU.subtract).then_inc(lo_ready, 1)

            def free_level(c, i):
                if c % 2 == 0:
                    for h in range(2):
                        pool.wait_ge(stack_in[h][c // 2], STACK_DMAS * QUADS * (i + 1))

            def diag_minus_max(h, half, count):
                pool.wait_ge(max_ready, count)
                part = diag[h][:, half * UNIT_SLOTS:(half + 1) * UNIT_SLOTS]
                nc.gpsimd.tensor_tensor(part, part, row_max[:, half].unsqueeze(2).broadcast_to([P, UNIT_SLOTS, P]),
                                        ALU.subtract).then_inc(diag_ready, 1)

            pool.sem_inc(diag_ready, 1)
            for c in range(CHUNKS):
                multiply(c, 0)
                if c > 0:
                    rest(c - 1, 0)
            rest(CHUNKS - 1, 0)
            diag_minus_max(0, 0, 1)
            with pool.Fori(0, STEPS) as i:
                for s in range(SLOTS):
                    for c in range(CHUNKS):
                        if mul_slot[c] == s:
                            free_level(c, i)
                            multiply(c, i + 1)
                            if c > 0:
                                rest(c - 1, i + 1)
                            if c == CHUNKS - 1:
                                rest(c, i + 1)
                    if s % UNIT_SLOTS == RED_SLOT:
                        u = s // UNIT_SLOTS + 1
                        diag_minus_max((u // 2) % 2, u % 2, UNITS * i + u + 1)

        @block.scalar
        def _(act):
            def cast(c, built):
                level, side = c // 2, c % 2
                if level < RAW:
                    act.wait_ge(decayed_ready, (CHUNKS - 2) * built + c + 1)
                else:
                    act.wait_ge(lo_ready, CHUNKS * built + CHUNKS - 2)
                src = half_view(qk[:], level, side) if level == RAW else compact(c, level)
                nc.scalar.copy(half_view(hi[:, level], level, side), src).then_inc(hi_ready, 1)

            act.sem_inc(acc_free, 1)
            for h in range(2):
                act.sem_inc(out_stored[h], QUADS * OUT_DMAS)
            for c in range(CHUNKS):
                cast(c, 0)
            act.sem_inc(exp_done, 2)
            with act.Fori(0, STEPS) as i:
                def take_unit(u):
                    act.wait_ge(acc_full, UNITS * i + u + 1)
                    act.wait_ge(out_stored[u % 2], OUT_DMAS * QUADS * (2 * i + u // 2 + 1))
                    nc.scalar.copy(heads_out[:, u % 2], acc[:]).then_inc(acc_free, 1)

                for s in range(SLOTS):
                    act.wait_ge(probs_used, s + 1)
                    for t in (2 * s, 2 * s + 1):
                        act.wait_ge(tile_full, t + 1)
                        nc.scalar.activation(probs[:, t % 4], tile[t % 2][:].rearrange("p a b -> p (a b)"), ACT.Exp,
                                             scale=1.0 / (SCALE * SCALE * HEAD_DIM ** 0.5)).then_inc(exp_done, 1)
                    if s % UNIT_SLOTS == 0 and s > 0:
                        take_unit(s // UNIT_SLOTS - 1)
                    for c in range(CHUNKS):
                        if hi_slot[c] == s:
                            cast(c, i + 1)
                take_unit(UNITS - 1)
                act.drain()
                act.sem_inc(probs_used, -SLOTS)
                act.sem_inc(tile_full, -EXPS)

        @block.vector
        def _(dve):
            def ring_bank(n):
                return ring[:, n % RING]

            def max_block(slot, b, i):
                h, q = b // BLOCKS % 2, b % BLOCKS
                out = part_max[:, b // UNIT_SLOTS % 2, b % UNIT_SLOTS]
                for k in range(ITEMS):
                    n = ring_item(slot, k)
                    if q == 0 and k == 0:
                        dve.wait_ge(mask_in[h], QUADS * (i + 1 + b // SLOTS))
                    dve.wait_ge(ring_full, n + AHEAD_ITEMS + 1)
                    if k < ITEMS - 1:
                        nc.vector.tensor_reduce(out[:, k:k + 1], ring_bank(n), AX.X, ALU.max).then_inc(ring_free, 1)
                        continue
                    nc.vector.tensor_reduce(out[:, 3:4], ring_bank(n)[:, 0:3 * P], AX.X,
                                            ALU.max).then_inc(blocks_seen, 1)
                    nc.vector.tensor_tensor_reduce(out=diag[h][:, q], in0=ring_bank(n)[:, 3 * P:4 * P], in1=mask[h][:],
                                                   scale=1.0, scalar=-3.0e38, op0=ALU.mult, op1=ALU.max,
                                                   accum_out=out[:, 4:5]).then_inc(ring_free, 1)

            def finish_max(par, seen, count):
                dve.wait_ge(blocks_seen, seen)
                if count is not None:
                    dve.wait_ge(diag_ready, count)
                nc.vector.tensor_reduce(row_max[:, par], part_max[:, par], AX.X, ALU.max).then_inc(max_ready, 1)

            def split_max(slot, unit_count):
                n = ring_item(slot, ITEMS)
                dve.wait_ge(ring_full, n + AHEAD_ITEMS + 1)
                if unit_count is not None:
                    dve.wait_ge(rows_in, ROW_DMAS * QUADS * unit_count)
                src = ring_bank(n)[0:UNIT_SLOTS, 0:P]
                nc.vector.tensor_scalar(max_hi[:], src, -1.0 / MAXUNIT, None, ALU.mult).then_inc(max_seen, 1)
                dve.wait_ge(max_seen, (unit_count if unit_count is not None else 0) + 1)
                nc.vector.scalar_tensor_tensor(out=max_lo[:], in0=src, scalar=-1.0 / MAXUNIT, in1=max_hi[:],
                                               op0=ALU.mult, op1=ALU.subtract).then_inc(rows_ready, 1)
                nc.vector.tensor_copy(scrap[:], src[:, 0:1]).then_inc(ring_free, 1)

            for h in range(2):
                nc.vector.memset(k_stack[h][STACK:STACK + MAXROWS], MAXUNIT).then_inc(const_ready, 1)
            for s in range(-LEAD, 0):
                max_block(s, s + LEAD, 0)
                if s % UNIT_SLOTS == RED_SLOT and s + LEAD >= UNIT_SLOTS:
                    finish_max(0, s + LEAD + 1, None)
                if s % UNIT_SLOTS == TURN_SLOT and s + LEAD >= UNIT_SLOTS:
                    split_max(s, None)
            with dve.Fori(0, STEPS) as i:
                for s in range(SLOTS):
                    max_block(s, s + LEAD, i)
                    u = s // UNIT_SLOTS + 1
                    if s % UNIT_SLOTS == RED_SLOT:
                        finish_max(u % 2, SLOTS * i + s + LEAD + 1, UNITS * i + u)
                    if s % UNIT_SLOTS == TURN_SLOT:
                        split_max(s, UNITS * i + u)
                dve.drain()
                dve.sem_inc(ring_full, -RING_STEP)

        @block.tensor
        def _(pe):
            def max_scores(slot, b, ks, i):
                h, q = b // BLOCKS % 2, b % BLOCKS
                parts = score_parts(q, None)
                banks = [[parts[0]], [parts[1]], [parts[2]], parts[3:]]
                for k in ks:
                    n = ring_item(slot, k)
                    if n + AHEAD_ITEMS - RING + 1 > 0:
                        pe.wait_ge(ring_free, n + AHEAD_ITEMS - RING + 1)
                    col = 0
                    for j, (level, first, width) in enumerate(banks[k]):
                        if q == 0 and (k == 0 or k >= 2):
                            pe.wait_ge(stack_in[h][level], STACK_DMAS * QUADS * (i + 1 + b // SLOTS))
                        last = nc.tensor.matmul(ring[:, n % RING, col:col + width],
                                                q_stack[h][0:STACK, level, q * P:(q + 1) * P],
                                                k_stack[h][0:STACK, level, first:first + width],
                                                start=(j == 0), stop=True, skip_group_check=True)
                        col += width
                    last.then_inc(ring_full, 1)

            def turn_max(slot, par, count):
                n = ring_item(slot, ITEMS)
                pe.wait_ge(ring_free, n + AHEAD_ITEMS - RING + 1)
                pe.wait_ge(max_ready, count)
                nc.tensor.transpose(ring[0:UNIT_SLOTS, n % RING, 0:P], row_max[:, par], ident[:]).then_inc(ring_full, 1)

            def scores(t):
                u, kb = t // BLOCKS, t % BLOCKS
                h, half = u // 2, u % 2
                pe.wait_ge(exp_done, t + 1)
                started = set()
                for level, first, width in score_parts(kb, half):
                    col = first - half * HALF
                    bank, at = col // 512, col % 512
                    out = tile[t % 2][:, bank, at:at + width]
                    if level == RAW:
                        last = nc.tensor.matmul(out, diag[h][:, kb], ident[:], is_transpose=True,
                                                start=bank not in started, stop=True, skip_group_check=True)
                    else:
                        last = nc.tensor.matmul(out, k_stack[h][:, level, kb * P:(kb + 1) * P],
                                                q_stack[h][:, level, first:first + width],
                                                start=bank not in started, stop=True, skip_group_check=True)
                    started.add(bank)
                last.then_inc(tile_full, 1)

            def products(j):
                u = j // UNIT_SLOTS
                h = u // 2
                for par in range(2):
                    t = 2 * j + par
                    pe.wait_ge(exp_done, t + 3)
                    for qt in range(2):
                        row = (2 * par + qt) * ROWS
                        last = nc.tensor.matmul(acc[row:row + ROWS], v_ones[h][:, t % BLOCKS],
                                                probs[:, t % 4, qt * 512:(qt + 1) * 512],
                                                start=(j % UNIT_SLOTS == 0), stop=(j % UNIT_SLOTS == UNIT_SLOTS - 1),
                                                skip_group_check=True)
                        if j % (2 * UNIT_SLOTS) == 2 * UNIT_SLOTS - 1 and (par, qt) == (0, 0):
                            last.then_inc(stack_free[h], 1)
                        if j % UNIT_SLOTS == UNIT_SLOTS - 1 and (par, qt) == (0, 1):
                            last.then_inc(probs_used, 1)
                last.then_inc(acc_full if j % UNIT_SLOTS == UNIT_SLOTS - 1 else probs_used, 1)

            pe.wait_ge(const_ready, 2)
            pe.sem_inc(probs_used, 2)
            pe.sem_inc(stack_free[1], 1)
            for s in range(-LEAD, 0):
                max_scores(s, s + LEAD, range(ITEMS), 0)
                if s % UNIT_SLOTS == TURN_SLOT and s + LEAD >= UNIT_SLOTS:
                    turn_max(s, 0, 1)
            with pe.Fori(0, STEPS) as i:
                for s in range(SLOTS):
                    if s % UNIT_SLOTS == 0:
                        u = s // UNIT_SLOTS
                        pe.wait_ge(rows_in, ROW_DMAS * QUADS * (UNITS * i + u + 1))
                        pe.wait_ge(diag_ready, UNITS * i + u + 2)
                    scores(2 * s)
                    max_scores(s, s + LEAD, (0, 1), i)
                    scores(2 * s + 1)
                    if s == SLOTS - 1:
                        products(s - 1)
                    max_scores(s, s + LEAD, (2, 3), i)
                    if s % UNIT_SLOTS == TURN_SLOT:
                        turn_max(s, (s // UNIT_SLOTS + 1) % 2, UNITS * i + s // UNIT_SLOTS + 2)
                    j = s if s == SLOTS - 1 else s - 1
                    if j >= 0:
                        if j % UNIT_SLOTS == 0:
                            pe.wait_ge(acc_free, UNITS * i + j // UNIT_SLOTS + 1)
                        if j % (2 * UNIT_SLOTS) == 0:
                            pe.wait_ge(v_in[j // (2 * UNIT_SLOTS)], QUADS * (i + 1))
                        products(j)
                pe.drain()
                pe.sem_inc(exp_done, -EXPS)
                pe.sem_inc(ring_free, -RING_STEP)


def ffn_block(nc, a, keep, scr, out):
    ident, w1t, w2t, wot = keep["ident"], keep["w1t"], keep["w2t"], keep["wot"]
    with ExitStack() as ctx:
        def sb(name, shape, dt=F32):
            return ctx.enter_context(nc.sbuf_tensor(name, shape, dt))

        def sem(name):
            return ctx.enter_context(nc.semaphore(name))

        sums_in = sb("sums_in", [P, 2, EC, 2, 2, GROUP])
        x_in = sb("x_res", [P, 2, TILES, EMBED])
        sums = sb("sums", [P, EC, 2, GROUP])
        heads = sb("heads", [P, EC, GROUP])
        x_bias = sb("x_bias", [P, TILES, EMBED])
        y = sb("y", [P, TILES, EMBED])
        y_bias = sb("y_bias", [P, 2, TILES, EMBED])
        z = sb("z", [P, TILES, EMBED])
        z_hi = sb("z_hi", [P, EC, GROUP], F16)
        z_lo = sb("z_lo", [P, EC, GROUP], F16)
        hidden = sb("hidden", [P, FC, GROUP])
        h_hi = sb("h_hi", [P, FC, GROUP], F16)
        h_lo = sb("h_lo", [P, FC, GROUP], F16)
        result = sb("result", [P, 2, TILES, EMBED])
        stats = sb("stats2", [P, TILES, 6])
        mv = sb("mv2", [P, TILES, 2])
        rstd = sb("rstd2", [P, TILES])
        spare = sb("spare2", [P, 1])
        up = ctx.enter_context(nc.psum_tensor("up", [P, 2, GROUP], F32))
        attn = ctx.enter_context(nc.psum_tensor("attn", [P, TILES, EMBED], F32))
        turn = ctx.enter_context(nc.psum_tensor("turn2", [P, EC, GROUP], F32))
        down = ctx.enter_context(nc.psum_tensor("down", [P, TILES, EMBED], F32))

        loaded = [sem(f"loaded{u}") for u in range(2)]
        stored = [sem(f"out_done{u}") for u in range(2)]
        heads_ready, x_bias_ready, attn_done, y_ready, y_bias_ready = (
            sem("heads_ready"), sem("x_bias_ready"), sem("attn_done"), sem("y_ready"), sem("y_bias_ready"))
        sqrt_in, sqrt_out, z_ready, turned = sem("sqrt_in2"), sem("sqrt_out2"), sem("z_ready"), sem("turned2")
        z_hi_ready, z_lo_ready = sem("z_hi_ready"), sem("z_lo_ready")
        up_done, up_taken, h_hi_ready, h_lo_ready = sem("up_done"), sem("up_taken"), sem("h_hi_ready"), sem("h_lo_ready")
        down_done, result_ready, dve_step = sem("down_done"), sem("result_ready"), sem("dve_step2")
        LOADS = EC + 1
        DVE_STEPS = 5
        LOOPED = GROUPS - 2
        block = ctx.enter_context(nc.Block())
        x_groups = a["x"].rearrange("b s e -> (b s) e").rearrange("(g t p) e -> g p t e", t=TILES, p=P)
        out_groups = out.rearrange("b s e -> (b s) e").rearrange("(g t p) e -> g p t e", t=TILES, p=P)
        out_scr = scr["out"].rearrange("(b c) r k p t -> b c p (r k) t", c=EC)

        def each_group(eng, body):
            with eng.Fori(0, LOOPED // 2) as i:
                for u in range(2):
                    body(2 * i + u, u, True)
            body(GROUPS - 2, 0, True)
            body(GROUPS - 1, 1, False)

        @block.sync
        def _(sp):
            def load(g, u):
                b, at = g // (SEQ // GROUP), (g % (SEQ // GROUP)) * GROUP
                for c in range(EC):
                    sp.dma_start(sums_in[:, u, c],
                                 out_scr[b, c, :, :, bass.ds(at, GROUP)]).then_inc(loaded[u], QUADS)
                sp.dma_start(x_in[:, u], x_groups[g]).then_inc(loaded[u], QUADS)

            def body(g, u, more, load_next=True):
                if load_next:
                    sp.wait_ge(heads_ready, g + 1)
                    sp.wait_ge(x_bias_ready, g + 1)
                    load(g + 2, u)
                sp.wait_ge(result_ready, g + 2)
                sp.dma_start(out_groups[g], result[:, u]).then_inc(stored[u], QUADS)

            for u in range(2):
                sp.sem_inc(stored[u], QUADS)
            load(0, 0)
            load(1, 1)
            with sp.Fori(0, LOOPED // 2) as i:
                for u in range(2):
                    body(2 * i + u, u, True)
            body(GROUPS - 2, 0, True, load_next=False)
            body(GROUPS - 1, 1, False, load_next=False)
            for u in range(2):
                sp.wait_ge(stored[u], (GROUPS // 2 + 1) * QUADS)

        @block.gpsimd
        def _(pool):
            def add_out_bias(g, u):
                pool.wait_ge(loaded[u], LOADS * QUADS * (g // 2 + 1))
                nc.gpsimd.tensor_tensor(x_bias[:], x_in[:, u], lead(keep["bo_all"][:], TILES), ALU.add
                                        ).then_inc(x_bias_ready, 1)

            def add_ffn_bias(g, u, seen):
                pool.wait_ge(y_ready, g + 1)
                pool.wait_ge(result_ready, seen)
                nc.gpsimd.tensor_tensor(y_bias[:, u], y[:], lead(keep["b2_all"][:], TILES), ALU.add
                                        ).then_inc(y_bias_ready, 1)

            def body(g, u, more):
                if more:
                    add_out_bias(g + 1, 1 - u)
                for f in range(FC):
                    pool.wait_ge(h_hi_ready, FC * g + f + 1)
                    nc.gpsimd.tensor_tensor(h_lo[:, f], hidden[:, f], h_hi[:, f], ALU.subtract).then_inc(h_lo_ready, 1)
                if more:
                    add_ffn_bias(g + 1, 1 - u, g + 1)

            add_out_bias(0, 0)
            add_ffn_bias(0, 0, 1)
            each_group(pool, body)

        @block.scalar
        def _(act):
            def root(g):
                act.wait_ge(sqrt_in, g + 1)
                nc.scalar.activation(rstd[:], rstd[:], ACT.Sqrt).then_inc(sqrt_out, 1)

            def split_z(g):
                act.wait_ge(turned, g + 1)
                nc.scalar.copy(z_hi[:], turn[:]).then_inc(z_hi_ready, 1)

            def body(g, u, more):
                for f in range(FC):
                    act.wait_ge(up_done, FC * g + f + 1)
                    nc.scalar.activation(hidden[:, f], up[:, f % 2], ACT.Relu, bias=keep["b1_col"][:, f:f + 1]
                                         ).then_inc(up_taken, 1)
                if more:
                    root(g + 1)
                    split_z(g + 1)

            act.sem_inc(up_taken, 1)
            root(0)
            split_z(0)
            each_group(act, body)

        @block.vector
        def _(dve):
            def divide(g, u):
                dve.wait_ge(loaded[u], LOADS * QUADS * (g // 2 + 1))
                nc.vector.tensor_tensor(sums[:], sums_in[:, u, :, 0], sums_in[:, u, :, 1], ALU.add).then_inc(dve_step, 1)
                dve.wait_ge(dve_step, DVE_STEPS * g + 1)
                nc.vector.reciprocal(sums[:, :, 1], sums[:, :, 1]).then_inc(dve_step, 1)
                dve.wait_ge(dve_step, DVE_STEPS * g + 2)
                nc.vector.tensor_tensor(heads[:], sums[:, :, 0], sums[:, :, 1], ALU.mult).then_inc(heads_ready, 1)

            def residual(g):
                dve.wait_ge(attn_done, g + 1)
                dve.wait_ge(x_bias_ready, g + 1)
                if not (isinstance(g, int) and g == 0):
                    dve.wait_ge(y_bias_ready, g)
                nc.vector.tensor_tensor(y[:], attn[:], x_bias[:], ALU.add).then_inc(y_ready, 1)
                dve.wait_ge(y_ready, g + 1)
                taken = [2]

                def step(ins):
                    taken[0] += 1
                    ins.then_inc(dve_step, 1)
                    dve.wait_ge(dve_step, DVE_STEPS * g + taken[0])

                normalize(nc, dve, y, z, stats, mv, rstd, spare, step, sqrt_in, sqrt_out, g + 1,
                          lambda ins: ins.then_inc(z_ready, 1))

            def rest_z(g):
                dve.wait_ge(z_hi_ready, g + 1)
                nc.vector.tensor_tensor(z_lo[:], turn[:], z_hi[:], ALU.subtract).then_inc(z_lo_ready, 1)

            def body(g, u, more):
                if more:
                    divide(g + 1, 1 - u)
                for f in range(FC):
                    dve.wait_ge(up_taken, FC * g + f + 2)
                    nc.vector.tensor_copy(h_hi[:, f], hidden[:, f]).then_inc(h_hi_ready, 1)
                if more:
                    residual(g + 1)
                dve.wait_ge(down_done, g + 1)
                dve.wait_ge(y_bias_ready, g + 1)
                dve.wait_ge(stored[u], QUADS * (g // 2 + 1))
                nc.vector.tensor_tensor(result[:, u], down[:], y_bias[:, u], ALU.add).then_inc(result_ready, 1)
                if more:
                    rest_z(g + 1)

            dve.sem_inc(result_ready, 1)
            divide(0, 0)
            residual(0)
            rest_z(0)
            each_group(dve, body)

        @block.tensor
        def _(pe):
            def attn_product(g):
                pe.wait_ge(heads_ready, g + 1)
                if not (isinstance(g, int) and g == 0):
                    pe.wait_ge(y_ready, g)
                for t in range(TILES):
                    for c in range(EC):
                        last = nc.tensor.matmul(attn[:, t], heads[:, c, t * P:(t + 1) * P], wot[:, c],
                                                start=(c == 0), stop=(c == EC - 1), skip_group_check=True)
                last.then_inc(attn_done, 1)

            def turn_z(g):
                pe.wait_ge(z_ready, g + 1)
                if not (isinstance(g, int) and g == 0):
                    pe.wait_ge(z_lo_ready, g)
                for c in range(EC):
                    for t in range(TILES):
                        last = nc.tensor.transpose(turn[:, c, t * P:(t + 1) * P], z[:, t, c * P:(c + 1) * P], ident[:])
                last.then_inc(turned, 1)

            def body(g, u, more):
                pe.wait_ge(z_lo_ready, g + 1)
                for f in range(FC):
                    pe.wait_ge(up_taken, FC * g + max(f, 1))
                    k = 0
                    for c in range(EC):
                        for part in (z_hi, z_lo):
                            last = nc.tensor.matmul(up[:, f % 2], w1t[:, c, f * P:(f + 1) * P], part[:, c],
                                                    start=(k == 0), stop=(k == 2 * EC - 1))
                            k += 1
                    last.then_inc(up_done, 1)
                if more:
                    attn_product(g + 1)
                pe.wait_ge(result_ready, g + 1)
                for f in range(FC):
                    pe.wait_ge(h_lo_ready, FC * g + f + 1)
                    for part in (h_hi, h_lo):
                        for t in range(TILES):
                            last = nc.tensor.matmul(down[:, t], part[:, f, t * P:(t + 1) * P], w2t[:, f],
                                                    start=(f == 0 and part is h_hi and t % 2 == 0),
                                                    stop=(f == FC - 1 and part is h_lo), skip_group_check=True)
                last.then_inc(down_done, 1)
                if more:
                    turn_z(g + 1)

            attn_product(0)
            turn_z(0)
            each_group(pe, body)


INPUTS = {"x": "L0_attn_x", "Wq": "L0_attn_Wq", "bq": "L0_attn_bq", "Wk": "L0_attn_Wk", "bk": "L0_attn_bk",
          "Wv": "L0_attn_Wv", "bv": "L0_attn_bv", "Wo": "L0_attn_Wo", "bo": "L0_attn_bo",
          "decay": "L0_attn_decay_params", "mix": "L0_attn_mix_weights",
          "W1": "L0_ffn_W1", "b1": "L0_ffn_b1", "W2": "L0_ffn_W2", "b2": "L0_ffn_b2"}


def build(nc, a, out):
    scr = {
        "qk": nc.dram_tensor("qk_scratch", [BATCH, 2, 8, 2, DECAYS, HEAD_DIM, SEQ], F32).ap(),
        "v": nc.dram_tensor("v_scratch", [BATCH, HEADS, P, BLOCKS, ROWS], F32).ap(),
        "table": nc.dram_tensor("table_scratch", [PAIRS, P, 2 * HALF], F32).ap(),
        "hat": nc.dram_tensor("hat_scratch", [HEADS, 2 * P], F32).ap(),
        "mask": nc.dram_tensor("mask_scratch", [HEADS, P, P], F32).ap(),
        "out": nc.dram_tensor("out_scratch", [BATCH * EC, 2, 2, P, SEQ], F32).ap(),
    }
    with ExitStack() as ctx:
        def sb(name, shape, dt=F32):
            return ctx.enter_context(nc.sbuf_tensor(name, shape, dt))

        keep = {"ident": sb("ident", [P, P]), "w1t": sb("w1t", [P, EC, FF], F16), "w2t": sb("w2t", [P, FC, EMBED], F16),
                "wot": sb("wot", [P, EC, EMBED]), "bo_all": sb("bo_all", [P, EMBED]), "b2_all": sb("b2_all", [P, EMBED]),
                "b1_col": sb("b1_col", [P, FC])}
        with ExitStack() as first:
            def sb1(name, shape, dt=F32):
                return first.enter_context(nc.sbuf_tensor(name, shape, dt))

            early = {"wqkvt": sb1("wqkvt", [P, 3, EC, EMBED]), "qscale": sb1("qscale", [P, 2, DECAYS]),
                     "qbias": sb1("qbias", [P, 2, DECAYS]), "kbias": sb1("kbias", [P, 2]),
                     "bv_all": sb1("bv_all", [P, EMBED])}
            setup_block(nc, a, keep, early, scr)
            token_block(nc, a, keep, early, scr)
        attention_block(nc, keep, scr)
        ffn_block(nc, a, keep, scr, out)


def kernel(**inputs):
    import numpy as np
    import concourse.bacc as bacc
    from concourse.bass_utils import run_bass_kernel_spmd

    nc = bacc.Bacc("TRN2", target_bir_lowering=False, num_devices=1)
    arrays, a = {}, {}
    for short, name in INPUTS.items():
        array = np.ascontiguousarray(inputs[name])
        arrays[f"in_{short}"] = array
        a[short] = nc.dram_tensor(f"in_{short}", array.shape, mybir.dt.from_np(array.dtype), kind="ExternalInput").ap()
    out = nc.dram_tensor("out", (BATCH, SEQ, EMBED), F32, kind="ExternalOutput").ap()
    build(nc, a, out)
    result = run_bass_kernel_spmd(nc, [arrays], core_ids=[0])
    return result.results[0]["out"]
```

```python
from contextlib import ExitStack

import concourse.bass as bass
from concourse import mybir

F32 = mybir.dt.float32
F16 = mybir.dt.float16
ALU = mybir.AluOpType
ACT = mybir.ActivationFunctionType
AX = mybir.AxisListType

P = 128
BATCH, SEQ, EMBED = 2, 2048, 256
HEADS, HEAD_DIM, DECAYS = 16, 16, 2
FF = 4 * EMBED
EC = EMBED // P
FC = FF // P
BLOCKS = SEQ // P
PAIRS = HEADS // 2
STEPS = BATCH * PAIRS
GROUP = 512
TILES = GROUP // P
GROUPS = BATCH * SEQ // GROUP
HALF = SEQ // 2
LEVELS = (1024, 512, 256, 128)
RAW = len(LEVELS)
ROWS = DECAYS * HEAD_DIM
STACK = 3 * ROWS
MAXROWS = 2
SCALE = 32.0
MAXUNIT = 1024.0
LN_EPS = 1e-5
Q_EPS = 1e-5
QUADS = 16


def lead(ap, n):
    p, x = ap.shape
    return ap.unsqueeze(1).broadcast_to([p, n, x])


def setup_block(nc, a, keep, early, scr):
    ident, w1t, w2t, wot = keep["ident"], keep["w1t"], keep["w2t"], keep["wot"]
    wqkvt, qscale, qbias = early["wqkvt"], early["qscale"], early["qbias"]
    kbias, bv_all = early["kbias"], early["bv_all"]
    NTAB = PAIRS
    with ExitStack() as ctx:
        def sb(name, shape, dt=F32):
            return ctx.enter_context(nc.sbuf_tensor(name, shape, dt))

        def sem(name):
            return ctx.enter_context(nc.semaphore(name))

        wn = sb("wn", [P, 4, EC, EMBED])
        w1n = sb("w1n", [P, FC, EMBED])
        w2n = sb("w2n", [P, EC, FF])
        ternary = sb("ternary", [P, 2, FF * EC])
        below = sb("below", [P, FF * EC])
        decay_rows = sb("decay_rows", [P, NTAB])
        table = sb("table", [P, NTAB, 2 * HALF])
        mix_rows = sb("mix_rows", [P, 2, DECAYS])
        mix_w = sb("mix_w", [P, 2, DECAYS])
        mix_m = sb("mix_m", [P, 2, 1])
        q_bias_in = sb("q_bias_in", [P, 2])
        k_bias_in = sb("k_bias_in", [P, 2])
        decay_h = sb("decay_h", [HEADS, DECAYS])
        mix_h = sb("mix_h", [HEADS, DECAYS])
        mix_hw = sb("mix_hw", [HEADS, DECAYS])
        mix_hm = sb("mix_hm", [HEADS, 1])
        power_up = sb("power_up", [HEADS, DECAYS, P])
        power_down = sb("power_down", [HEADS, DECAYS, P])
        hat = sb("hat", [HEADS, 2 * P])
        hankel = sb("hankel", [P, HEADS, P])
        flip = sb("flip", [P, P])
        masks = sb("masks", [P, HEADS, P])
        ones = sb("ones", [P, P])
        abs_sum = sb("abs_sum", [P, 2])
        cut = sb("cut", [P, 2])
        neg_cut = sb("neg_cut", [P, 2])
        bank = ctx.enter_context(nc.psum_tensor("setup_bank", [P, 8, 512], F32))

        w_in, ffn_in, small_in = sem("w_in"), sem("ffn_in"), sem("small_in")
        ident_done, ones_done, turned, turned_out = sem("ident_done"), sem("ones_done"), sem("turned"), sem("turned_out")
        dve_step, pool_step, act_step = sem("dve_step"), sem("pool_step"), sem("act_step")
        sums_ready, total_ready, ternary_ready = sem("sums_ready"), sem("total_ready"), sem("ternary_ready")
        hat_ready, hat_stored, hankel_in = sem("hat_ready"), sem("hat_stored"), sem("hankel_in")
        flipped, masks_ready, table_ready, stored = sem("flipped"), sem("masks_ready"), sem("table_ready"), sem("stored")
        mix_exp, mix_diff = sem("mix_exp"), sem("mix_diff")
        block = ctx.enter_context(nc.Block())

        @block.sync
        def _(sp):
            for m, name in enumerate(("Wq", "Wk", "Wv", "Wo")):
                sp.dma_start(wn[:, m], a[name].rearrange("(c p) e -> p c e", p=P)).then_inc(w_in, QUADS)
            sp.dma_start(w1n[:], a["W1"].rearrange("(c p) e -> p c e", p=P)).then_inc(ffn_in, QUADS)
            sp.dma_start(w2n[:], a["W2"].rearrange("(c p) f -> p c f", p=P)).then_inc(ffn_in, QUADS)
            sp.wait_ge(hat_ready, 1)
            sp.dma_start(scr["hat"], hat[:]).then_inc(hat_stored, QUADS)
            sp.wait_ge(hat_stored, QUADS)
            windows = bass.AP(scr["hat"].tensor, 0, [[1, P], [2 * P, HEADS], [1, P]])
            sp.dma_start(hankel[:], windows).then_inc(hankel_in, QUADS)
            sp.wait_ge(table_ready, 2)
            sp.dma_start(scr["table"].rearrange("t p x -> p t x"), table[:]).then_inc(stored, QUADS)
            sp.wait_ge(masks_ready, 4)
            sp.dma_start(scr["mask"].rearrange("h p x -> p h x"), masks[:]).then_inc(stored, QUADS)
            sp.wait_ge(stored, 2 * QUADS)

        @block.gpsimd
        def _(pool):
            nc.gpsimd.memset(ident[:], 0.0).then_inc(pool_step, 1)
            nc.gpsimd.memset(flip[:], 0.0).then_inc(pool_step, 1)
            pool.wait_ge(pool_step, 2)
            nc.gpsimd.affine_select(out=ident[:], in_=ident[:], compare_op=ALU.not_equal, fill=1.0, base=0,
                                    pattern=[[-1, P]], channel_multiplier=1).then_inc(ident_done, 1)
            nc.gpsimd.affine_select(out=flip[:], in_=flip[:], compare_op=ALU.not_equal, fill=1.0, base=1 - P,
                                    pattern=[[1, P]], channel_multiplier=1).then_inc(ident_done, 1)
            pool.wait_ge(dve_step, 2)
            step = 2
            n = 1
            while n < HALF:
                part = table[:, :, 2 * HALF - n:2 * HALF]
                top = table[:, :, 2 * HALF - n:2 * HALF - n + 1].broadcast_to([P, NTAB, n])
                ins = nc.gpsimd.tensor_tensor(table[:, :, 2 * HALF - 2 * n:2 * HALF - n], part, top, ALU.mult)
                n *= 2
                if n < HALF:
                    step += 1
                    ins.then_inc(pool_step, 1)
                    pool.wait_ge(pool_step, step)
                else:
                    ins.then_inc(table_ready, 1)

        @block.scalar
        def _(act):
            for name, tile in (("bo", keep["bo_all"]), ("b2", keep["b2_all"]), ("bv", bv_all)):
                src = bass.AP(a[name].tensor, 0, [[0, P], [1, EMBED]])
                act.dma_start(tile[:], src).then_inc(small_in, QUADS)
            act.dma_start(keep["b1_col"][:], a["b1"].rearrange("(c p) -> p c", p=P), allow_slow_non_contiguous=True).then_inc(small_in, QUADS)
            act.dma_start(q_bias_in[:], a["bq"].rearrange("(c p) -> p c", p=P), allow_slow_non_contiguous=True).then_inc(small_in, QUADS)
            act.dma_start(k_bias_in[:], a["bk"].rearrange("(c p) -> p c", p=P), allow_slow_non_contiguous=True).then_inc(small_in, QUADS)
            act.dma_start(decay_h[:], a["decay"]).then_inc(small_in, QUADS)
            act.dma_start(mix_h[:], a["mix"]).then_inc(small_in, QUADS)
            for m in range(2):
                src = bass.AP(a["mix"].tensor, m * 8 * DECAYS, [[DECAYS, 8], [0, HEAD_DIM], [1, DECAYS]])
                act.dma_start(mix_rows[:, m, :], src).then_inc(small_in, QUADS)
            for r in range(8):
                src = bass.AP(a["decay"].tensor, (r // 4) * DECAYS + r % 2, [[0, HEAD_DIM], [2 * DECAYS, NTAB]])
                act.dma_start(decay_rows[HEAD_DIM * r:HEAD_DIM * (r + 1), :], src,
                              allow_slow_non_contiguous=True).then_inc(small_in, QUADS)
            act.wait_ge(mix_diff, 2)
            nc.scalar.activation(mix_w[:], mix_w[:], ACT.Exp).then_inc(mix_exp, 1)
            nc.scalar.activation(mix_hw[:], mix_hw[:], ACT.Exp).then_inc(mix_exp, 1)
            for m in range(4):
                act.wait_ge(turned, m + 1)
                dst = wot[:] if m == 3 else wqkvt[:, m]
                nc.scalar.copy(dst.rearrange("p c f -> p (c f)"), bank[:, m]).then_inc(turned_out, 1)

        @block.vector
        def _(dve):
            steps = [0]

            def then(ins):
                steps[0] += 1
                ins.then_inc(dve_step, 1)
                dve.wait_ge(dve_step, steps[0])

            small = 18 * QUADS
            dve.wait_ge(small_in, small)
            nc.vector.memset(ones[:], 1.0).then_inc(ones_done, 1)
            then(nc.vector.tensor_scalar(decay_rows[:], decay_rows[:], 0.01, 0.9999, ALU.max, ALU.min))
            then(nc.vector.tensor_copy(table[:, :, 2 * HALF - 1], decay_rows[:]))
            nc.vector.memset(table[:, :, 0:1], 1.0)
            then(nc.vector.tensor_copy(table[:, :, 1], decay_rows[:]))
            nc.vector.tensor_reduce(mix_m[:], mix_rows[:], AX.X, ALU.max)
            then(nc.vector.tensor_reduce(mix_hm[:], mix_h[:], AX.X, ALU.max))
            nc.vector.tensor_tensor(mix_w[:], mix_rows[:], mix_m[:].broadcast_to([P, 2, DECAYS]),
                                    ALU.subtract).then_inc(mix_diff, 1)
            nc.vector.tensor_scalar(mix_hw[:], mix_h[:], mix_hm[:, 0:1], None, ALU.subtract).then_inc(mix_diff, 1)
            then(nc.vector.tensor_scalar(decay_h[:], decay_h[:], 0.01, 0.9999, ALU.max, ALU.min))
            dve.wait_ge(mix_exp, 2)
            nc.vector.tensor_reduce(mix_m[:], mix_w[:], AX.X, ALU.add)
            then(nc.vector.tensor_reduce(mix_hm[:], mix_hw[:], AX.X, ALU.add))
            nc.vector.reciprocal(mix_m[:], mix_m[:])
            then(nc.vector.reciprocal(mix_hm[:], mix_hm[:]))
            nc.vector.tensor_tensor(mix_w[:], mix_w[:], mix_m[:].broadcast_to([P, 2, DECAYS]), ALU.mult)
            then(nc.vector.tensor_scalar(mix_hw[:], mix_hw[:], mix_hm[:, 0:1], None, ALU.mult))
            nc.vector.tensor_scalar(kbias[:], k_bias_in[:], SCALE, None, ALU.mult)
            then(nc.vector.tensor_scalar(qscale[:], mix_w[:], SCALE, None, ALU.mult))
            nc.vector.tensor_tensor(qbias[:], qscale[:], q_bias_in[:].unsqueeze(2).broadcast_to([P, 2, DECAYS]), ALU.mult)
            nc.vector.memset(power_up[:, :, 0:1], 1.0)
            nc.vector.tensor_copy(power_up[:, :, 1], decay_h[:])
            then(nc.vector.tensor_copy(power_down[:, :, P - 1], decay_h[:]))
            n = 1
            while n < P:
                top = min(n, P - 1 - n)
                if top > 0:
                    nc.vector.tensor_tensor(power_up[:, :, n + 1:n + 1 + top], power_up[:, :, 1:1 + top],
                                            power_up[:, :, n:n + 1].broadcast_to([HEADS, DECAYS, top]), ALU.mult)
                then(nc.vector.tensor_tensor(power_down[:, :, P - 2 * n:P - n], power_down[:, :, P - n:P],
                                             power_down[:, :, P - n:P - n + 1].broadcast_to([HEADS, DECAYS, n]), ALU.mult))
                n *= 2
            nc.vector.memset(hat[:, 2 * P - 1:2 * P], 0.0)
            nc.vector.tensor_scalar(hat[:, 0:P - 1], power_down[:, 0, 1:P], mix_hw[:, 0:1], None, ALU.mult)
            then(nc.vector.tensor_scalar(hat[:, P - 1:2 * P - 1], power_up[:, 0, :], mix_hw[:, 0:1], None, ALU.mult))
            nc.vector.scalar_tensor_tensor(out=hat[:, 0:P - 1], in0=power_down[:, 1, 1:P], scalar=mix_hw[:, 1:2],
                                           in1=hat[:, 0:P - 1], op0=ALU.mult, op1=ALU.add)
            nc.vector.scalar_tensor_tensor(out=hat[:, P - 1:2 * P - 1], in0=power_up[:, 1, :], scalar=mix_hw[:, 1:2],
                                           in1=hat[:, P - 1:2 * P - 1], op0=ALU.mult, op1=ALU.add).then_inc(hat_ready, 1)
            n = 1
            while n < HALF:
                top = min(n, HALF - 1 - n)
                if top > 0:
                    ins = nc.vector.tensor_tensor(table[:, :, n + 1:n + 1 + top], table[:, :, 1:1 + top],
                                                  table[:, :, n:n + 1].broadcast_to([P, NTAB, top]), ALU.mult)
                    if 2 * n >= HALF:
                        ins.then_inc(table_ready, 1)
                    else:
                        then(ins)
                n *= 2
            dve.wait_ge(ffn_in, 2 * QUADS)
            flat = (w1n[:].rearrange("p c e -> p (c e)"), w2n[:].rearrange("p c e -> p (c e)"))
            for m in range(2):
                nc.vector.tensor_reduce(abs_sum[:, m:m + 1], flat[m], AX.X, ALU.add,
                                        apply_absolute_value=True).then_inc(sums_ready, 1)
            dve.wait_ge(total_ready, 1)
            then(nc.vector.tensor_scalar(cut[:], bank[:, 4, 0:2], 1.0 / (FF * EMBED), Q_EPS, ALU.mult, ALU.add))
            nc.vector.tensor_scalar(neg_cut[:], cut[:], -0.5, None, ALU.mult)
            then(nc.vector.tensor_scalar(cut[:], cut[:], 0.5, None, ALU.mult))
            for m in range(2):
                then(nc.vector.tensor_scalar(below[:], flat[m], neg_cut[:, m:m + 1], None, ALU.is_lt))
                then(nc.vector.scalar_tensor_tensor(out=ternary[:, m], in0=flat[m], scalar=cut[:, m:m + 1],
                                                    in1=below[:], op0=ALU.is_gt, op1=ALU.subtract))
            nc.vector.tensor_copy(below[:, 0:1], ternary[:, 0, 0:1]).then_inc(ternary_ready, 1)
            for q in range(4):
                dve.wait_ge(flipped, q + 1)
                nc.vector.tensor_copy(masks[:].rearrange("p h x -> p (h x)")[:, q * 512:(q + 1) * 512],
                                      bank[:, 4 + q]).then_inc(masks_ready, 1)
            for q in range(8):
                dve.wait_ge(turned, 4 + q + 1)
                out = (w1t[:, q // 2, (q % 2) * 512:(q % 2 + 1) * 512] if q < 4 else
                       w2t[:, 2 * (q - 4):2 * (q - 4) + 2, :].rearrange("p c e -> p (c e)"))
                nc.vector.tensor_copy(out, bank[:, q])

        @block.tensor
        def _(pe):
            pe.wait_ge(ident_done, 2)
            pe.wait_ge(w_in, 4 * QUADS)
            for m in range(4):
                for ec in range(EC):
                    for fc in range(EC):
                        last = nc.tensor.transpose(bank[:, m, (ec * EC + fc) * P:(ec * EC + fc + 1) * P],
                                                   wn[:, m, fc, ec * P:(ec + 1) * P], ident[:])
                last.then_inc(turned, 1)
            pe.wait_ge(ones_done, 1)
            pe.wait_ge(sums_ready, 2)
            nc.tensor.matmul(bank[:, 4, 0:2], ones[:], abs_sum[:], start=True, stop=True).then_inc(total_ready, 1)
            pe.wait_ge(ternary_ready, 1)
            pe.wait_ge(hankel_in, QUADS)
            for q in range(4):
                nc.tensor.matmul(bank[:, 4 + q], flip[:], hankel[:].rearrange("p h x -> p (h x)")[:, q * 512:(q + 1) * 512],
                                 start=True, stop=True).then_inc(flipped, 1)
            tern1 = ternary[:, 0].rearrange("p (c e) -> p c e", c=FC)
            tern2 = ternary[:, 1].rearrange("p (c f) -> p c f", c=EC)
            for q in range(8):
                if q < 4:
                    pe.wait_ge(turned_out, q + 1)
                else:
                    pe.wait_ge(masks_ready, q - 3)
                for j in range(4):
                    if q < 4:
                        src = tern1[:, (q % 2) * 4 + j, (q // 2) * P:(q // 2 + 1) * P]
                    else:
                        src = tern2[:, j % 2, (2 * (q - 4) + j // 2) * P:(2 * (q - 4) + j // 2 + 1) * P]
                    last = nc.tensor.transpose(bank[:, q, j * P:(j + 1) * P], src, ident[:])
                last.then_inc(turned, 1)


def normalize(nc, dve, x, out, stats, mv, rstd, spare, step, sqrt_in, sqrt_out, sqrt_count, last):
    for t in range(TILES):
        ins = nc.vector.bn_stats(stats[:, t], x[:, t])
    step(ins)
    nc.vector.memset(spare[:], 0.0)
    for t in range(TILES):
        ins = nc.vector.bn_aggr(mv[:, t], stats[:, t])
    step(ins)
    nc.vector.tensor_scalar(rstd[:], mv[:, :, 1], LN_EPS, None, ALU.add).then_inc(sqrt_in, 1)
    dve.wait_ge(sqrt_out, sqrt_count)
    step(nc.vector.reciprocal(rstd[:], rstd[:]))
    for t in range(TILES):
        ins = nc.vector.tensor_scalar(out[:, t], x[:, t], mv[:, t, 0:1], rstd[:, t:t + 1], ALU.subtract, ALU.mult)
    last(ins)


def token_block(nc, a, keep, early, scr):
    ident = keep["ident"]
    wqkvt, qscale, qbias = early["wqkvt"], early["qscale"], early["qbias"]
    kbias, bv_all = early["kbias"], early["bv_all"]
    with ExitStack() as ctx:
        def sb(name, shape, dt=F32):
            return ctx.enter_context(nc.sbuf_tensor(name, shape, dt))

        def sem(name):
            return ctx.enter_context(nc.semaphore(name))

        x_in = sb("x_in", [P, 2, TILES, EMBED])
        x_hat = sb("x_hat", [P, 2, TILES, EMBED])
        x_t = sb("x_t", [P, 2, EC, GROUP])
        q_out = sb("q_out", [P, 2, 2, DECAYS, GROUP])
        k_out = sb("k_out", [P, 2, 2, GROUP])
        v_out = sb("v_out", [P, 2, TILES, HEADS, ROWS])
        stats = sb("stats", [P, TILES, 6])
        mv = sb("mv", [P, TILES, 2])
        rstd = sb("rstd", [P, TILES])
        spare = sb("spare", [P, 1])
        turn = ctx.enter_context(nc.psum_tensor("turn", [P, EC, GROUP], F32))
        v_bank = ctx.enter_context(nc.psum_tensor("v_bank", [P, 2, 512], F32))
        qk_bank = ctx.enter_context(nc.psum_tensor("qk_bank", [P, 4, GROUP], F32))

        x_loaded = [sem(f"x_loaded{u}") for u in range(2)]
        stored = [sem(f"stored{u}") for u in range(2)]
        hat_done, sqrt_in, sqrt_out = sem("hat_done"), sem("sqrt_in"), sem("sqrt_out")
        turned, xt_dve, xt_act = sem("turned"), sem("xt_dve"), sem("xt_act")
        v_done, v_taken, qk_done, q_taken, k_taken = (sem("v_done"), sem("v_taken"), sem("qk_done"),
                                                      sem("q_taken"), sem("k_taken"))
        dve_step, credit = sem("dve_step"), sem("credit")
        DVE_STEPS = 3
        STORES = TILES + 8
        block = ctx.enter_context(nc.Block())
        x_groups = a["x"].rearrange("b s e -> (b s) e").rearrange("(i u t p) e -> i u p t e", u=2, t=TILES, p=P)
        v_scr = scr["v"].rearrange("b h p k c -> b p k h c")

        @block.sync
        def _(sp):
            for u in range(2):
                sp.sem_inc(stored[u], STORES * QUADS)
            with sp.Fori(0, GROUPS // 2) as i:
                for u in range(2):
                    b, half = sp.snap(i // 2), sp.snap(i % 2)
                    at = half * (2 * GROUP) + u * GROUP
                    kb = half * (2 * TILES) + u * TILES
                    g1 = 2 * i + u + 1
                    sp.wait_ge(v_taken, 2 * g1 + 2)
                    for t in range(TILES):
                        sp.dma_start(v_scr[b, :, kb + t], v_out[:, u, t]).then_inc(stored[u], QUADS)
                    sp.wait_ge(q_taken, 2 * g1 + 2)
                    sp.wait_ge(k_taken, 2 * g1 + 2)
                    for m in range(2):
                        for n in range(DECAYS):
                            sp.dma_start(scr["qk"][b, m, :, 1, n, :, bass.ds(at, GROUP)],
                                           k_out[:, u, m, :]).then_inc(stored[u], QUADS)
                    for m in range(2):
                        for n in range(DECAYS):
                            sp.dma_start(scr["qk"][b, m, :, 0, n, :, bass.ds(at, GROUP)],
                                           q_out[:, u, m, n, :]).then_inc(stored[u], QUADS)
            for u in range(2):
                sp.wait_ge(stored[u], (GROUPS // 2 + 1) * STORES * QUADS)

        @block.gpsimd
        def _(pool):
            pool.sem_inc(hat_done, 2)
            with pool.Fori(0, GROUPS // 2) as i:
                for u in range(2):
                    pool.wait_ge(hat_done, 2 * i + u + 1)
                    pool.dma_start(x_in[:, u], x_groups[i, u]).then_inc(x_loaded[u], QUADS)

        @block.vector
        def _(dve):
            nc.vector.memset(v_out[:], 1.0).then_inc(credit, 1)
            dve.wait_ge(credit, 1)
            dve.sem_inc(xt_dve, 1)
            dve.sem_inc(v_taken, 2)
            dve.sem_inc(k_taken, 2)
            with dve.Fori(0, GROUPS // 2) as i:
                for u in range(2):
                    g = 2 * i + u
                    taken = [0]

                    def step(ins, g=g, taken=taken):
                        taken[0] += 1
                        ins.then_inc(dve_step, 1)
                        dve.wait_ge(dve_step, DVE_STEPS * g + taken[0])

                    dve.wait_ge(x_loaded[u], QUADS * (i + 1))
                    dve.wait_ge(turned, g + 1)
                    normalize(nc, dve, x_in[:, u], x_hat[:, u], stats, mv, rstd, spare, step, sqrt_in, sqrt_out, g + 1,
                              lambda ins: ins.then_inc(hat_done, 1))
                    dve.wait_ge(turned, g + 2)
                    dve.wait_ge(qk_done, 4 * g + 4)
                    nc.vector.tensor_copy(x_t[:, u, 1], turn[:, 1]).then_inc(xt_dve, 1)
                    dve.wait_ge(stored[u], STORES * QUADS * (i + 1))
                    for h in range(2):
                        dve.wait_ge(v_done, 2 * g + h + 1)
                        nc.vector.tensor_tensor(
                            v_out[:, u, 2 * h:2 * h + 2, :, 0:HEAD_DIM],
                            v_bank[:, h].rearrange("p (t h d) -> p t h d", t=2, d=HEAD_DIM),
                            bv_all[:].rearrange("p (h d) -> p h d", d=HEAD_DIM).unsqueeze(1)
                            .broadcast_to([P, 2, HEADS, HEAD_DIM]), ALU.add).then_inc(v_taken, 1)
                    for m in range(2):
                        dve.wait_ge(qk_done, 4 * g + m + 9)
                        nc.vector.tensor_scalar(k_out[:, u, m], qk_bank[:, m], SCALE, kbias[:, m:m + 1],
                                                ALU.mult, ALU.add).then_inc(k_taken, 1)

        @block.scalar
        def _(act):
            act.sem_inc(xt_act, 1)
            act.sem_inc(q_taken, 2)
            with act.Fori(0, GROUPS // 2) as i:
                for u in range(2):
                    g = 2 * i + u
                    act.wait_ge(sqrt_in, g + 1)
                    nc.scalar.activation(rstd[:], rstd[:], ACT.Sqrt).then_inc(sqrt_out, 1)
                    act.wait_ge(turned, g + 2)
                    act.wait_ge(qk_done, 4 * g + 4)
                    nc.scalar.copy(x_t[:, u, 0], turn[:, 0]).then_inc(xt_act, 1)
                    act.wait_ge(stored[u], STORES * QUADS * (i + 1))
                    for m in range(2):
                        act.wait_ge(qk_done, 4 * g + m + 11)
                        for n in range(DECAYS):
                            ins = nc.scalar.activation(q_out[:, u, m, n], qk_bank[:, 2 + m], ACT.Identity,
                                                       bias=qbias[:, m, n:n + 1], scale=qscale[:, m, n:n + 1])
                        ins.then_inc(q_taken, 1)

        @block.tensor
        def _(pe):
            pe.sem_inc(turned, 1)
            pe.sem_inc(qk_done, 8)
            with pe.Fori(0, GROUPS // 2) as i:
                for u in range(2):
                    g = 2 * i + u
                    pe.wait_ge(hat_done, g + 3)
                    pe.wait_ge(xt_dve, g + 1)
                    pe.wait_ge(xt_act, g + 1)
                    for c in range(EC):
                        for t in range(TILES):
                            last = nc.tensor.transpose(turn[:, c, t * P:(t + 1) * P],
                                                       x_hat[:, u, t, c * P:(c + 1) * P], ident[:])
                    last.then_inc(turned, 1)
                    pe.wait_ge(xt_dve, g + 2)
                    pe.wait_ge(xt_act, g + 2)
                    pe.wait_ge(v_taken, 2 * g + 2)
                    for t in range(TILES):
                        for c in range(EC):
                            last = nc.tensor.matmul(v_bank[:, t // 2, (t % 2) * EMBED:(t % 2 + 1) * EMBED],
                                                    x_t[:, u, c, t * P:(t + 1) * P], wqkvt[:, 2, c],
                                                    start=(c == 0), stop=(c == EC - 1), skip_group_check=True)
                        if t % 2:
                            last.then_inc(v_done, 1)
                    for k, (w, m) in enumerate(((1, 0), (1, 1), (0, 0), (0, 1))):
                        if k == 0:
                            pe.wait_ge(k_taken, 2 * g + 2)
                        if k == 2:
                            pe.wait_ge(q_taken, 2 * g + 2)
                        for c in range(EC):
                            last = nc.tensor.matmul(qk_bank[:, k], wqkvt[:, w, c, m * P:(m + 1) * P], x_t[:, u, c],
                                                    start=(c == 0), stop=(c == EC - 1))
                        last.then_inc(qk_done, 1)


SLOTS = BLOCKS * 2
UNIT_SLOTS = BLOCKS // 2
UNITS = 4
LEAD = UNIT_SLOTS + 4
RING = 3
ITEMS = 4
RED_SLOT, TURN_SLOT = 4, 5
RING_STEP = ITEMS * SLOTS + UNITS
AHEAD_ITEMS = ITEMS * LEAD + 1
EXPS = 2 * SLOTS


def ring_item(slot, k):
    turns = sum(1 for s in range(min(slot, 0), max(slot, 0)) if s % UNIT_SLOTS == TURN_SLOT and s >= 1 - UNIT_SLOTS)
    return ITEMS * slot + k + (turns if slot > 0 else -turns)


def score_parts(block, side):
    at = block * P
    parts = []
    for level, hs in enumerate(LEVELS):
        mate = (at // hs) ^ 1
        for col in range(mate * hs, (mate + 1) * hs, min(hs, 512)):
            parts.append((level, col, min(hs, 512)))
    parts.append((RAW, at, P))
    return [p for p in parts if side is None or p[1] // HALF == side]


def attention_block(nc, keep, scr):
    ident = keep["ident"]
    with ExitStack() as ctx:
        def sb(name, shape, dt=F32):
            return ctx.enter_context(nc.sbuf_tensor(name, shape, dt))

        def sem(name):
            return ctx.enter_context(nc.semaphore(name))

        q_stack = [sb(f"q_stack{h}", [STACK + MAXROWS, 2, RAW + 1, HALF], F16) for h in range(2)]
        k_stack = [sb(f"k_stack{h}", [STACK + MAXROWS, RAW + 1, SEQ], F16) for h in range(2)]
        hi = sb("hi", [P, RAW + 1, SEQ], F16)
        lo = sb("lo", [P, RAW + 1, SEQ], F16)
        qk = sb("qk", [P, SEQ])
        table = sb("table_in", [P, 2 * HALF])
        decayed = sb("decayed", [P, 2, HALF])
        probs = sb("probs", [P, 4, HALF])
        diag = [sb(f"diag{h}", [P, BLOCKS, P]) for h in range(2)]
        mask = [sb(f"mask{h}", [P, P]) for h in range(2)]
        v_ones = [sb(f"v_ones{h}", [P, BLOCKS, ROWS]) for h in range(2)]
        part_max = sb("part_max", [P, 2, UNIT_SLOTS, 5])
        row_max = sb("row_max", [P, 2, MAXROWS * RAW * UNIT_SLOTS])
        max_rows = sb("max_rows", [MAXROWS * RAW * UNIT_SLOTS, P], F16)
        scrap = sb("scrap", [UNIT_SLOTS, 1])
        heads_out = sb("heads_out", [P, 2, 512])
        tile = [ctx.enter_context(nc.psum_tensor(f"tile{t}", [P, 2, 512], F32)) for t in range(2)]
        ring = ctx.enter_context(nc.psum_tensor("ring", [P, RING, 512], F32))
        acc = ctx.enter_context(nc.psum_tensor("acc", [P, 512], F32))

        tile_full = sem("tile_full")
        exp_done = sem("exp_done")
        probs_used = sem("probs_used")
        ring_full = sem("ring_full")
        ring_free = sem("ring_free")
        acc_full, acc_free = sem("acc_full"), sem("acc_free")
        out_stored = [sem(f"out_stored{h}") for h in range(2)]
        blocks_seen = sem("blocks_seen")
        max_ready, max_seen = sem("max_ready"), sem("max_seen")
        rows_ready, rows_in = sem("rows_ready"), sem("rows_in")
        diag_ready = sem("diag_ready")
        stack_free = [sem(f"stack_free{h}") for h in range(2)]
        raw_in = [sem(f"raw_in{h}") for h in range(2)]
        k_in = [[sem(f"k_in{h}_{x}") for x in range(2)] for h in range(2)]
        q_in = [[sem(f"q_in{h}_{x}") for x in range(2)] for h in range(2)]
        mask_in = [sem(f"mask_in{h}") for h in range(2)]
        v_in = [sem(f"v_in{h}") for h in range(2)]
        qk_in = sem("qk_in")
        decayed_ready, hi_ready, lo_ready = sem("decayed_ready"), sem("hi_ready"), sem("lo_ready")
        const_ready = sem("const_ready")
        LO_ROWS = RAW * UNIT_SLOTS
        CHUNKS = 2 * (RAW + 1)
        PART_DMAS = 3

        block = ctx.enter_context(nc.Block())

        def half_view(t, level, side):
            if level == RAW:
                return t[:, side * HALF:(side + 1) * HALF].unsqueeze(1)
            hs = LEVELS[level]
            return t.rearrange("p (r s x) -> p r s x", s=2, x=hs)[:, :, side, :]

        def factors(level, side):
            hs = LEVELS[level]
            part = table[:, 2 * HALF - hs:2 * HALF] if side == 0 else table[:, 0:hs]
            return lead(part, HALF // hs)

        def chunk(c):
            return (RAW if c < 2 else (c - 2) // 2), c % 2

        def compact(c, level):
            hs = HALF if level == RAW else LEVELS[level]
            return decayed[:, c % 2].rearrange("p (r x) -> p r x", x=hs)

        mul_slot = (1, 1, 2, 3, 5, 6, 8, 10, 11, 12)
        hi_slot = (0, 1, 4, 5, 7, 8, 10, 12, 13, 14)

        @block.sync
        def _(sp):
            def load_qk(pair):
                sp.dma_start(qk[:], scr["qk"].rearrange("b m (h s) k n d t -> (b m h) (s k n d) t", s=2)[pair]
                             ).then_inc(qk_in, QUADS)
                sp.dma_start(table[:], scr["table"][pair % PAIRS]).then_inc(qk_in, QUADS)

            def load_part(h, k, done, level, count, first, columns):
                row = (2 * h + k) * ROWS
                for j, part in enumerate((hi, lo, hi) if k else (hi, hi, lo)):
                    src = part[row:row + ROWS, level:level + count, first:first + columns]
                    if k:
                        dst = k_stack[h][j * ROWS:(j + 1) * ROWS, level:level + count, first:first + columns]
                    elif columns == HALF:
                        dst = q_stack[h][j * ROWS:(j + 1) * ROWS, first // HALF, level:level + count]
                    else:
                        dst = q_stack[h][j * ROWS:(j + 1) * ROWS, :, level]
                    sp.dma_start(dst, src).then_inc(done, QUADS)

            def load_raw(h, builds):
                sp.wait_ge(lo_ready, CHUNKS * (builds - 1) + 2)
                for k in range(2):
                    load_part(h, k, raw_in[h], RAW, 1, 0, SEQ)

            def load_q(h, half):
                load_part(h, 0, q_in[h][half], 0, RAW, half * HALF, HALF)

            def load_k(h):
                for x in range(2):
                    load_part(h, 1, k_in[h][x], 2 * x, 2, 0, SEQ)

            def load_v(h, pair):
                sp.dma_start(v_ones[h][:], scr["v"].rearrange("b (h s) p k c -> (b h) s p k c", s=2)[pair, h]
                             ).then_inc(v_in[h], QUADS)

            def load_mask(h, pair):
                sp.dma_start(mask[h][:], scr["mask"].rearrange("(h s) p x -> h s p x", s=2)[pair % PAIRS, h]
                             ).then_inc(mask_in[h], QUADS)

            def store_max_rows(h, half, count):
                sp.wait_ge(rows_ready, count)
                sp.dma_start(q_stack[h][STACK:STACK + MAXROWS, half, 0:RAW],
                             max_rows[:]).then_inc(rows_in, QUADS)

            def store_out(i, u):
                sp.wait_ge(acc_free, UNITS * i + u + 2)
                h, half = u // 2, u % 2
                row = (i // PAIRS) * HEADS + i * 2 + (half * HEADS + h)
                sp.dma_start(scr["out"].rearrange("b f h r t -> (b f h) r t")[row], heads_out[:, u % 2]
                             ).then_inc(out_stored[u % 2], QUADS)

            load_qk(0)
            for h in range(2):
                load_mask(h, 0)
            load_v(0, 0)
            load_raw(0, 1)
            load_raw(1, 1)
            sp.wait_ge(lo_ready, CHUNKS)
            load_k(0)
            load_q(0, 0)
            load_q(0, 1)
            load_q(1, 0)
            load_qk(1)
            store_max_rows(0, 0, 1)
            with sp.Fori(0, STEPS) as i:
                sp.wait_ge(stack_free[1], i + 1)
                load_k(1)
                load_q(1, 1)
                sp.wait_ge(acc_free, UNITS * i + 1)
                load_v(1, i)
                store_max_rows(0, 1, UNITS * i + 2)
                sp.wait_ge(blocks_seen, SLOTS * i + BLOCKS + 1)
                load_mask(0, (i + 1) % STEPS)
                load_raw(0, i + 2)
                store_out(i, 0)
                store_max_rows(1, 0, UNITS * i + 3)
                sp.wait_ge(lo_ready, CHUNKS * (i + 2))
                load_q(0, 0)
                sp.wait_ge(stack_free[0], i + 1)
                load_k(0)
                load_q(0, 1)
                store_out(i, 1)
                load_v(0, (i + 1) % STEPS)
                load_qk((i + 2) % STEPS)
                store_max_rows(1, 1, UNITS * i + 4)
                sp.wait_ge(blocks_seen, SLOTS * i + 2 * BLOCKS + 1)
                load_mask(1, (i + 1) % STEPS)
                load_raw(1, i + 2)
                store_out(i, 2)
                load_q(1, 0)
                store_max_rows(0, 0, UNITS * i + 5)
                store_out(i, 3)
            for h in range(2):
                sp.wait_ge(out_stored[h], (2 * STEPS + 1) * QUADS)
                sp.wait_ge(mask_in[h], QUADS * (STEPS + 1))
                sp.wait_ge(raw_in[h], 2 * PART_DMAS * QUADS * (STEPS + 1))
                sp.wait_ge(q_in[h][0], PART_DMAS * QUADS * (STEPS + 1))
                for done in (q_in[h][1], k_in[h][0], k_in[h][1]):
                    sp.wait_ge(done, PART_DMAS * QUADS * (STEPS + 1 - h))
            sp.wait_ge(v_in[0], QUADS * (STEPS + 1))
            sp.wait_ge(v_in[1], QUADS * STEPS)
            sp.wait_ge(qk_in, 2 * QUADS * (STEPS + 2))
            sp.wait_ge(rows_in, QUADS * (UNITS * STEPS + 1))

        @block.gpsimd
        def _(pool):
            def level_free(level, builds):
                for h in range(2):
                    for done in (q_in[h][0], q_in[h][1], k_in[h][level // 2]):
                        pool.wait_ge(done, PART_DMAS * QUADS * builds)

            def multiply(c, builds):
                level, side = chunk(c)
                if not isinstance(builds, int) and side == 0 and level != 3:
                    level_free(level, builds)
                if c == 2:
                    pool.wait_ge(qk_in, 2 * QUADS * (builds + 1))
                if c >= 4 or not isinstance(builds, int):
                    pool.wait_ge(lo_ready, CHUNKS * builds + max(c - 1, 2))
                nc.gpsimd.tensor_tensor(compact(c, level), half_view(qk[:], level, side), factors(level, side),
                                        ALU.mult).then_inc(decayed_ready, 1)

            def rest(c, builds):
                level, side = chunk(c)
                pool.wait_ge(hi_ready, CHUNKS * builds + c + 1)
                src = half_view(qk[:], level, side) if level == RAW else compact(c, level)
                nc.gpsimd.tensor_tensor(half_view(lo[:, level], level, side), src, half_view(hi[:, level], level, side),
                                        ALU.subtract).then_inc(lo_ready, 1)

            def build_chunk(c, builds):
                if c < 2:
                    rest(c, builds)
                else:
                    multiply(c, builds)
                    if c > 2:
                        rest(c - 1, builds)
                    if c == CHUNKS - 1:
                        rest(c, builds)

            def diag_minus_max(h, half, count):
                pool.wait_ge(max_ready, count)
                part = diag[h][:, half * UNIT_SLOTS:(half + 1) * UNIT_SLOTS]
                nc.gpsimd.tensor_tensor(part, part, row_max[:, half, 0:UNIT_SLOTS].unsqueeze(2).broadcast_to([P, UNIT_SLOTS, P]),
                                        ALU.subtract).then_inc(diag_ready, 1)

            pool.sem_inc(diag_ready, 1)
            for c in range(CHUNKS):
                build_chunk(c, 0)
            diag_minus_max(0, 0, 1)
            with pool.Fori(0, STEPS) as i:
                for s in range(SLOTS):
                    for c in range(CHUNKS):
                        if mul_slot[c] == s:
                            build_chunk(c, i + 1)
                    if s % UNIT_SLOTS == RED_SLOT:
                        u = s // UNIT_SLOTS + 1
                        diag_minus_max((u // 2) % 2, u % 2, UNITS * i + u + 1)

        @block.scalar
        def _(act):
            def cast(c, builds):
                level, side = chunk(c)
                if level < RAW:
                    act.wait_ge(decayed_ready, (CHUNKS - 2) * builds + c - 1)
                elif side == 0:
                    act.wait_ge(qk_in, 2 * QUADS * (builds + 1))
                    if not isinstance(builds, int):
                        for h in range(2):
                            act.wait_ge(raw_in[h], 2 * PART_DMAS * QUADS * builds)
                src = half_view(qk[:], level, side) if level == RAW else compact(c, level)
                nc.scalar.copy(half_view(hi[:, level], level, side), src).then_inc(hi_ready, 1)

            act.sem_inc(acc_free, 1)
            for h in range(2):
                act.sem_inc(out_stored[h], QUADS)
            for c in range(CHUNKS):
                cast(c, 0)
            act.sem_inc(exp_done, 2)
            with act.Fori(0, STEPS) as i:
                def take_unit(u):
                    act.wait_ge(acc_full, UNITS * i + u + 1)
                    act.wait_ge(out_stored[u % 2], QUADS * (2 * i + u // 2 + 1))
                    nc.scalar.copy(heads_out[:, u % 2], acc[:]).then_inc(acc_free, 1)

                for s in range(SLOTS):
                    act.wait_ge(probs_used, s + 1)
                    for t in (2 * s, 2 * s + 1):
                        act.wait_ge(tile_full, t + 1)
                        nc.scalar.activation(probs[:, t % 4], tile[t % 2][:].rearrange("p a b -> p (a b)"), ACT.Exp,
                                             scale=1.0 / (SCALE * SCALE * HEAD_DIM ** 0.5)).then_inc(exp_done, 1)
                    if s % UNIT_SLOTS == 0 and s > 0:
                        take_unit(s // UNIT_SLOTS - 1)
                    for c in range(CHUNKS):
                        if hi_slot[c] == s:
                            cast(c, i + 1)
                take_unit(UNITS - 1)
                act.drain()
                act.sem_inc(probs_used, -SLOTS)
                act.sem_inc(tile_full, -EXPS)

        @block.vector
        def _(dve):
            def ring_bank(n):
                return ring[:, n % RING]

            def max_block(slot, b, i):
                h, q = b // BLOCKS % 2, b % BLOCKS
                out = part_max[:, b // UNIT_SLOTS % 2, b % UNIT_SLOTS]
                for k in range(ITEMS):
                    n = ring_item(slot, k)
                    if q == 0 and k == 0:
                        dve.wait_ge(mask_in[h], QUADS * (i + 1 + b // SLOTS))
                    dve.wait_ge(ring_full, n + AHEAD_ITEMS + 1)
                    if k < ITEMS - 1:
                        nc.vector.tensor_reduce(out[:, k:k + 1], ring_bank(n), AX.X, ALU.max).then_inc(ring_free, 1)
                        continue
                    nc.vector.tensor_reduce(out[:, 3:4], ring_bank(n)[:, 0:3 * P], AX.X,
                                            ALU.max).then_inc(blocks_seen, 1)
                    nc.vector.tensor_tensor_reduce(out=diag[h][:, q], in0=ring_bank(n)[:, 3 * P:4 * P], in1=mask[h][:],
                                                   scale=1.0, scalar=-3.0e38, op0=ALU.mult, op1=ALU.max,
                                                   accum_out=out[:, 4:5]).then_inc(ring_free, 1)

            def finish_max(par, seen, count):
                dve.wait_ge(blocks_seen, seen)
                if count is not None:
                    dve.wait_ge(diag_ready, count)
                parts = part_max[:, par].unsqueeze(1).broadcast_to([P, MAXROWS * RAW, UNIT_SLOTS, ITEMS + 1])
                nc.vector.tensor_reduce(row_max[:, par].rearrange("p (r b) -> p r b", b=UNIT_SLOTS), parts, AX.X,
                                        ALU.max).then_inc(max_ready, 1)

            def split_max(slot, unit_count):
                n = ring_item(slot, ITEMS)
                dve.wait_ge(ring_full, n + AHEAD_ITEMS + 1)
                if unit_count is not None:
                    dve.wait_ge(rows_in, QUADS * unit_count)
                src = ring_bank(n)[0:MAXROWS * LO_ROWS, 0:P]
                nc.vector.tensor_scalar(max_rows[:], src, -1.0 / MAXUNIT, None, ALU.mult).then_inc(max_seen, 1)
                dve.wait_ge(max_seen, (unit_count if unit_count is not None else 0) + 1)
                nc.vector.scalar_tensor_tensor(out=max_rows[LO_ROWS:], in0=src[LO_ROWS:], scalar=-1.0 / MAXUNIT,
                                               in1=max_rows[LO_ROWS:], op0=ALU.mult,
                                               op1=ALU.subtract).then_inc(rows_ready, 1)
                nc.vector.tensor_copy(scrap[:], src[0:UNIT_SLOTS, 0:1]).then_inc(ring_free, 1)

            for h in range(2):
                nc.vector.memset(k_stack[h][STACK:STACK + MAXROWS], MAXUNIT).then_inc(const_ready, 1)
            for s in range(-LEAD, 0):
                max_block(s, s + LEAD, 0)
                if s % UNIT_SLOTS == RED_SLOT and s + LEAD >= UNIT_SLOTS:
                    finish_max(0, s + LEAD + 1, None)
                if s % UNIT_SLOTS == TURN_SLOT and s + LEAD >= UNIT_SLOTS:
                    split_max(s, None)
            with dve.Fori(0, STEPS) as i:
                for s in range(SLOTS):
                    max_block(s, s + LEAD, i)
                    u = s // UNIT_SLOTS + 1
                    if s % UNIT_SLOTS == RED_SLOT:
                        finish_max(u % 2, SLOTS * i + s + LEAD + 1, UNITS * i + u)
                    if s % UNIT_SLOTS == TURN_SLOT:
                        split_max(s, UNITS * i + u)
                dve.drain()
                dve.sem_inc(ring_full, -RING_STEP)

        @block.tensor
        def _(pe):
            def max_scores(slot, b, ks, i):
                h, q = b // BLOCKS % 2, b % BLOCKS
                q0 = q * P % HALF
                parts = score_parts(q, None)
                banks = [[parts[0]], [parts[1]], [parts[2]], parts[3:]]
                for k in ks:
                    n = ring_item(slot, k)
                    if n + AHEAD_ITEMS - RING + 1 > 0:
                        pe.wait_ge(ring_free, n + AHEAD_ITEMS - RING + 1)
                    need = {(0, 0): (k_in[h][0], q_in[h][0]), (0, 3): (k_in[h][1],),
                            (UNIT_SLOTS, 0): (q_in[h][1],)}.get((q, k), ())
                    for done in need:
                        pe.wait_ge(done, PART_DMAS * QUADS * (i + 1 + b // SLOTS))
                    if (q, k) == (0, 3):
                        pe.wait_ge(raw_in[h], 2 * PART_DMAS * QUADS * (i + 1 + b // SLOTS))
                    col = 0
                    for j, (level, first, width) in enumerate(banks[k]):
                        last = nc.tensor.matmul(ring[:, n % RING, col:col + width],
                                                q_stack[h][0:STACK, q // UNIT_SLOTS, level, q0:q0 + P],
                                                k_stack[h][0:STACK, level, first:first + width],
                                                start=(j == 0), stop=True, skip_group_check=True)
                        col += width
                    last.then_inc(ring_full, 1)

            def turn_max(slot, par, count):
                n = ring_item(slot, ITEMS)
                pe.wait_ge(ring_free, n + AHEAD_ITEMS - RING + 1)
                pe.wait_ge(max_ready, count)
                nc.tensor.transpose(ring[0:MAXROWS * LO_ROWS, n % RING, 0:P], row_max[:, par], ident[:]).then_inc(ring_full, 1)

            def scores(t):
                u, kb = t // BLOCKS, t % BLOCKS
                h, half = u // 2, u % 2
                pe.wait_ge(exp_done, t + 1)
                started = set()
                for level, first, width in score_parts(kb, half):
                    col = first - half * HALF
                    bank, at = col // 512, col % 512
                    out = tile[t % 2][:, bank, at:at + width]
                    if level == RAW:
                        last = nc.tensor.matmul(out, diag[h][:, kb], ident[:], is_transpose=True,
                                                start=bank not in started, stop=True, skip_group_check=True)
                    else:
                        last = nc.tensor.matmul(out, k_stack[h][:, level, kb * P:(kb + 1) * P],
                                                q_stack[h][:, half, level, col:col + width],
                                                start=bank not in started, stop=True, skip_group_check=True)
                    started.add(bank)
                last.then_inc(tile_full, 1)

            def products(j):
                u = j // UNIT_SLOTS
                h = u // 2
                for par in range(2):
                    t = 2 * j + par
                    pe.wait_ge(exp_done, t + 3)
                    for qt in range(2):
                        row = (2 * par + qt) * ROWS
                        last = nc.tensor.matmul(acc[row:row + ROWS], v_ones[h][:, t % BLOCKS],
                                                probs[:, t % 4, qt * 512:(qt + 1) * 512],
                                                start=(j % UNIT_SLOTS == 0), stop=(j % UNIT_SLOTS == UNIT_SLOTS - 1),
                                                skip_group_check=True)
                        if j % (2 * UNIT_SLOTS) == 2 * UNIT_SLOTS - 1 and (par, qt) == (0, 0):
                            last.then_inc(stack_free[h], 1)
                        if j % UNIT_SLOTS == UNIT_SLOTS - 1 and (par, qt) == (0, 1):
                            last.then_inc(probs_used, 1)
                last.then_inc(acc_full if j % UNIT_SLOTS == UNIT_SLOTS - 1 else probs_used, 1)

            pe.wait_ge(const_ready, 2)
            pe.sem_inc(probs_used, 2)
            pe.sem_inc(stack_free[1], 1)
            for s in range(-LEAD, 0):
                max_scores(s, s + LEAD, range(ITEMS), 0)
                if s % UNIT_SLOTS == TURN_SLOT and s + LEAD >= UNIT_SLOTS:
                    turn_max(s, 0, 1)
            with pe.Fori(0, STEPS) as i:
                for s in range(SLOTS):
                    if s % UNIT_SLOTS == 0:
                        u = s // UNIT_SLOTS
                        pe.wait_ge(rows_in, QUADS * (UNITS * i + u + 1))
                        pe.wait_ge(diag_ready, UNITS * i + u + 2)
                    scores(2 * s)
                    max_scores(s, s + LEAD, (0, 1), i)
                    scores(2 * s + 1)
                    if s == SLOTS - 1:
                        products(s - 1)
                    max_scores(s, s + LEAD, (2, 3), i)
                    if s % UNIT_SLOTS == TURN_SLOT:
                        turn_max(s, (s // UNIT_SLOTS + 1) % 2, UNITS * i + s // UNIT_SLOTS + 2)
                    j = s if s == SLOTS - 1 else s - 1
                    if j >= 0:
                        if j % UNIT_SLOTS == 0:
                            pe.wait_ge(acc_free, UNITS * i + j // UNIT_SLOTS + 1)
                        if j % (2 * UNIT_SLOTS) == 0:
                            pe.wait_ge(v_in[j // (2 * UNIT_SLOTS)], QUADS * (i + 1))
                        products(j)
                pe.drain()
                pe.sem_inc(exp_done, -EXPS)
                pe.sem_inc(ring_free, -RING_STEP)


def ffn_block(nc, a, keep, scr, out):
    ident, w1t, w2t, wot = keep["ident"], keep["w1t"], keep["w2t"], keep["wot"]
    with ExitStack() as ctx:
        def sb(name, shape, dt=F32):
            return ctx.enter_context(nc.sbuf_tensor(name, shape, dt))

        def sem(name):
            return ctx.enter_context(nc.semaphore(name))

        sums_in = sb("sums_in", [P, 2, EC, 2, 2, GROUP])
        x_in = sb("x_res", [P, 2, TILES, EMBED])
        sums = sb("sums", [P, EC, 2, GROUP])
        heads = sb("heads", [P, EC, GROUP])
        x_bias = sb("x_bias", [P, TILES, EMBED])
        y = sb("y", [P, TILES, EMBED])
        y_bias = sb("y_bias", [P, 2, TILES, EMBED])
        z = sb("z", [P, TILES, EMBED])
        z_hi = sb("z_hi", [P, EC, GROUP], F16)
        z_lo = sb("z_lo", [P, EC, GROUP], F16)
        hidden = sb("hidden", [P, FC, GROUP])
        h_hi = sb("h_hi", [P, FC, GROUP], F16)
        h_lo = sb("h_lo", [P, FC, GROUP], F16)
        result = sb("result", [P, 2, TILES, EMBED])
        stats = sb("stats2", [P, TILES, 6])
        mv = sb("mv2", [P, TILES, 2])
        rstd = sb("rstd2", [P, TILES])
        spare = sb("spare2", [P, 1])
        up = ctx.enter_context(nc.psum_tensor("up", [P, 2, GROUP], F32))
        attn = ctx.enter_context(nc.psum_tensor("attn", [P, TILES, EMBED], F32))
        turn = ctx.enter_context(nc.psum_tensor("turn2", [P, EC, GROUP], F32))
        down = ctx.enter_context(nc.psum_tensor("down", [P, TILES, EMBED], F32))

        loaded = [sem(f"loaded{u}") for u in range(2)]
        stored = [sem(f"out_done{u}") for u in range(2)]
        heads_ready, x_bias_ready, attn_done, y_ready, y_bias_ready = (
            sem("heads_ready"), sem("x_bias_ready"), sem("attn_done"), sem("y_ready"), sem("y_bias_ready"))
        sqrt_in, sqrt_out, z_ready, turned = sem("sqrt_in2"), sem("sqrt_out2"), sem("z_ready"), sem("turned2")
        z_hi_ready, z_lo_ready = sem("z_hi_ready"), sem("z_lo_ready")
        up_done, up_taken, h_hi_ready, h_lo_ready = sem("up_done"), sem("up_taken"), sem("h_hi_ready"), sem("h_lo_ready")
        down_done, result_ready, dve_step = sem("down_done"), sem("result_ready"), sem("dve_step2")
        LOADS = 4 * EC + 1
        DVE_STEPS = 5
        LOOPED = GROUPS - 2
        block = ctx.enter_context(nc.Block())
        x_groups = a["x"].rearrange("b s e -> (b s) e").rearrange("(g t p) e -> g p t e", t=TILES, p=P)
        out_groups = out.rearrange("b s e -> (b s) e").rearrange("(g t p) e -> g p t e", t=TILES, p=P)
        out_scr = scr["out"].rearrange("b f (c h) (r q k d) t -> (b f) q c r k h d t", c=EC, r=2, q=2, k=2)

        def each_group(eng, body):
            with eng.Fori(0, LOOPED // 2) as i:
                for u in range(2):
                    body(2 * i + u, u, True)
            body(GROUPS - 2, 0, True)
            body(GROUPS - 1, 1, False)

        @block.sync
        def _(sp):
            def load(pair, u):
                for c in range(EC):
                    for r in range(2):
                        for k in range(2):
                            sp.dma_start(sums_in[:, u, c, r, k], out_scr[pair, u, c, r, k]).then_inc(loaded[u], QUADS)
                sp.dma_start(x_in[:, u], x_groups[pair * 2 + u]).then_inc(loaded[u], QUADS)

            def body(pair, u, load_next=True):
                g = pair * 2 + u
                if load_next:
                    sp.wait_ge(heads_ready, g + 1)
                    sp.wait_ge(x_bias_ready, g + 1)
                    load(pair + 1, u)
                sp.wait_ge(result_ready, g + 2)
                sp.dma_start(out_groups[g], result[:, u]).then_inc(stored[u], QUADS)

            for u in range(2):
                sp.sem_inc(stored[u], QUADS)
            load(0, 0)
            load(0, 1)
            with sp.Fori(0, LOOPED // 2) as i:
                for u in range(2):
                    body(i, u)
            for u in range(2):
                body(LOOPED // 2, u, load_next=False)
            for u in range(2):
                sp.wait_ge(stored[u], (GROUPS // 2 + 1) * QUADS)

        @block.gpsimd
        def _(pool):
            def add_out_bias(g, u):
                pool.wait_ge(loaded[u], LOADS * QUADS * (g // 2 + 1))
                nc.gpsimd.tensor_tensor(x_bias[:], x_in[:, u], lead(keep["bo_all"][:], TILES), ALU.add
                                        ).then_inc(x_bias_ready, 1)

            def add_ffn_bias(g, u, seen):
                pool.wait_ge(y_ready, g + 1)
                pool.wait_ge(result_ready, seen)
                nc.gpsimd.tensor_tensor(y_bias[:, u], y[:], lead(keep["b2_all"][:], TILES), ALU.add
                                        ).then_inc(y_bias_ready, 1)

            def body(g, u, more):
                if more:
                    add_out_bias(g + 1, 1 - u)
                for f in range(FC):
                    pool.wait_ge(h_hi_ready, FC * g + f + 1)
                    nc.gpsimd.tensor_tensor(h_lo[:, f], hidden[:, f], h_hi[:, f], ALU.subtract).then_inc(h_lo_ready, 1)
                if more:
                    add_ffn_bias(g + 1, 1 - u, g + 1)

            add_out_bias(0, 0)
            add_ffn_bias(0, 0, 1)
            each_group(pool, body)

        @block.scalar
        def _(act):
            def root(g):
                act.wait_ge(sqrt_in, g + 1)
                nc.scalar.activation(rstd[:], rstd[:], ACT.Sqrt).then_inc(sqrt_out, 1)

            def split_z(g):
                act.wait_ge(turned, g + 1)
                nc.scalar.copy(z_hi[:], turn[:]).then_inc(z_hi_ready, 1)

            def body(g, u, more):
                for f in range(FC):
                    act.wait_ge(up_done, FC * g + f + 1)
                    nc.scalar.activation(hidden[:, f], up[:, f % 2], ACT.Relu, bias=keep["b1_col"][:, f:f + 1]
                                         ).then_inc(up_taken, 1)
                if more:
                    root(g + 1)
                    split_z(g + 1)

            act.sem_inc(up_taken, 1)
            root(0)
            split_z(0)
            each_group(act, body)

        @block.vector
        def _(dve):
            def divide(g, u):
                dve.wait_ge(loaded[u], LOADS * QUADS * (g // 2 + 1))
                nc.vector.tensor_tensor(sums[:], sums_in[:, u, :, 0], sums_in[:, u, :, 1], ALU.add).then_inc(dve_step, 1)
                dve.wait_ge(dve_step, DVE_STEPS * g + 1)
                nc.vector.reciprocal(sums[:, :, 1], sums[:, :, 1]).then_inc(dve_step, 1)
                dve.wait_ge(dve_step, DVE_STEPS * g + 2)
                nc.vector.tensor_tensor(heads[:], sums[:, :, 0], sums[:, :, 1], ALU.mult).then_inc(heads_ready, 1)

            def residual(g):
                dve.wait_ge(attn_done, g + 1)
                dve.wait_ge(x_bias_ready, g + 1)
                if not (isinstance(g, int) and g == 0):
                    dve.wait_ge(y_bias_ready, g)
                nc.vector.tensor_tensor(y[:], attn[:], x_bias[:], ALU.add).then_inc(y_ready, 1)
                dve.wait_ge(y_ready, g + 1)
                taken = [2]

                def step(ins):
                    taken[0] += 1
                    ins.then_inc(dve_step, 1)
                    dve.wait_ge(dve_step, DVE_STEPS * g + taken[0])

                normalize(nc, dve, y, z, stats, mv, rstd, spare, step, sqrt_in, sqrt_out, g + 1,
                          lambda ins: ins.then_inc(z_ready, 1))

            def rest_z(g):
                dve.wait_ge(z_hi_ready, g + 1)
                nc.vector.tensor_tensor(z_lo[:], turn[:], z_hi[:], ALU.subtract).then_inc(z_lo_ready, 1)

            def body(g, u, more):
                if more:
                    divide(g + 1, 1 - u)
                for f in range(FC):
                    dve.wait_ge(up_taken, FC * g + f + 2)
                    nc.vector.tensor_copy(h_hi[:, f], hidden[:, f]).then_inc(h_hi_ready, 1)
                if more:
                    residual(g + 1)
                dve.wait_ge(down_done, g + 1)
                dve.wait_ge(y_bias_ready, g + 1)
                dve.wait_ge(stored[u], QUADS * (g // 2 + 1))
                nc.vector.tensor_tensor(result[:, u], down[:], y_bias[:, u], ALU.add).then_inc(result_ready, 1)
                if more:
                    rest_z(g + 1)

            dve.sem_inc(result_ready, 1)
            divide(0, 0)
            residual(0)
            rest_z(0)
            each_group(dve, body)

        @block.tensor
        def _(pe):
            def attn_product(g):
                pe.wait_ge(heads_ready, g + 1)
                if not (isinstance(g, int) and g == 0):
                    pe.wait_ge(y_ready, g)
                for t in range(TILES):
                    for c in range(EC):
                        last = nc.tensor.matmul(attn[:, t], heads[:, c, t * P:(t + 1) * P], wot[:, c],
                                                start=(c == 0), stop=(c == EC - 1), skip_group_check=True)
                last.then_inc(attn_done, 1)

            def turn_z(g):
                pe.wait_ge(z_ready, g + 1)
                if not (isinstance(g, int) and g == 0):
                    pe.wait_ge(z_lo_ready, g)
                for c in range(EC):
                    for t in range(TILES):
                        last = nc.tensor.transpose(turn[:, c, t * P:(t + 1) * P], z[:, t, c * P:(c + 1) * P], ident[:])
                last.then_inc(turned, 1)

            def body(g, u, more):
                pe.wait_ge(z_lo_ready, g + 1)
                for f in range(FC):
                    pe.wait_ge(up_taken, FC * g + max(f, 1))
                    k = 0
                    for c in range(EC):
                        for part in (z_hi, z_lo):
                            last = nc.tensor.matmul(up[:, f % 2], w1t[:, c, f * P:(f + 1) * P], part[:, c],
                                                    start=(k == 0), stop=(k == 2 * EC - 1))
                            k += 1
                    last.then_inc(up_done, 1)
                if more:
                    attn_product(g + 1)
                pe.wait_ge(result_ready, g + 1)
                for f in range(FC):
                    pe.wait_ge(h_lo_ready, FC * g + f + 1)
                    for part in (h_hi, h_lo):
                        for t in range(TILES):
                            last = nc.tensor.matmul(down[:, t], part[:, f, t * P:(t + 1) * P], w2t[:, f],
                                                    start=(f == 0 and part is h_hi and t % 2 == 0),
                                                    stop=(f == FC - 1 and part is h_lo), skip_group_check=True)
                last.then_inc(down_done, 1)
                if more:
                    turn_z(g + 1)

            attn_product(0)
            turn_z(0)
            each_group(pe, body)


INPUTS = {"x": "L0_attn_x", "Wq": "L0_attn_Wq", "bq": "L0_attn_bq", "Wk": "L0_attn_Wk", "bk": "L0_attn_bk",
          "Wv": "L0_attn_Wv", "bv": "L0_attn_bv", "Wo": "L0_attn_Wo", "bo": "L0_attn_bo",
          "decay": "L0_attn_decay_params", "mix": "L0_attn_mix_weights",
          "W1": "L0_ffn_W1", "b1": "L0_ffn_b1", "W2": "L0_ffn_W2", "b2": "L0_ffn_b2"}


def build(nc, a, out):
    scr = {
        "qk": nc.dram_tensor("qk_scratch", [BATCH, 2, 8, 2, DECAYS, HEAD_DIM, SEQ], F32).ap(),
        "v": nc.dram_tensor("v_scratch", [BATCH, HEADS, P, BLOCKS, ROWS], F32).ap(),
        "table": nc.dram_tensor("table_scratch", [PAIRS, P, 2 * HALF], F32).ap(),
        "hat": nc.dram_tensor("hat_scratch", [HEADS, 2 * P], F32).ap(),
        "mask": nc.dram_tensor("mask_scratch", [HEADS, P, P], F32).ap(),
        "out": nc.dram_tensor("out_scratch", [BATCH, 2, HEADS, P, GROUP], F32).ap(),
    }
    with ExitStack() as ctx:
        def sb(name, shape, dt=F32):
            return ctx.enter_context(nc.sbuf_tensor(name, shape, dt))

        keep = {"ident": sb("ident", [P, P]), "w1t": sb("w1t", [P, EC, FF], F16), "w2t": sb("w2t", [P, FC, EMBED], F16),
                "wot": sb("wot", [P, EC, EMBED]), "bo_all": sb("bo_all", [P, EMBED]), "b2_all": sb("b2_all", [P, EMBED]),
                "b1_col": sb("b1_col", [P, FC])}
        with ExitStack() as first:
            def sb1(name, shape, dt=F32):
                return first.enter_context(nc.sbuf_tensor(name, shape, dt))

            early = {"wqkvt": sb1("wqkvt", [P, 3, EC, EMBED]), "qscale": sb1("qscale", [P, 2, DECAYS]),
                     "qbias": sb1("qbias", [P, 2, DECAYS]), "kbias": sb1("kbias", [P, 2]),
                     "bv_all": sb1("bv_all", [P, EMBED])}
            setup_block(nc, a, keep, early, scr)
            token_block(nc, a, keep, early, scr)
        attention_block(nc, keep, scr)
        ffn_block(nc, a, keep, scr, out)


def kernel(**inputs):
    import numpy as np
    import concourse.bacc as bacc
    from concourse.bass_utils import run_bass_kernel_spmd

    nc = bacc.Bacc("TRN2", target_bir_lowering=False, num_devices=1)
    arrays, a = {}, {}
    for short, name in INPUTS.items():
        array = np.ascontiguousarray(inputs[name])
        arrays[f"in_{short}"] = array
        a[short] = nc.dram_tensor(f"in_{short}", array.shape, mybir.dt.from_np(array.dtype), kind="ExternalInput").ap()
    out = nc.dram_tensor("out", (BATCH, SEQ, EMBED), F32, kind="ExternalOutput").ap()
    build(nc, a, out)
    result = run_bass_kernel_spmd(nc, [arrays], core_ids=[0])
    return result.results[0]["out"]
```

```python
from contextlib import ExitStack

import concourse.bass as bass
from concourse import mybir

F32 = mybir.dt.float32
F16 = mybir.dt.float16
ALU = mybir.AluOpType
ACT = mybir.ActivationFunctionType
AX = mybir.AxisListType

P = 128
BATCH, SEQ, EMBED = 2, 2048, 256
HEADS, HEAD_DIM, DECAYS = 16, 16, 2
FF = 4 * EMBED
EC = EMBED // P
FC = FF // P
BLOCKS = SEQ // P
PAIRS = HEADS // 2
STEPS = BATCH * PAIRS
GROUP = 512
TILES = GROUP // P
GROUPS = BATCH * SEQ // GROUP
HALF = SEQ // 2
LEVELS = (1024, 512, 256, 128)
RAW = len(LEVELS)
ROWS = DECAYS * HEAD_DIM
STACK = 3 * ROWS
MAXROWS = 2
SCALE = 32.0
W_SCALE = 64.0
MAXUNIT = 1024.0
LN_EPS = 1e-5
Q_EPS = 1e-5
QUADS = 16


def lead(ap, n):
    p, x = ap.shape
    return ap.unsqueeze(1).broadcast_to([p, n, x])


def normalize(nc, dve, x, out, stats, mv, rstd, spare, step, sqrt_in, sqrt_out, sqrt_count, last,
              meanwhile=None):
    for t in range(TILES):
        ins = nc.vector.bn_stats(stats[:, t], x[:, t])
    step(ins)
    nc.vector.memset(spare[:], 0.0)
    for t in range(TILES):
        ins = nc.vector.bn_aggr(mv[:, t], stats[:, t])
    step(ins)
    nc.vector.tensor_scalar(rstd[:], mv[:, :, 1], LN_EPS, None, ALU.add).then_inc(sqrt_in, 1)
    if meanwhile:
        meanwhile()
    dve.wait_ge(sqrt_out, sqrt_count)
    step(nc.vector.reciprocal(rstd[:], rstd[:]))
    for t in range(TILES):
        ins = nc.vector.tensor_scalar(out[:, t], x[:, t], mv[:, t, 0:1], rstd[:, t:t + 1], ALU.subtract, ALU.mult)
    last(ins)


def for_groups(eng, body):
    with eng.Fori(0, GROUPS // 2 - 1) as i:
        for u in range(2):
            body(2 * i + u, u, 2)
    body(GROUPS - 2, 0, 1)
    body(GROUPS - 1, 1, 0)


class PairBuilder:

    CHUNKS = 2 * (RAW + 1)

    def __init__(self, nc, scr, sb, sem):
        self.nc, self.scr = nc, scr
        self.hi = sb("hi", [P, RAW + 1, SEQ], F16)
        self.lo = sb("lo", [P, RAW + 1, SEQ], F16)
        self.qk = sb("qk", [P, SEQ])
        self.table = sb("table_in", [P, 2 * HALF])
        self.decayed = sb("decayed", [P, 2, HALF])
        self.qk_in = sem("qk_in")
        self.decayed_ready, self.hi_ready, self.lo_ready = sem("decayed_ready"), sem("hi_ready"), sem("lo_ready")

    LOADS = 5

    def load(self, sp, pair):
        half = P // 2
        sp.dma_start(self.qk[0:half], self.scr["q"].rearrange("b m (h s) n d t -> (b m h) (s n d) t", s=2)[pair]
                     ).then_inc(self.qk_in, QUADS)
        k_rows = self.scr["k"].rearrange("b m (h s) d t -> (b m h) s d t", s=2)[pair]
        for s in range(2):
            first = half + s * ROWS
            sp.dma_start(self.qk[first:first + ROWS],
                         k_rows[s].unsqueeze(0).broadcast_to([DECAYS, HEAD_DIM, SEQ])).then_inc(self.qk_in, QUADS)
        factors = self.scr["table"].rearrange("(h s) n x -> h (s n) x", s=2)[pair % PAIRS]
        for k in range(2):
            sp.dma_start(self.table[k * half:(k + 1) * half],
                         factors.unsqueeze(1).broadcast_to([2 * DECAYS, HEAD_DIM, 2 * HALF])).then_inc(self.qk_in, QUADS)

    def loaded(self, builds):
        return self.LOADS * QUADS * (builds + 1)

    def at(self, c):
        return (RAW if c < 2 else (c - 2) // 2), c % 2

    def half_view(self, t, level, side):
        if level == RAW:
            return t[:, side * HALF:(side + 1) * HALF].unsqueeze(1)
        hs = LEVELS[level]
        return t.rearrange("p (r s x) -> p r s x", s=2, x=hs)[:, :, side, :]

    def factors(self, level, side):
        hs = LEVELS[level]
        part = self.table[:, 2 * HALF - hs:2 * HALF] if side == 0 else self.table[:, 0:hs]
        return lead(part, HALF // hs)

    def source(self, c):
        level, side = self.at(c)
        if level == RAW:
            return self.half_view(self.qk[:], level, side)
        return self.decayed[:, c % 2].rearrange("p (r x) -> p r x", x=LEVELS[level])

    def multiply(self, c):
        level, side = self.at(c)
        self.nc.gpsimd.tensor_tensor(self.source(c), self.half_view(self.qk[:], level, side),
                                     self.factors(level, side), ALU.mult).then_inc(self.decayed_ready, 1)

    def cast(self, act, c, builds):
        level, side = self.at(c)
        if level < RAW:
            act.wait_ge(self.decayed_ready, (self.CHUNKS - 2) * builds + c - 1)
        self.nc.scalar.copy(self.half_view(self.hi[:, level], level, side), self.source(c)).then_inc(self.hi_ready, 1)

    def rest(self, eng, ops, c, builds):
        level, side = self.at(c)
        eng.wait_ge(self.hi_ready, self.CHUNKS * builds + c + 1)
        ops.tensor_tensor(self.half_view(self.lo[:, level], level, side), self.source(c),
                                     self.half_view(self.hi[:, level], level, side), ALU.subtract).then_inc(self.lo_ready, 1)


def token_block(nc, a, keep, builder, scr):
    ident, wot = keep["ident"], keep["wot"]
    with ExitStack() as ctx:
        def sb(name, shape, dt=F32):
            return ctx.enter_context(nc.sbuf_tensor(name, shape, dt))

        def sem(name):
            return ctx.enter_context(nc.semaphore(name))

        wn = sb("wn", [P, 4, EC, EMBED])
        w_hi = sb("w_hi", [P, 3, EC, EMBED], F16)
        w_lo = sb("w_lo", [P, 3, EC, EMBED], F16)
        bv_all = sb("bv_all", [P, EMBED])
        qscale = sb("qscale", [P, 2, DECAYS])
        qbias = sb("qbias", [P, 2, DECAYS])
        kbias = sb("kbias", [P, 2])
        q_bias_in = sb("q_bias_in", [P, 2])
        k_bias_in = sb("k_bias_in", [P, 2])
        mix_w = sb("mix_w", [P, 2, DECAYS])
        mix_m = sb("mix_m", [P, 2, 1])
        mix_h = sb("mix_h", [HEADS, DECAYS])
        mix_hm = sb("mix_hm", [HEADS, 1])
        decay_h = sb("decay_h", [HEADS, DECAYS])
        power = sb("power", [HEADS, DECAYS, 2 * HALF])
        hat_part = sb("hat_part", [HEADS, 2 * P])
        hat = sb("hat", [HEADS, 2 * P])
        w_rows = sb("w_rows", [P, 2, FC * EMBED])
        above = sb("above", [P, FC * EMBED], F16)
        below = sb("below", [P, FC * EMBED], F16)
        ones = sb("ones", [P, P])
        abs_sum = sb("abs_sum", [P, 2])
        cut = sb("cut", [P, 2])
        neg_cut = sb("neg_cut", [P, 2])
        x = sb("x_tokens", [P, 2, TILES, EMBED])
        xt_hi = sb("xt_hi", [P, 2, EC, GROUP], F16)
        xt_lo = sb("xt_lo", [P, 2, EC, GROUP], F16)
        q_out = sb("q_out", [P, 2, 2, DECAYS, GROUP])
        k_out = sb("k_out", [P, 2, 2, GROUP])
        v_out = sb("v_out", [P, 2, HEADS, TILES, ROWS])
        stats = sb("stats", [P, TILES, 6])
        mv = sb("mv", [P, TILES, 2])
        rstd = sb("rstd", [P, TILES])
        spare = sb("spare", [P, 1])
        turn = ctx.enter_context(nc.psum_tensor("turn", [P, EC, GROUP], F32))
        v_bank = ctx.enter_context(nc.psum_tensor("v_bank", [P, 2, 512], F32))
        qk_bank = ctx.enter_context(nc.psum_tensor("qk_bank", [P, 4, GROUP], F32))

        w_in, small_in, later_in = sem("w_in"), sem("small_in"), sem("later_in")
        ident_done, ones_done = sem("ident_done"), sem("ones_done")
        w_turned, w_taken, w_lo_ready = sem("w_turned"), sem("w_taken"), sem("w_lo_ready")
        mix_diff, mix_exp, mix_ready, decay_ready = sem("mix_diff"), sem("mix_exp"), sem("mix_ready"), sem("decay_ready")
        pool_step, dve_first = sem("pool_step"), sem("dve_first")
        power_ready, hat_ready, tables_out = sem("power_ready"), sem("hat_ready"), sem("tables_out")
        x_loaded = [sem(f"x_loaded{u}") for u in range(2)]
        stored = [sem(f"stored{u}") for u in range(2)]
        hat_done, sqrt_in, sqrt_out = sem("hat_done"), sem("sqrt_in"), sem("sqrt_out")
        turned, xt_dve, xt_act = sem("turned"), sem("xt_dve"), sem("xt_act")
        v_done, v_taken, qk_done, q_taken, k_taken = (sem("v_done"), sem("v_taken"), sem("qk_done"),
                                                      sem("q_taken"), sem("k_taken"))
        dve_step = sem("dve_step")
        ffn_w_in, sums_ready = sem("ffn_w_in"), sem("sums_ready")
        total_ready, cuts_ready = sem("total_ready"), sem("cuts_ready")
        compared = sem("compared")
        DVE_STEPS = 3
        STORES = 1 + 2 + 2 * DECAYS
        HALF_GROUPS = GROUPS // BATCH
        block = ctx.enter_context(nc.Block())
        x_groups = a["x"].rearrange("b s e -> (b s) e").rearrange("(g t p) e -> g p t e", t=TILES, p=P)

        @block.sync
        def _(sp):
            def load_x(g, u):
                sp.dma_start(x[:, u], x_groups[g]).then_inc(x_loaded[u], QUADS)

            def store(b, at, kb, g, u, x_after=True, first_pair=False):
                sp.wait_ge(v_taken, 2 * g + 4)
                sp.dma_start(scr["v"][b].rearrange("h p k c -> p h k c")[:, :, bass.ds(kb, TILES)],
                             v_out[:, u]).then_inc(stored[u], QUADS)
                if x_after:
                    sp.wait_ge(turned, g + 3)
                    load_x(g + 3, 1 - u)
                if first_pair:
                    builder.load(sp, 0)
                sp.wait_ge(q_taken, 2 * g + 4)
                sp.wait_ge(k_taken, 2 * g + 4)
                for m in range(2):
                    sp.dma_start(scr["k"][b, m, :, :, bass.ds(at, GROUP)], k_out[:, u, m, :]).then_inc(stored[u], QUADS)
                for m in range(2):
                    for n in range(DECAYS):
                        sp.dma_start(scr["q"][b, m, :, n, :, bass.ds(at, GROUP)],
                                     q_out[:, u, m, n, :]).then_inc(stored[u], QUADS)

            load_x(0, 0)
            for m, (name, chunks) in enumerate((("W1", FC), ("W2", EC))):
                sp.dma_start(w_rows[:, m].rearrange("p (c e) -> p c e", c=chunks),
                             a[name].rearrange("(c p) e -> p c e", p=P)).then_inc(ffn_w_in, QUADS)
            for m, name in ((2, "Wv"), (1, "Wk"), (0, "Wq"), (3, "Wo")):
                sp.dma_start(wn[:, m], a[name].rearrange("(c p) e -> p c e", p=P)).then_inc(w_in, QUADS)
            load_x(1, 1)
            for u in range(2):
                sp.sem_inc(stored[u], STORES * QUADS)
            sp.wait_ge(turned, 2)
            load_x(2, 0)
            with sp.Fori(0, HALF_GROUPS // 2) as i:
                for u in range(2):
                    g = 2 * i + u
                    store(0, i * (2 * GROUP) + u * GROUP, i * (2 * TILES) + u * TILES, g, u)
            sp.wait_ge(tables_out, 2 * QUADS)
            for u in range(2):
                sp.wait_ge(stored[u], (HALF_GROUPS // 2 + 1) * STORES * QUADS)
            for g in range(HALF_GROUPS, GROUPS):
                u = g % 2
                at = (g - HALF_GROUPS) * GROUP
                store(1, at, at // P, g, u, x_after=g + 3 < GROUPS, first_pair=g == HALF_GROUPS)
            for u in range(2):
                sp.wait_ge(stored[u], (GROUPS // 2 + 1) * STORES * QUADS)

        @block.gpsimd
        def _(pool):
            steps = [0]

            def then(ins):
                steps[0] += 1
                ins.then_inc(pool_step, 1)
                pool.wait_ge(pool_step, steps[0])

            then(nc.gpsimd.memset(ident[:], 0.0))
            nc.gpsimd.affine_select(out=ident[:], in_=ident[:], compare_op=ALU.not_equal, fill=1.0, base=0,
                                    pattern=[[-1, P]], channel_multiplier=1).then_inc(ident_done, 1)
            nc.gpsimd.memset(v_out[:, 0, :, :, HEAD_DIM:ROWS], W_SCALE).then_inc(ones_done, 1)
            nc.gpsimd.memset(v_out[:, 1, :, :, HEAD_DIM:ROWS], W_SCALE).then_inc(ones_done, 1)
            pool.wait_ge(ident_done, 1)
            nc.gpsimd.tensor_copy(keep["ident16"][:], ident[:])
            pool.wait_ge(decay_ready, 1)
            nc.gpsimd.memset(power[:, :, 0:1], 1.0)
            nc.gpsimd.tensor_copy(power[:, :, 1], decay_h[:])
            then(nc.gpsimd.tensor_copy(power[:, :, 2 * HALF - 1], decay_h[:]))
            n = 1
            while n < HALF:
                top = min(n, HALF - 1 - n)
                if top > 0:
                    ins = nc.gpsimd.tensor_tensor(power[:, :, n + 1:n + 1 + top], power[:, :, 1:1 + top],
                                                  power[:, :, n:n + 1].broadcast_to([HEADS, DECAYS, top]), ALU.mult)
                    if 2 * n >= HALF:
                        ins.then_inc(power_ready, 1)
                down = power[:, :, 2 * HALF - n:2 * HALF]
                ins = nc.gpsimd.tensor_tensor(power[:, :, 2 * HALF - 2 * n:2 * HALF - n], down,
                                              down[:, :, 0:1].broadcast_to([HEADS, DECAYS, n]), ALU.mult)
                n *= 2
                if n < HALF:
                    then(ins)
                else:
                    ins.then_inc(power_ready, 1)
            pool.wait_ge(power_ready, 2)
            pool.dma_start(scr["table"], power[:]).then_inc(tables_out, QUADS)
            pool.wait_ge(mix_ready, 1)
            sides = ((0, P - 1, 2 * HALF - P + 1), (P - 1, P, 0))
            nc.gpsimd.memset(hat[:, 2 * P - 1:2 * P], 0.0)
            for at, n, first in sides:
                nc.gpsimd.tensor_tensor(hat_part[:, at:at + n], power[:, 0, first:first + n],
                                        mix_h[:, 0:1].broadcast_to([HEADS, n]), ALU.mult)
                ins = nc.gpsimd.tensor_tensor(hat[:, at:at + n], power[:, 1, first:first + n],
                                              mix_h[:, 1:2].broadcast_to([HEADS, n]), ALU.mult)
            then(ins)
            nc.gpsimd.tensor_tensor(hat[:, 0:2 * P - 1], hat[:, 0:2 * P - 1], hat_part[:, 0:2 * P - 1],
                                    ALU.add).then_inc(hat_ready, 1)
            pool.wait_ge(hat_ready, 1)
            pool.dma_start(scr["hat"], lead(hat[:], P)).then_inc(tables_out, QUADS)
            pool.wait_ge(cuts_ready, 2)
            for m in range(2):
                if m == 1:
                    pool.wait_ge(compared, 2)
                nc.gpsimd.tensor_scalar(above[:], w_rows[:, m], cut[:, m:m + 1], None, ALU.is_gt)
                nc.gpsimd.tensor_scalar(below[:], w_rows[:, m], neg_cut[:, m:m + 1], None, ALU.is_lt
                                        ).then_inc(compared, 1)
                pool.wait_ge(compared, 2 * m + 1)
                nc.gpsimd.tensor_tensor(keep["ternary"][:, m], above[:], below[:], ALU.subtract).then_inc(compared, 1)
            pool.wait_ge(builder.qk_in, builder.loaded(0))
            for c in range(2, builder.CHUNKS):
                if c >= 4:
                    pool.wait_ge(builder.lo_ready, c - 1)
                builder.multiply(c)

        @block.vector
        def _(dve):
            steps = [0]

            def first(ins):
                steps[0] += 1
                ins.then_inc(dve_first, 1)
                dve.wait_ge(dve_first, steps[0])

            def sum_weights():
                dve.wait_ge(ffn_w_in, 2 * QUADS)
                for m in range(2):
                    nc.vector.tensor_reduce(abs_sum[:, m:m + 1], w_rows[:, m], AX.X, ALU.add,
                                            apply_absolute_value=True).then_inc(sums_ready, 1)

            def x_hat_of(g, u, meanwhile=None):
                taken = [0]

                def step(ins):
                    taken[0] += 1
                    ins.then_inc(dve_step, 1)
                    dve.wait_ge(dve_step, DVE_STEPS * g + taken[0])

                dve.wait_ge(x_loaded[u], QUADS * (g // 2 + 1))
                normalize(nc, dve, x[:, u], x[:, u], stats, mv, rstd, spare, step, sqrt_in, sqrt_out, g + 1,
                          lambda ins: ins.then_inc(hat_done, 1), meanwhile)

            def x_t_of(g, u):
                dve.wait_ge(xt_act, g + 2)
                dve.wait_ge(qk_done, 4 * g + 4)
                nc.vector.tensor_tensor(xt_lo[:, u], turn[:], xt_hi[:, u], ALU.subtract).then_inc(xt_dve, 1)

            dve.sem_inc(xt_dve, 1)
            dve.sem_inc(v_taken, 2)
            dve.sem_inc(k_taken, 2)
            nc.vector.memset(ones[:], 1.0)
            x_hat_of(0, 0, sum_weights)
            dve.wait_ge(small_in, 7 * QUADS)
            nc.vector.tensor_reduce(mix_m[:], mix_w[:], AX.X, ALU.max)
            first(nc.vector.tensor_reduce(mix_hm[:], mix_h[:], AX.X, ALU.max))
            nc.vector.tensor_tensor(mix_w[:], mix_w[:], mix_m[:].broadcast_to([P, 2, DECAYS]),
                                    ALU.subtract).then_inc(mix_diff, 1)
            nc.vector.tensor_scalar(mix_h[:], mix_h[:], mix_hm[:, 0:1], None, ALU.subtract).then_inc(mix_diff, 1)
            nc.vector.tensor_scalar(decay_h[:], decay_h[:], 0.01, 0.9999, ALU.max, ALU.min).then_inc(decay_ready, 1)
            dve.wait_ge(mix_exp, 2)
            nc.vector.tensor_reduce(mix_m[:], mix_w[:], AX.X, ALU.add)
            first(nc.vector.tensor_reduce(mix_hm[:], mix_h[:], AX.X, ALU.add))
            nc.vector.reciprocal(mix_m[:], mix_m[:])
            first(nc.vector.reciprocal(mix_hm[:], mix_hm[:]))
            nc.vector.tensor_scalar(mix_h[:], mix_h[:], mix_hm[:, 0:1], None, ALU.mult).then_inc(mix_ready, 1)
            first(nc.vector.tensor_tensor(mix_w[:], mix_w[:], mix_m[:].broadcast_to([P, 2, DECAYS]), ALU.mult))
            nc.vector.tensor_scalar(kbias[:], k_bias_in[:], SCALE, None, ALU.mult)
            nc.vector.tensor_scalar(bv_all[:], bv_all[:], W_SCALE, None, ALU.mult)
            first(nc.vector.tensor_scalar(qscale[:], mix_w[:], SCALE, None, ALU.mult))
            first(nc.vector.tensor_tensor(qbias[:], qscale[:], q_bias_in[:].unsqueeze(2).broadcast_to([P, 2, DECAYS]),
                                          ALU.mult))
            first(nc.vector.tensor_scalar(qscale[:], qscale[:], 1.0 / W_SCALE, None, ALU.mult))
            x_t_of(0, 0)
            for k, m in enumerate((2, 1, 0)):
                dve.wait_ge(w_taken, k + 1)
                nc.vector.scalar_tensor_tensor(out=w_lo[:, m].rearrange("p c f -> p (c f)"), in0=qk_bank[:, m],
                                               scalar=W_SCALE, in1=w_hi[:, m].rearrange("p c f -> p (c f)"),
                                               op0=ALU.mult, op1=ALU.subtract).then_inc(w_lo_ready, 1)
            dve.wait_ge(total_ready, 1)
            nc.vector.tensor_scalar(cut[:], v_bank[:, 0, 0:2], 1.0 / (FF * EMBED), Q_EPS, ALU.mult, ALU.add
                                    ).then_inc(cuts_ready, 1)
            dve.wait_ge(cuts_ready, 1)
            nc.vector.tensor_scalar(neg_cut[:], cut[:], -0.5, None, ALU.mult)
            nc.vector.tensor_scalar(cut[:], cut[:], 0.5, None, ALU.mult).then_inc(cuts_ready, 1)
            x_hat_of(1, 1)
            dve.wait_ge(ones_done, 2)

            def body(g, u, more, rests=()):
                dve.wait_ge(stored[u], STORES * QUADS * (g // 2 + 1))
                for h in range(2):
                    dve.wait_ge(v_done, 2 * g + h + 1)
                    nc.vector.tensor_tensor(
                        v_out[:, u, :, 2 * h:2 * h + 2, 0:HEAD_DIM].rearrange("p h t d -> p t h d"),
                        v_bank[:, h].rearrange("p (t h d) -> p t h d", t=2, d=HEAD_DIM),
                        bv_all[:].rearrange("p (h d) -> p h d", d=HEAD_DIM).unsqueeze(1)
                        .broadcast_to([P, 2, HEADS, HEAD_DIM]), ALU.add).then_inc(v_taken, 1)
                if more >= 1:
                    x_t_of(g + 1, 1 - u)
                if more >= 2:
                    x_hat_of(g + 2, u)
                for m in range(2):
                    dve.wait_ge(qk_done, 4 * g + m + 9)
                    nc.vector.tensor_scalar(k_out[:, u, m], qk_bank[:, m], SCALE / W_SCALE, kbias[:, m:m + 1],
                                            ALU.mult, ALU.add).then_inc(k_taken, 1)
                for c in rests:
                    builder.rest(dve, nc.vector, c, 0)

            with dve.Fori(0, HALF_GROUPS // 2) as i:
                for u in range(2):
                    body(2 * i + u, u, 2)
            body(HALF_GROUPS, 0, 2)
            body(HALF_GROUPS + 1, 1, 2, rests=(0, 1, 2, 3))
            body(HALF_GROUPS + 2, 0, 1, rests=(4, 5))
            body(HALF_GROUPS + 3, 1, 0, rests=(6, 7, 8, 9))

        @block.scalar
        def _(act):
            act.dma_start(decay_h[:], a["decay"]).then_inc(small_in, QUADS)
            act.dma_start(mix_h[:], a["mix"]).then_inc(small_in, QUADS)
            for m in range(2):
                src = bass.AP(a["mix"].tensor, m * 8 * DECAYS, [[DECAYS, 8], [0, HEAD_DIM], [1, DECAYS]])
                act.dma_start(mix_w[:, m, :], src).then_inc(small_in, QUADS)
            for name, tile in (("bq", q_bias_in), ("bk", k_bias_in)):
                act.dma_start(tile[:], a[name].rearrange("(c p) -> p c", p=P),
                              allow_slow_non_contiguous=True).then_inc(small_in, QUADS)
            act.dma_start(bv_all[:], bass.AP(a["bv"].tensor, 0, [[0, P], [1, EMBED]])).then_inc(small_in, QUADS)
            for name, tile in (("bo", keep["bo_all"]), ("b2", keep["b2_all"])):
                act.dma_start(tile[:], bass.AP(a[name].tensor, 0, [[0, P], [1, EMBED]])).then_inc(later_in, QUADS)
            act.dma_start(keep["b1_col"][:], a["b1"].rearrange("(c p) -> p c", p=P),
                          allow_slow_non_contiguous=True).then_inc(later_in, QUADS)
            def root(g):
                act.wait_ge(sqrt_in, g + 1)
                nc.scalar.activation(rstd[:], rstd[:], ACT.Sqrt).then_inc(sqrt_out, 1)

            def x_t_of(g, u):
                act.wait_ge(turned, g + 2)
                act.wait_ge(qk_done, 4 * g + 4)
                nc.scalar.copy(xt_hi[:, u], turn[:]).then_inc(xt_act, 1)

            act.sem_inc(xt_act, 1)
            act.sem_inc(q_taken, 2)
            root(0)
            act.wait_ge(mix_diff, 2)
            nc.scalar.activation(mix_w[:], mix_w[:], ACT.Exp).then_inc(mix_exp, 1)
            nc.scalar.activation(mix_h[:], mix_h[:], ACT.Exp).then_inc(mix_exp, 1)
            x_t_of(0, 0)
            for k, m in enumerate((2, 1, 0, 3)):
                act.wait_ge(w_turned, k + 1)
                if m == 3:
                    nc.scalar.copy(wot[:].rearrange("p c f -> p (c f)"), qk_bank[:, m]).then_inc(w_taken, 1)
                else:
                    nc.scalar.activation(w_hi[:, m].rearrange("p c f -> p (c f)"), qk_bank[:, m], ACT.Copy,
                                         scale=W_SCALE).then_inc(w_taken, 1)
            root(1)

            def body(g, u, more, casts=()):
                if more >= 1:
                    x_t_of(g + 1, 1 - u)
                if more >= 2:
                    root(g + 2)
                for c in casts:
                    if c == 0:
                        act.wait_ge(builder.qk_in, builder.loaded(0))
                    builder.cast(act, c, 0)
                act.wait_ge(stored[u], STORES * QUADS * (g // 2 + 1))
                for m in range(2):
                    act.wait_ge(qk_done, 4 * g + m + 11)
                    for n in range(DECAYS):
                        ins = nc.scalar.activation(q_out[:, u, m, n], qk_bank[:, 2 + m], ACT.Identity,
                                                   bias=qbias[:, m, n:n + 1], scale=qscale[:, m, n:n + 1])
                    ins.then_inc(q_taken, 1)
            with act.Fori(0, HALF_GROUPS // 2) as i:
                for u in range(2):
                    body(2 * i + u, u, 2)
            body(HALF_GROUPS, 0, 2)
            body(HALF_GROUPS + 1, 1, 2, casts=(0, 1, 2, 3))
            body(HALF_GROUPS + 2, 0, 1, casts=(4, 5))
            body(HALF_GROUPS + 3, 1, 0, casts=(6, 7))
            for c in (8, 9):
                builder.cast(act, c, 0)
            act.wait_ge(later_in, 3 * QUADS)

        @block.tensor
        def _(pe):
            def turn_x(g, u):
                pe.wait_ge(hat_done, g + 1)
                pe.wait_ge(xt_dve, g + 1)
                pe.wait_ge(xt_act, g + 1)
                for c in range(EC):
                    for t in range(TILES):
                        last = nc.tensor.transpose(turn[:, c, t * P:(t + 1) * P], x[:, u, t, c * P:(c + 1) * P], ident[:])
                last.then_inc(turned, 1)

            def turn_w(m):
                for ec in range(EC):
                    for fc in range(EC):
                        last = nc.tensor.transpose(qk_bank[:, m, (ec * EC + fc) * P:(ec * EC + fc + 1) * P],
                                                   wn[:, m, fc, ec * P:(ec + 1) * P], ident[:])
                last.then_inc(w_turned, 1)

            pe.sem_inc(turned, 1)
            pe.sem_inc(qk_done, 8)
            pe.wait_ge(ident_done, 1)
            turn_x(0, 0)
            pe.wait_ge(w_in, 4 * QUADS)
            for m in (2, 1, 0, 3):
                turn_w(m)
            pe.wait_ge(sums_ready, 2)
            nc.tensor.matmul(v_bank[:, 0, 0:2], ones[:], abs_sum[:], start=True, stop=True).then_inc(total_ready, 1)
            pe.wait_ge(w_taken, 4)
            pe.wait_ge(w_lo_ready, 3)
            pe.wait_ge(cuts_ready, 1)

            def body(g, u, more):
                pe.wait_ge(xt_dve, g + 2)
                pe.wait_ge(xt_act, g + 2)
                pe.wait_ge(v_taken, 2 * g + 2)
                parts = [(c, x_part, w_part) for c in range(EC)
                         for x_part, w_part in ((xt_hi, w_hi), (xt_lo, w_hi), (xt_hi, w_lo))]
                for t in range(TILES):
                    for j, (c, x_part, w_part) in enumerate(parts):
                        last = nc.tensor.matmul(v_bank[:, t // 2, (t % 2) * EMBED:(t % 2 + 1) * EMBED],
                                                x_part[:, u, c, t * P:(t + 1) * P], w_part[:, 2, c],
                                                start=(j == 0), stop=(j == len(parts) - 1), skip_group_check=True)
                    if t % 2:
                        last.then_inc(v_done, 1)
                if more >= 1:
                    turn_x(g + 1, 1 - u)
                for k, (w, m) in enumerate(((1, 0), (1, 1), (0, 0), (0, 1))):
                    if k == 0:
                        pe.wait_ge(k_taken, 2 * g + 2)
                    if k == 2:
                        pe.wait_ge(q_taken, 2 * g + 2)
                    for j, (c, x_part, w_part) in enumerate(parts):
                        last = nc.tensor.matmul(qk_bank[:, k], w_part[:, w, c, m * P:(m + 1) * P], x_part[:, u, c],
                                                start=(j == 0), stop=(j == len(parts) - 1))
                    last.then_inc(qk_done, 1)

            for_groups(pe, body)


SLOTS = BLOCKS * 2
UNIT_SLOTS = BLOCKS // 2
UNITS = 4
LEAD = UNIT_SLOTS + 4
RING = 3
ITEMS = 4
RED_SLOT, TURN_SLOT = 4, 5
RING_STEP = ITEMS * SLOTS + UNITS
AHEAD_ITEMS = ITEMS * LEAD + 1
EXPS = 2 * SLOTS


def ring_item(slot, k):
    turns = sum(1 for s in range(min(slot, 0), max(slot, 0)) if s % UNIT_SLOTS == TURN_SLOT and s >= 1 - UNIT_SLOTS)
    return ITEMS * slot + k + (turns if slot > 0 else -turns)


def score_parts(block, side):
    at = block * P
    parts = []
    for level, hs in enumerate(LEVELS):
        mate = (at // hs) ^ 1
        for col in range(mate * hs, (mate + 1) * hs, min(hs, 512)):
            parts.append((level, col, min(hs, 512)))
    parts.append((RAW, at, P))
    return [p for p in parts if side is None or p[1] // HALF == side]


def attention_block(nc, keep, builder, scr):
    ident = keep["ident"]
    with ExitStack() as ctx:
        def sb(name, shape, dt=F32):
            return ctx.enter_context(nc.sbuf_tensor(name, shape, dt))

        def sem(name):
            return ctx.enter_context(nc.semaphore(name))

        q_stack = [sb(f"q_stack{h}", [STACK + MAXROWS, 2, RAW + 1, HALF], F16) for h in range(2)]
        k_stack = [sb(f"k_stack{h}", [STACK + MAXROWS, RAW + 1, SEQ], F16) for h in range(2)]
        probs = sb("probs", [P, 4, HALF])
        diag = [sb(f"diag{h}", [P, BLOCKS, P]) for h in range(2)]
        mask = [sb(f"mask{h}", [P, P]) for h in range(2)]
        v_ones = [sb(f"v_ones{h}", [P, BLOCKS, ROWS]) for h in range(2)]
        part_max = sb("part_max", [P, 2, UNIT_SLOTS, 5])
        row_max = sb("row_max", [P, 2, UNIT_SLOTS])
        max_repeated = sb("max_repeated", [P, MAXROWS * RAW, UNIT_SLOTS])
        max_rows = sb("max_rows", [MAXROWS * RAW * UNIT_SLOTS, P], F16)
        scrap = sb("scrap", [UNIT_SLOTS, 1])
        unit = sb("unit", [P, 1])
        warm = sb("warm", [P, 1])
        heads_out = sb("heads_out", [P, 2, 512])
        tile = [ctx.enter_context(nc.psum_tensor(f"tile{t}", [P, 2, 512], F32)) for t in range(2)]
        ring = ctx.enter_context(nc.psum_tensor("ring", [P, RING, 512], F32))
        acc = ctx.enter_context(nc.psum_tensor("acc", [P, 512], F32))

        tile_full = sem("tile_full")
        exp_done = sem("exp_done")
        probs_used = sem("probs_used")
        ring_full = sem("ring_full")
        ring_free = sem("ring_free")
        acc_full, acc_free = sem("acc_full"), sem("acc_free")
        out_stored = [sem(f"out_stored{h}") for h in range(2)]
        blocks_seen = sem("blocks_seen")
        max_ready, max_seen = sem("max_ready"), sem("max_seen")
        repeated_ready = sem("repeated_ready")
        rows_ready, rows_in = sem("rows_ready"), sem("rows_in")
        diag_ready = sem("diag_ready")
        stack_free = [sem(f"stack_free{h}") for h in range(2)]
        raw_in = [sem(f"raw_in{h}") for h in range(2)]
        k_in = [[sem(f"k_in{h}_{x}") for x in range(2)] for h in range(2)]
        q_in = [[sem(f"q_in{h}_{x}") for x in range(2)] for h in range(2)]
        mask_in = [sem(f"mask_in{h}") for h in range(2)]
        v_in = [sem(f"v_in{h}") for h in range(2)]
        qk_in, lo_ready = builder.qk_in, builder.lo_ready
        unit_ready, const_ready = sem("unit_ready"), sem("const_ready")
        LO_ROWS = RAW * UNIT_SLOTS
        CHUNKS = builder.CHUNKS
        PART_DMAS = 3

        block = ctx.enter_context(nc.Block())

        masks = bass.AP(scr["hat"].tensor, P - 1, [[4 * P * P, PAIRS], [2 * P * P, 2], [2 * P - 1, P], [1, P]])

        order = [("rest", 0), ("rest", 1), ("product", 2)]
        for c in range(3, CHUNKS):
            order += [("product", c), ("rest", c - 1)]
        order.append(("rest", CHUNKS - 1))
        pool_steps = (order[:5], order[5:14], order[14:], [])
        hi_slot = (0, 1, 4, 5, 7, 8, 10, 12, 14, 15)

        @block.sync
        def _(sp):
            def load_part(h, k, done, level, count, first, columns):
                row = (2 * k + h) * ROWS
                hi, lo = builder.hi, builder.lo
                for j, part in enumerate((hi, lo, hi) if k else (hi, hi, lo)):
                    src = part[row:row + ROWS, level:level + count, first:first + columns]
                    if k:
                        dst = k_stack[h][j * ROWS:(j + 1) * ROWS, level:level + count, first:first + columns]
                    elif columns == HALF:
                        dst = q_stack[h][j * ROWS:(j + 1) * ROWS, first // HALF, level:level + count]
                    else:
                        dst = q_stack[h][j * ROWS:(j + 1) * ROWS, :, level]
                    sp.dma_start(dst, src).then_inc(done, QUADS)

            def load_raw(h, builds):
                sp.wait_ge(lo_ready, CHUNKS * (builds - 1) + 2)
                for k in range(2):
                    load_part(h, k, raw_in[h], RAW, 1, 0, SEQ)

            def load_q(h, half):
                load_part(h, 0, q_in[h][half], 0, RAW, half * HALF, HALF)

            def load_k(h, levels=(0, 1)):
                for x in levels:
                    load_part(h, 1, k_in[h][x], 2 * x, 2, 0, SEQ)

            def load_v(h, pair):
                sp.dma_start(v_ones[h][:], scr["v"].rearrange("b (h s) p k c -> (b h) s p k c", s=2)[pair, h]
                             ).then_inc(v_in[h], QUADS)

            def load_mask(h, pair):
                sp.dma_start(mask[h][:], masks[pair % PAIRS, h]
                             ).then_inc(mask_in[h], QUADS)

            def store_max_rows(h, half, count):
                sp.wait_ge(rows_ready, count)
                sp.dma_start(q_stack[h][STACK:STACK + MAXROWS, half, 0:RAW],
                             max_rows[:]).then_inc(rows_in, QUADS)

            def store_out(i, u):
                sp.wait_ge(acc_free, UNITS * i + u + 2)
                h, half = u // 2, u % 2
                row = (i // PAIRS) * HEADS + i * 2 + (half * HEADS + h)
                sp.dma_start(scr["out"].rearrange("b f h r t -> (b f h) r t")[row], heads_out[:, u % 2]
                             ).then_inc(out_stored[u % 2], QUADS)

            load_q(0, 0)
            load_k(0)
            load_mask(0, 0)
            load_raw(0, 1)
            load_mask(1, 0)
            load_q(0, 1)
            load_v(0, 0)
            load_raw(1, 1)
            load_q(1, 0)
            builder.load(sp, 1)
            store_max_rows(0, 0, 1)
            with sp.Fori(0, STEPS) as i:
                sp.wait_ge(stack_free[1], i + 1)
                load_k(1)
                load_q(1, 1)
                sp.wait_ge(acc_free, UNITS * i + 1)
                load_v(1, i)
                store_max_rows(0, 1, UNITS * i + 2)
                sp.wait_ge(blocks_seen, SLOTS * i + BLOCKS + 1)
                load_mask(0, (i + 1) % STEPS)
                load_raw(0, i + 2)
                store_out(i, 0)
                store_max_rows(1, 0, UNITS * i + 3)
                sp.wait_ge(lo_ready, CHUNKS * (i + 1) + 6)
                sp.wait_ge(stack_free[0], i + 1)
                load_k(0, levels=(0,))
                sp.wait_ge(lo_ready, CHUNKS * (i + 2))
                load_q(0, 0)
                load_k(0, levels=(1,))
                load_q(0, 1)
                store_out(i, 1)
                load_v(0, (i + 1) % STEPS)
                builder.load(sp, (i + 2) % STEPS)
                store_max_rows(1, 1, UNITS * i + 4)
                sp.wait_ge(blocks_seen, SLOTS * i + 2 * BLOCKS + 1)
                load_mask(1, (i + 1) % STEPS)
                load_raw(1, i + 2)
                store_out(i, 2)
                load_q(1, 0)
                store_max_rows(0, 0, UNITS * i + 5)
                store_out(i, 3)
            for h in range(2):
                sp.wait_ge(out_stored[h], (2 * STEPS + 1) * QUADS)
                sp.wait_ge(mask_in[h], QUADS * (STEPS + 1))
                sp.wait_ge(raw_in[h], 2 * PART_DMAS * QUADS * (STEPS + 1))
                sp.wait_ge(q_in[h][0], PART_DMAS * QUADS * (STEPS + 1))
                for done in (q_in[h][1], k_in[h][0], k_in[h][1]):
                    sp.wait_ge(done, PART_DMAS * QUADS * (STEPS + 1 - h))
            sp.wait_ge(v_in[0], QUADS * (STEPS + 1))
            sp.wait_ge(v_in[1], QUADS * STEPS)
            sp.wait_ge(qk_in, builder.loaded(STEPS + 1))
            sp.wait_ge(rows_in, QUADS * (UNITS * STEPS + 1))

        @block.gpsimd
        def _(pool):
            def level_free(level, builds):
                for h in range(2):
                    for done in (q_in[h][0], q_in[h][1], k_in[h][level // 2]):
                        pool.wait_ge(done, PART_DMAS * QUADS * builds)

            def free(c, builds):
                level, side = builder.at(c)
                if side == 0 and level != 3:
                    level_free(level, builds)
                if c == 2:
                    pool.wait_ge(qk_in, builder.loaded(builds))
                pool.wait_ge(lo_ready, CHUNKS * builds + max(c - 1, 2))

            def diag_minus_max(h, half, count):
                pool.wait_ge(max_ready, count)
                part = diag[h][:, half * UNIT_SLOTS:(half + 1) * UNIT_SLOTS]
                nc.gpsimd.tensor_tensor(part, part, row_max[:, half].unsqueeze(2).broadcast_to([P, UNIT_SLOTS, P]),
                                        ALU.subtract).then_inc(diag_ready, 1)

            pool.sem_inc(diag_ready, 1)
            diag_minus_max(0, 0, 1)
            with pool.Fori(0, STEPS) as i:
                for u in range(1, UNITS + 1):
                    for step, c in pool_steps[u - 1]:
                        if step == "product":
                            free(c, i + 1)
                            builder.multiply(c)
                        else:
                            builder.rest(pool, nc.gpsimd, c, i + 1)
                    diag_minus_max((u // 2) % 2, u % 2, UNITS * i + u + 1)

        @block.scalar
        def _(act):
            def cast(c, builds):
                if c == 0:
                    act.wait_ge(qk_in, builder.loaded(builds))
                    for h in range(2):
                        act.wait_ge(raw_in[h], 2 * PART_DMAS * QUADS * builds)
                builder.cast(act, c, builds)

            act.sem_inc(acc_free, 1)
            for h in range(2):
                act.sem_inc(out_stored[h], QUADS)
            act.wait_ge(unit_ready, 1)
            for h in range(2):
                rows = k_stack[h][STACK:STACK + MAXROWS, 0:RAW].rearrange("p l x -> p (l x)")
                nc.scalar.copy(rows, unit[STACK:STACK + MAXROWS].broadcast_to([MAXROWS, RAW * SEQ])
                               ).then_inc(const_ready, 1)

            def repeat_max(par, count):
                act.wait_ge(max_ready, count)
                nc.scalar.copy(max_repeated[:], row_max[:, par].unsqueeze(1).broadcast_to([P, MAXROWS * RAW, UNIT_SLOTS])
                               ).then_inc(repeated_ready, 1)

            nc.scalar.activation(warm[:], ident[:, 0:1], ACT.Exp)
            repeat_max(0, 1)
            act.sem_inc(exp_done, 2)
            with act.Fori(0, STEPS) as i:
                def take_unit(u):
                    act.wait_ge(acc_full, UNITS * i + u + 1)
                    act.wait_ge(out_stored[u % 2], QUADS * (2 * i + u // 2 + 1))
                    nc.scalar.copy(heads_out[:, u % 2], acc[:]).then_inc(acc_free, 1)

                for s in range(SLOTS):
                    act.wait_ge(probs_used, s + 1)
                    for t in (2 * s, 2 * s + 1):
                        if s % UNIT_SLOTS == TURN_SLOT and t % 2:
                            u = s // UNIT_SLOTS + 1
                            repeat_max(u % 2, UNITS * i + u + 1)
                        act.wait_ge(tile_full, t + 1)
                        nc.scalar.activation(probs[:, t % 4], tile[t % 2][:].rearrange("p a b -> p (a b)"), ACT.Exp,
                                             scale=1.0 / (SCALE * SCALE * HEAD_DIM ** 0.5)).then_inc(exp_done, 1)
                    if s % UNIT_SLOTS == 0 and s > 0:
                        take_unit(s // UNIT_SLOTS - 1)
                    for c in range(CHUNKS):
                        if hi_slot[c] == s:
                            cast(c, i + 1)
                take_unit(UNITS - 1)
                act.drain()
                act.sem_inc(probs_used, -SLOTS)
                act.sem_inc(tile_full, -EXPS)

        @block.vector
        def _(dve):
            def ring_bank(n):
                return ring[:, n % RING]

            def max_block(slot, b, i):
                h, q = b // BLOCKS % 2, b % BLOCKS
                out = part_max[:, b // UNIT_SLOTS % 2, b % UNIT_SLOTS]
                for k in range(ITEMS):
                    n = ring_item(slot, k)
                    if q == 0 and k == ITEMS - 1:
                        dve.wait_ge(mask_in[h], QUADS * (i + 1 + b // SLOTS))
                    dve.wait_ge(ring_full, n + AHEAD_ITEMS + 1)
                    if k < ITEMS - 1:
                        nc.vector.tensor_reduce(out[:, k:k + 1], ring_bank(n), AX.X, ALU.max).then_inc(ring_free, 1)
                        continue
                    nc.vector.tensor_reduce(out[:, 3:4], ring_bank(n)[:, 0:3 * P], AX.X,
                                            ALU.max).then_inc(blocks_seen, 1)
                    nc.vector.tensor_tensor_reduce(out=diag[h][:, q], in0=ring_bank(n)[:, 3 * P:4 * P], in1=mask[h][:],
                                                   scale=1.0, scalar=-3.0e38, op0=ALU.mult, op1=ALU.max,
                                                   accum_out=out[:, 4:5]).then_inc(ring_free, 1)

            def finish_max(par, seen, count):
                dve.wait_ge(blocks_seen, seen)
                if count is not None:
                    dve.wait_ge(diag_ready, count)
                nc.vector.tensor_reduce(row_max[:, par], part_max[:, par], AX.X, ALU.max).then_inc(max_ready, 1)

            def split_max(slot, unit_count):
                n = ring_item(slot, ITEMS)
                dve.wait_ge(ring_full, n + AHEAD_ITEMS + 1)
                if unit_count is not None:
                    dve.wait_ge(rows_in, QUADS * unit_count)
                src = ring_bank(n)[0:MAXROWS * LO_ROWS, 0:P]
                nc.vector.tensor_scalar(max_rows[:], src, -1.0 / MAXUNIT, None, ALU.mult).then_inc(max_seen, 1)
                dve.wait_ge(max_seen, (unit_count if unit_count is not None else 0) + 1)
                nc.vector.scalar_tensor_tensor(out=max_rows[LO_ROWS:], in0=src[LO_ROWS:], scalar=-1.0 / MAXUNIT,
                                               in1=max_rows[LO_ROWS:], op0=ALU.mult,
                                               op1=ALU.subtract).then_inc(rows_ready, 1)
                nc.vector.tensor_copy(scrap[:], src[0:UNIT_SLOTS, 0:1]).then_inc(ring_free, 1)

            nc.vector.memset(unit[:], MAXUNIT).then_inc(unit_ready, 1)
            for s in range(-LEAD, 0):
                max_block(s, s + LEAD, 0)
                if s % UNIT_SLOTS == RED_SLOT and s + LEAD >= UNIT_SLOTS:
                    finish_max(0, s + LEAD + 1, None)
                if s % UNIT_SLOTS == TURN_SLOT and s + LEAD >= UNIT_SLOTS:
                    split_max(s, None)
            with dve.Fori(0, STEPS) as i:
                for s in range(SLOTS):
                    max_block(s, s + LEAD, i)
                    u = s // UNIT_SLOTS + 1
                    if s % UNIT_SLOTS == RED_SLOT:
                        finish_max(u % 2, SLOTS * i + s + LEAD + 1, UNITS * i + u)
                    if s % UNIT_SLOTS == TURN_SLOT:
                        split_max(s, UNITS * i + u)
                dve.drain()
                dve.sem_inc(ring_full, -RING_STEP)

        @block.tensor
        def _(pe):
            def max_scores(slot, b, ks, i):
                h, q = b // BLOCKS % 2, b % BLOCKS
                q0 = q * P % HALF
                parts = score_parts(q, None)
                banks = [[parts[0]], [parts[1]], [parts[2]], parts[3:]]
                for k in ks:
                    n = ring_item(slot, k)
                    if n + AHEAD_ITEMS - RING + 1 > 0:
                        pe.wait_ge(ring_free, n + AHEAD_ITEMS - RING + 1)
                    need = {(0, 0): (k_in[h][0], q_in[h][0]), (0, 3): (k_in[h][1],),
                            (UNIT_SLOTS, 0): (q_in[h][1],)}.get((q, k), ())
                    for done in need:
                        pe.wait_ge(done, PART_DMAS * QUADS * (i + 1 + b // SLOTS))
                    if (q, k) == (0, 3):
                        pe.wait_ge(raw_in[h], 2 * PART_DMAS * QUADS * (i + 1 + b // SLOTS))
                    col = 0
                    for j, (level, first, width) in enumerate(banks[k]):
                        last = nc.tensor.matmul(ring[:, n % RING, col:col + width],
                                                q_stack[h][0:STACK, q // UNIT_SLOTS, level, q0:q0 + P],
                                                k_stack[h][0:STACK, level, first:first + width],
                                                start=(j == 0), stop=True, skip_group_check=True)
                        col += width
                    last.then_inc(ring_full, 1)

            def turn_max(slot, count):
                n = ring_item(slot, ITEMS)
                pe.wait_ge(ring_free, n + AHEAD_ITEMS - RING + 1)
                pe.wait_ge(repeated_ready, count)
                nc.tensor.transpose(ring[0:MAXROWS * LO_ROWS, n % RING, 0:P],
                                    max_repeated[:].rearrange("p r b -> p (r b)"), ident[:]).then_inc(ring_full, 1)

            def scores(t):
                u, kb = t // BLOCKS, t % BLOCKS
                h, half = u // 2, u % 2
                pe.wait_ge(exp_done, t + 1)
                started = set()
                for level, first, width in score_parts(kb, half):
                    col = first - half * HALF
                    bank, at = col // 512, col % 512
                    out = tile[t % 2][:, bank, at:at + width]
                    if level == RAW:
                        last = nc.tensor.matmul(out, diag[h][:, kb], ident[:], is_transpose=True,
                                                start=bank not in started, stop=True, skip_group_check=True)
                    else:
                        last = nc.tensor.matmul(out, k_stack[h][:, level, kb * P:(kb + 1) * P],
                                                q_stack[h][:, half, level, col:col + width],
                                                start=bank not in started, stop=True, skip_group_check=True)
                    started.add(bank)
                last.then_inc(tile_full, 1)

            def products(j):
                u = j // UNIT_SLOTS
                h = u // 2
                for par in range(2):
                    t = 2 * j + par
                    pe.wait_ge(exp_done, t + 3)
                    for qt in range(2):
                        row = (2 * par + qt) * ROWS
                        last = nc.tensor.matmul(acc[row:row + ROWS], v_ones[h][:, t % BLOCKS],
                                                probs[:, t % 4, qt * 512:(qt + 1) * 512],
                                                start=(j % UNIT_SLOTS == 0), stop=(j % UNIT_SLOTS == UNIT_SLOTS - 1),
                                                skip_group_check=True)
                        if j % (2 * UNIT_SLOTS) == 2 * UNIT_SLOTS - 1 and (par, qt) == (0, 0):
                            last.then_inc(stack_free[h], 1)
                        if j % UNIT_SLOTS == UNIT_SLOTS - 1 and (par, qt) == (0, 1):
                            last.then_inc(probs_used, 1)
                last.then_inc(acc_full if j % UNIT_SLOTS == UNIT_SLOTS - 1 else probs_used, 1)

            pe.sem_inc(probs_used, 2)
            pe.sem_inc(stack_free[1], 1)
            for s in range(-LEAD, 0):
                max_scores(s, s + LEAD, range(ITEMS), 0)
                if s % UNIT_SLOTS == TURN_SLOT and s + LEAD >= UNIT_SLOTS:
                    turn_max(s, 1)
            pe.wait_ge(const_ready, 2)
            with pe.Fori(0, STEPS) as i:
                for s in range(SLOTS):
                    if s % UNIT_SLOTS == 0:
                        u = s // UNIT_SLOTS
                        pe.wait_ge(rows_in, QUADS * (UNITS * i + u + 1))
                        pe.wait_ge(diag_ready, UNITS * i + u + 2)
                    scores(2 * s)
                    max_scores(s, s + LEAD, (0, 1), i)
                    scores(2 * s + 1)
                    if s == SLOTS - 1:
                        products(s - 1)
                    max_scores(s, s + LEAD, (2, 3), i)
                    j = s if s == SLOTS - 1 else s - 1
                    if j >= 0:
                        if j % UNIT_SLOTS == 0:
                            pe.wait_ge(acc_free, UNITS * i + j // UNIT_SLOTS + 1)
                        if j % (2 * UNIT_SLOTS) == 0:
                            pe.wait_ge(v_in[j // (2 * UNIT_SLOTS)], QUADS * (i + 1))
                        products(j)
                    if s % UNIT_SLOTS == TURN_SLOT:
                        turn_max(s, UNITS * i + s // UNIT_SLOTS + 2)
                pe.drain()
                pe.sem_inc(exp_done, -EXPS)
                pe.sem_inc(ring_free, -RING_STEP)


def ffn_block(nc, a, keep, scr, out):
    ident, wot, ternary = keep["ident"], keep["wot"], keep["ternary"]
    PART = HEADS * GROUP // P
    with ExitStack() as ctx:
        def sb(name, shape, dt=F32):
            return ctx.enter_context(nc.sbuf_tensor(name, shape, dt))

        def sem(name):
            return ctx.enter_context(nc.semaphore(name))

        w1t = sb("w1t", [P, EC, FF], F16)
        w2t = sb("w2t", [P, FC, EMBED], F16)
        sums_in = sb("sums_in", [P, 2, EC, 2, GROUP])
        p_sums_in = sb("p_sums_in", [P, 2, 2, PART])
        p_sums = sb("p_sums", [P, PART])
        inv = sb("inv", [P, PART])
        inv_all = sb("inv_all", [P, 2, EC, GROUP])
        x_in = sb("x_res", [P, 2, TILES, EMBED])
        sums = sb("sums", [P, EC, GROUP])
        heads = sb("heads", [P, EC, GROUP])
        x_bias = sb("x_bias", [P, TILES, EMBED])
        y = sb("y", [P, TILES, EMBED])
        y_bias = sb("y_bias", [P, 2, TILES, EMBED])
        z = sb("z", [P, TILES, EMBED])
        z_hi = sb("z_hi", [P, EC, GROUP], F16)
        z_lo = sb("z_lo", [P, EC, GROUP], F16)
        hidden = sb("hidden", [P, FC, GROUP])
        h_hi = sb("h_hi", [P, FC, GROUP], F16)
        h_lo = sb("h_lo", [P, FC, GROUP], F16)
        result = sb("result", [P, 2, TILES, EMBED])
        stats = sb("stats2", [P, TILES, 6])
        mv = sb("mv2", [P, TILES, 2])
        rstd = sb("rstd2", [P, TILES])
        spare = sb("spare2", [P, 1])
        up = ctx.enter_context(nc.psum_tensor("up", [P, 2, GROUP], F32))
        attn = ctx.enter_context(nc.psum_tensor("attn", [P, TILES, EMBED], F32))
        turn = ctx.enter_context(nc.psum_tensor("turn2", [P, EC, GROUP], F32))
        down = ctx.enter_context(nc.psum_tensor("down", [P, TILES, EMBED], F32))

        loaded = [sem(f"loaded{u}") for u in range(2)]
        stored = [sem(f"out_done{u}") for u in range(2)]
        heads_ready, x_bias_ready, attn_done, y_ready, y_bias_ready = (
            sem("heads_ready"), sem("x_bias_ready"), sem("attn_done"), sem("y_ready"), sem("y_bias_ready"))
        sqrt_in, sqrt_out, z_ready, turned = sem("sqrt_in2"), sem("sqrt_out2"), sem("z_ready"), sem("turned2")
        z_hi_ready, z_lo_ready = sem("z_hi_ready"), sem("z_lo_ready")
        up_done, up_taken, h_hi_ready, h_lo_ready = sem("up_done"), sem("up_taken"), sem("h_hi_ready"), sem("h_lo_ready")
        down_done, result_ready, dve_step = sem("down_done"), sem("result_ready"), sem("dve_step2")
        w_turned, w_taken = sem("ffn_w_turned"), sem("ffn_w_taken")
        p_sums_loaded = [sem(f"p_sums_loaded{u}") for u in range(2)]
        p_sums_added, inv_ready, inv_stored = sem("p_sums_added"), sem("inv_ready"), sem("inv_stored")
        inv_in = [sem(f"inv_in{u}") for u in range(2)]
        W_BANKS = 4
        LOADS = 2 * EC + 1
        TURN_AT = 6
        DVE_STEPS = 4
        LOOPED = GROUPS - 2
        block = ctx.enter_context(nc.Block())
        x_groups = a["x"].rearrange("b s e -> (b s) e").rearrange("(g t p) e -> g p t e", t=TILES, p=P)
        out_groups = out.rearrange("b s e -> (b s) e").rearrange("(g t p) e -> g p t e", t=TILES, p=P)
        out_scr = scr["out"].rearrange("b f (c h) (r q k d) t -> k (b f) q c r h d t", c=EC, r=2, q=2, k=2)[0]
        p_scr = scr["out"].rearrange("b f h (r q k d) t -> k d (b f) q r h t", r=2, q=2, k=2)[1, 0]

        def w_bank(q):
            q = q % W_BANKS
            return up[:, q] if q < 2 else down[:, 2 * (q - 2):2 * (q - 1)].rearrange("p t e -> p (t e)")

        @block.sync
        def _(sp):
            def load_p_sums(pair, u):
                for r in range(2):
                    sp.dma_start(p_sums_in[:, u, r], p_scr[pair, u, r].rearrange("h (j x) -> h j x", x=PART)
                                 ).then_inc(p_sums_loaded[u], QUADS)

            def load(pair, u):
                for c in range(EC):
                    for r in range(2):
                        sp.dma_start(sums_in[:, u, c, r], out_scr[pair, u, c, r]).then_inc(loaded[u], QUADS)
                sp.dma_start(x_in[:, u], x_groups[pair * 2 + u]).then_inc(loaded[u], QUADS)

            def store_inverse(g):
                sp.wait_ge(inv_ready, g + 1)
                sp.dma_start(scr["inv"][g], inv[:]).then_inc(inv_stored, QUADS)

            def spread_inverse(g, u):
                sp.wait_ge(inv_stored, (g + 1) * QUADS)
                rows = scr["inv"][g].rearrange("(c h j) x -> c h (j x)", c=EC, h=HEADS // EC)
                for c in range(EC):
                    sp.dma_start(inv_all[:, u, c], rows[c].unsqueeze(1).broadcast_to([HEADS // EC, HEAD_DIM, GROUP])
                                 ).then_inc(inv_in[u], QUADS)

            def body(pair, u, load_next=True):
                g = pair * 2 + u
                if load_next:
                    sp.wait_ge(heads_ready, g + 1)
                    sp.wait_ge(x_bias_ready, g + 1)
                    load_p_sums(pair + 1, u)
                    load(pair + 1, u)
                    store_inverse(g + 2)
                    spread_inverse(g + 2, u)
                sp.wait_ge(result_ready, g + 2)
                sp.dma_start(out_groups[g], result[:, u]).then_inc(stored[u], QUADS)

            for u in range(2):
                sp.sem_inc(stored[u], QUADS)
            for u in range(2):
                load_p_sums(0, u)
            store_inverse(0)
            load(0, 0)
            spread_inverse(0, 0)
            store_inverse(1)
            load(0, 1)
            spread_inverse(1, 1)
            with sp.Fori(0, LOOPED // 2) as i:
                for u in range(2):
                    body(i, u)
            for u in range(2):
                body(LOOPED // 2, u, load_next=False)
            for u in range(2):
                sp.wait_ge(stored[u], (GROUPS // 2 + 1) * QUADS)

        @block.gpsimd
        def _(pool):
            def add_out_bias(g, u):
                pool.wait_ge(loaded[u], LOADS * QUADS * (g // 2 + 1))
                nc.gpsimd.tensor_tensor(x_bias[:], x_in[:, u], lead(keep["bo_all"][:], TILES), ALU.add
                                        ).then_inc(x_bias_ready, 1)

            def add_ffn_bias(g, u, seen):
                pool.wait_ge(y_ready, g + 1)
                pool.wait_ge(result_ready, seen)
                nc.gpsimd.tensor_tensor(y_bias[:, u], y[:], lead(keep["b2_all"][:], TILES), ALU.add
                                        ).then_inc(y_bias_ready, 1)

            def body(g, u, more):
                if more:
                    add_out_bias(g + 1, 1 - u)
                for f in range(FC):
                    pool.wait_ge(h_hi_ready, FC * g + f + 1)
                    nc.gpsimd.tensor_tensor(h_lo[:, f], hidden[:, f], h_hi[:, f], ALU.subtract).then_inc(h_lo_ready, 1)
                if more:
                    add_ffn_bias(g + 1, 1 - u, g + 1)

            add_out_bias(0, 0)
            add_ffn_bias(0, 0, 1)
            for_groups(pool, body)

        @block.scalar
        def _(act):
            def root(g):
                act.wait_ge(sqrt_in, g + 1)
                nc.scalar.activation(rstd[:], rstd[:], ACT.Sqrt).then_inc(sqrt_out, 1)

            def split_z(g):
                act.wait_ge(turned, g + 1)
                nc.scalar.copy(z_hi[:], turn[:]).then_inc(z_hi_ready, 1)

            def body(g, u, more):
                for f in range(FC):
                    act.wait_ge(up_done, FC * g + f + 1)
                    nc.scalar.activation(hidden[:, f], up[:, f % 2], ACT.Relu, bias=keep["b1_col"][:, f:f + 1]
                                         ).then_inc(up_taken, 1)
                if more:
                    root(g + 1)
                    split_z(g + 1)

            act.sem_inc(up_taken, 1)
            for q in range(2 * W_BANKS):
                act.wait_ge(w_turned, q + 1)
                out = (w1t[:, q // 2, (q % 2) * 512:(q % 2 + 1) * 512] if q < 4 else
                       w2t[:, 2 * (q - 4):2 * (q - 4) + 2, :].rearrange("p c e -> p (c e)"))
                nc.scalar.copy(out, w_bank(q)).then_inc(w_taken, 1)
            root(0)
            split_z(0)
            for_groups(act, body)

        @block.vector
        def _(dve):
            def divide(g, u):
                dve.wait_ge(inv_in[u], EC * QUADS * (g // 2 + 1))
                dve.wait_ge(loaded[u], LOADS * QUADS * (g // 2 + 1))
                nc.vector.tensor_tensor(sums[:], sums_in[:, u, :, 0], sums_in[:, u, :, 1], ALU.add).then_inc(dve_step, 1)
                dve.wait_ge(dve_step, DVE_STEPS * g + 1)
                nc.vector.tensor_tensor(heads[:], sums[:], inv_all[:, u], ALU.mult).then_inc(heads_ready, 1)

            def invert(g, u, previous_store):
                dve.wait_ge(p_sums_loaded[u], 2 * QUADS * (g // 2 + 1))
                if previous_store:
                    dve.wait_ge(inv_stored, QUADS * g)
                nc.vector.tensor_tensor(p_sums[:], p_sums_in[:, u, 0], p_sums_in[:, u, 1], ALU.add).then_inc(p_sums_added, 1)
                dve.wait_ge(p_sums_added, g + 1)
                nc.vector.reciprocal(inv[:], p_sums[:]).then_inc(inv_ready, 1)

            def residual(g, first=False):
                dve.wait_ge(attn_done, g + 1)
                dve.wait_ge(x_bias_ready, g + 1)
                if not first:
                    dve.wait_ge(y_bias_ready, g)
                nc.vector.tensor_tensor(y[:], attn[:], x_bias[:], ALU.add).then_inc(y_ready, 1)
                dve.wait_ge(y_ready, g + 1)
                taken = [1]

                def step(ins):
                    taken[0] += 1
                    ins.then_inc(dve_step, 1)
                    dve.wait_ge(dve_step, DVE_STEPS * g + taken[0])

                normalize(nc, dve, y, z, stats, mv, rstd, spare, step, sqrt_in, sqrt_out, g + 1,
                          lambda ins: ins.then_inc(z_ready, 1))

            def rest_z(g):
                dve.wait_ge(z_hi_ready, g + 1)
                nc.vector.tensor_tensor(z_lo[:], turn[:], z_hi[:], ALU.subtract).then_inc(z_lo_ready, 1)

            def body(g, u, more):
                if more:
                    divide(g + 1, 1 - u)
                for f in range(FC):
                    dve.wait_ge(up_taken, FC * g + f + 2)
                    nc.vector.tensor_copy(h_hi[:, f], hidden[:, f]).then_inc(h_hi_ready, 1)
                if more:
                    residual(g + 1)
                if more == 2:
                    invert(g + 2, u, True)
                if more:
                    rest_z(g + 1)
                dve.wait_ge(down_done, g + 1)
                dve.wait_ge(y_bias_ready, g + 1)
                dve.wait_ge(stored[u], QUADS * (g // 2 + 1))
                nc.vector.tensor_tensor(result[:, u], down[:], y_bias[:, u], ALU.add).then_inc(result_ready, 1)

            dve.sem_inc(result_ready, 1)
            invert(0, 0, False)
            invert(1, 1, True)
            divide(0, 0)
            residual(0, first=True)
            rest_z(0)
            for_groups(dve, body)

        @block.tensor
        def _(pe):
            def attn_product(g, first=False):
                pe.wait_ge(heads_ready, g + 1)
                if not first:
                    pe.wait_ge(y_ready, g)
                for t in range(TILES):
                    for c in range(EC):
                        last = nc.tensor.matmul(attn[:, t], heads[:, c, t * P:(t + 1) * P], wot[:, c],
                                                start=(c == 0), stop=(c == EC - 1), skip_group_check=True)
                last.then_inc(attn_done, 1)

            def turn_z(g, first=False):
                pe.wait_ge(z_ready, g + 1)
                if not first:
                    pe.wait_ge(z_lo_ready, g)
                for c in range(EC):
                    for t in range(TILES):
                        last = nc.tensor.transpose(turn[:, c, t * P:(t + 1) * P], z[:, t, c * P:(c + 1) * P], ident[:])
                last.then_inc(turned, 1)

            def body(g, u, more):
                pe.wait_ge(z_lo_ready, g + 1)
                for f in range(FC):
                    pe.wait_ge(up_taken, FC * g + max(f, 1))
                    k = 0
                    for c in range(EC):
                        for part in (z_hi, z_lo):
                            last = nc.tensor.matmul(up[:, f % 2], w1t[:, c, f * P:(f + 1) * P], part[:, c],
                                                    start=(k == 0), stop=(k == 2 * EC - 1))
                            k += 1
                    last.then_inc(up_done, 1)
                if more:
                    attn_product(g + 1)
                pe.wait_ge(result_ready, g + 1)
                for f in range(FC):
                    if more and f == TURN_AT:
                        turn_z(g + 1)
                    pe.wait_ge(h_lo_ready, FC * g + f + 1)
                    for part in (h_hi, h_lo):
                        for t in range(TILES):
                            last = nc.tensor.matmul(down[:, t], part[:, f, t * P:(t + 1) * P], w2t[:, f],
                                                    start=(f == 0 and part is h_hi and t % 2 == 0),
                                                    stop=(f == FC - 1 and part is h_lo), skip_group_check=True)
                last.then_inc(down_done, 1)

            def turn_w(m):
                rows = (ternary[:, 0].rearrange("p (c e) -> p c e", c=FC), ternary[:, 1].rearrange("p (c f) -> p c f", c=EC))
                for q in range(W_BANKS):
                    if m == 1:
                        pe.wait_ge(w_taken, q + 1)
                    for j in range(4):
                        if m == 0:
                            src = rows[0][:, (q % 2) * 4 + j, (q // 2) * P:(q // 2 + 1) * P]
                        else:
                            src = rows[1][:, j % 2, (2 * q + j // 2) * P:(2 * q + j // 2 + 1) * P]
                        last = nc.tensor.matmul(w_bank(q)[:, j * P:(j + 1) * P], src, keep["ident16"][:],
                                                start=(j == 0), stop=True, skip_group_check=True)
                    last.then_inc(w_turned, 1)

            turn_w(0)
            turn_w(1)
            attn_product(0, first=True)
            pe.wait_ge(w_taken, 2 * W_BANKS)
            turn_z(0, first=True)
            for_groups(pe, body)


INPUTS = {"x": "L0_attn_x", "Wq": "L0_attn_Wq", "bq": "L0_attn_bq", "Wk": "L0_attn_Wk", "bk": "L0_attn_bk",
          "Wv": "L0_attn_Wv", "bv": "L0_attn_bv", "Wo": "L0_attn_Wo", "bo": "L0_attn_bo",
          "decay": "L0_attn_decay_params", "mix": "L0_attn_mix_weights",
          "W1": "L0_ffn_W1", "b1": "L0_ffn_b1", "W2": "L0_ffn_W2", "b2": "L0_ffn_b2"}


def build(nc, a, out):
    scr = {
        "inv": nc.dram_tensor("inv_scratch", [GROUPS, P, HEADS * GROUP // P], F32).ap(),
        "q": nc.dram_tensor("q_scratch", [BATCH, 2, 8, DECAYS, HEAD_DIM, SEQ], F32).ap(),
        "k": nc.dram_tensor("k_scratch", [BATCH, 2, 8, HEAD_DIM, SEQ], F32).ap(),
        "v": nc.dram_tensor("v_scratch", [BATCH, HEADS, P, BLOCKS, ROWS], F32).ap(),
        "table": nc.dram_tensor("table_scratch", [HEADS, DECAYS, 2 * HALF], F32).ap(),
        "hat": nc.dram_tensor("hat_scratch", [HEADS, P, 2 * P], F32).ap(),
        "out": nc.dram_tensor("out_scratch", [BATCH, 2, HEADS, P, GROUP], F32).ap(),
    }
    with ExitStack() as ctx:
        def sb(name, shape, dt=F32):
            return ctx.enter_context(nc.sbuf_tensor(name, shape, dt))

        keep = {"ident": sb("ident", [P, P]), "ident16": sb("ident16", [P, P], F16),
                "ternary": sb("ternary", [P, 2, FC * EMBED], F16),
                "wot": sb("wot", [P, EC, EMBED]), "bo_all": sb("bo_all", [P, EMBED]), "b2_all": sb("b2_all", [P, EMBED]),
                "b1_col": sb("b1_col", [P, FC])}
        with ExitStack() as scores:
            builder = PairBuilder(nc, scr, lambda name, shape, dt=F32: scores.enter_context(nc.sbuf_tensor(name, shape, dt)),
                                  lambda name: scores.enter_context(nc.semaphore(name)))
            token_block(nc, a, keep, builder, scr)
            attention_block(nc, keep, builder, scr)
        ffn_block(nc, a, keep, scr, out)


def kernel(**inputs):
    import numpy as np
    import concourse.bacc as bacc
    from concourse.bass_utils import run_bass_kernel_spmd

    nc = bacc.Bacc("TRN2", target_bir_lowering=False, num_devices=1)
    arrays, a = {}, {}
    for short, name in INPUTS.items():
        array = np.ascontiguousarray(inputs[name])
        arrays[f"in_{short}"] = array
        a[short] = nc.dram_tensor(f"in_{short}", array.shape, mybir.dt.from_np(array.dtype), kind="ExternalInput").ap()
    out = nc.dram_tensor("out", (BATCH, SEQ, EMBED), F32, kind="ExternalOutput").ap()
    build(nc, a, out)
    result = run_bass_kernel_spmd(nc, [arrays], core_ids=[0])
    return result.results[0]["out"]
```
